# Optimizing a Trainium2 kernel written in Bass

```python
import numpy as np
import jax
import jax.numpy as jnp

def _softmax(x, axis=-1):
    return jax.nn.softmax(x, axis=axis)

def _gelu(x):
    return jax.nn.gelu(x, approximate=True)

def _silu(x):
    return jax.nn.silu(x)

def _sigmoid(x):
    return jax.nn.sigmoid(x)

def _layernorm(x, axis=-1, eps=1e-05):
    m = jnp.mean(x, axis=axis, keepdims=True)
    v = jnp.var(x, axis=axis, keepdims=True)
    return (x - m) / jnp.sqrt(v + eps)

def _scatter_add(tgt, idx, src, axis=0):
    return tgt.at[idx].add(src)

def _segment_sum(src, seg, n):
    return jax.ops.segment_sum(src, seg, n)
kernel_name = 'mk_gnn_resnorm_d4_gnn_r32_e42820'

def setup_inputs(seed: int=0):
    np.random.seed(seed)
    _w = jnp.asarray

    def _rec_inputs():
        import jax
        import jax.numpy as jnp
        _gk = jax.random.key(seed)
        x = -0.0003713 + 1 * jax.random.normal(jax.random.fold_in(_gk, 1), (3125, 256), jnp.float32)
        src = jax.random.randint(jax.random.fold_in(_gk, 2), (50000,), 0, 3125, jnp.int32)
        dst = jnp.minimum((3125 * jax.random.uniform(jax.random.fold_in(_gk, 3), (50000,)) ** 2.0).astype(jnp.int32), 99999)
        _o = jnp.argsort(dst, stable=True)
        src = src[_o]
        dst = dst[_o]
        edge_attr_64 = 0.000279952 + 1.00013 * jax.random.normal(jax.random.fold_in(_gk, 12), (50000, 64), jnp.float32)
        return (x, src, dst, edge_attr_64)
    x, src, dst, edge_attr_64 = _rec_inputs()

    def _L0_gnn_setup():
        import jax, jax.numpy as jnp
        import numpy as np
        N = 50000
        E = 25000
        D = 256

        def _gcn_norm(edge_index, n_nodes):
            loop = jnp.arange(n_nodes, dtype=edge_index.dtype)
            row = jnp.concatenate([edge_index[0], loop])
            col = jnp.concatenate([edge_index[1], loop])
            deg = jax.ops.segment_sum(jnp.ones_like(col, dtype=jnp.float32), col, num_segments=n_nodes)
            dinv = jnp.where(deg > 0, jax.lax.rsqrt(deg), 0.0)
            norm = dinv[row] * dinv[col]
            return (row, col, norm)

        def _gcn_conv(h, row, col, norm, W, b, n_nodes):
            h = h @ W.T
            msg = h[row] * norm[:, None]
            out = jax.ops.segment_sum(msg, col, num_segments=n_nodes)
            return out + b
        key = jax.random.key(seed)
        ks = jax.random.split(key, 8)
        scale = 1.0 / np.sqrt(D)
        x = jax.random.normal(ks[0], (N, D), dtype=jnp.float32)
        edge_index = jax.random.randint(ks[1], (2, E), 0, N, dtype=jnp.int32)
        W1 = jax.random.normal(ks[2], (D, D), dtype=jnp.float32) * scale
        b1 = jnp.zeros((D,), dtype=jnp.float32)
        W2 = jax.random.normal(ks[3], (D, D), dtype=jnp.float32) * scale
        b2 = jnp.zeros((D,), dtype=jnp.float32)
        W3 = jax.random.normal(ks[4], (D, D), dtype=jnp.float32) * scale
        b3 = jnp.zeros((D,), dtype=jnp.float32)
        return {'x': x, 'edge_index': edge_index, 'W1': W1, 'b1': b1, 'W2': W2, 'b2': b2, 'W3': W3, 'b3': b3}
    _L0_gnn_all = _L0_gnn_setup()
    _L0_gnn_in = {k: v for k, v in _L0_gnn_all.items() if k in ('W1', 'b1', 'W2', 'b2', 'W3', 'b3')}
    del _L0_gnn_all

    def _L1_gnn_setup():
        import jax, jax.numpy as jnp
        import numpy as np
        N_NODES = 3125
        N_EDGES = 100000
        IN_F = 256
        OUT_F = 256
        NEG_SLOPE = 0.2
        key = jax.random.key(seed)
        ks = jax.random.split(key, 8)
        x = jax.random.normal(ks[0], (N_NODES, IN_F), dtype=jnp.float32)
        Wv = jax.random.normal(ks[1], (IN_F, OUT_F), dtype=jnp.float32) / np.sqrt(IN_F)
        bv = jnp.zeros((OUT_F,), dtype=jnp.float32)
        wq = jax.random.normal(ks[2], (OUT_F,), dtype=jnp.float32) / np.sqrt(OUT_F)
        bq = jnp.zeros((), dtype=jnp.float32)
        wk = jax.random.normal(ks[3], (OUT_F,), dtype=jnp.float32) / np.sqrt(OUT_F)
        bk = jnp.zeros((), dtype=jnp.float32)
        src = jax.random.randint(ks[4], (N_EDGES,), 0, N_NODES, dtype=jnp.int32)
        dst = jax.random.randint(ks[5], (N_EDGES,), 0, N_NODES, dtype=jnp.int32)
        return {'x': x, 'Wv': Wv, 'bv': bv, 'wq': wq, 'bq': bq, 'wk': wk, 'bk': bk, 'src': src, 'dst': dst}
    _L1_gnn_all = _L1_gnn_setup()
    _L1_gnn_in = {k: v for k, v in _L1_gnn_all.items() if k in ('Wv', 'bv', 'wq', 'bq', 'wk', 'bk')}
    del _L1_gnn_all

    def _L2_gnn_setup():
        import jax, jax.numpy as jnp
        import numpy as np
        N = 3125
        E = 10000
        CIN = 256
        EDIM = 64
        EEMB = 256
        H = 1024
        LN_EPS = 1e-05

        def _ln(x, g, b):
            m = jnp.mean(x, axis=-1, keepdims=True)
            v = jnp.var(x, axis=-1, keepdims=True)
            return (x - m) * jax.lax.rsqrt(v + LN_EPS) * g + b
        key = jax.random.key(seed)
        ks = jax.random.split(key, 16)

        def w(k, i, o):
            return (jax.random.normal(k, (i, o), jnp.float32) / np.sqrt(i)).astype(jnp.float32)
        return {'x': jax.random.normal(ks[0], (N, CIN), jnp.float32), 'edge_index': jax.random.randint(ks[1], (2, E), 0, N, dtype=jnp.int64), 'edge_attr': jax.random.normal(ks[2], (E, EDIM), jnp.float32), 'eps': jnp.float32(0.0), 'ee_w1': w(ks[3], EDIM, EEMB), 'ee_b1': jnp.zeros((EEMB,), jnp.float32), 'ee_w2': w(ks[4], EEMB, CIN), 'ee_b2': jnp.zeros((CIN,), jnp.float32), 'w1': w(ks[5], CIN, H), 'b1': jnp.zeros((H,), jnp.float32), 'g1': jnp.ones((H,), jnp.float32), 'be1': jnp.zeros((H,), jnp.float32), 'w2': w(ks[6], H, H), 'b2': jnp.zeros((H,), jnp.float32), 'g2': jnp.ones((H,), jnp.float32), 'be2': jnp.zeros((H,), jnp.float32), 'w3': w(ks[7], H, CIN), 'b3': jnp.zeros((CIN,), jnp.float32), 'bn_g': jnp.ones((CIN,), jnp.float32), 'bn_b': jnp.zeros((CIN,), jnp.float32)}
    _L2_gnn_all = _L2_gnn_setup()
    _L2_gnn_in = {k: v for k, v in _L2_gnn_all.items() if k in ('eps', 'ee_w1', 'ee_b1', 'ee_w2', 'ee_b2', 'w1', 'b1', 'g1', 'be1', 'w2', 'b2', 'g2', 'be2', 'w3', 'b3', 'bn_g', 'bn_b')}
    del _L2_gnn_all

    def _L3_gnn_setup():
        import jax, jax.numpy as jnp
        import numpy as np
        N_NODES = 50000
        NODE_DIM = 256
        HIDDEN = 256
        N_EDGES = 25000
        NEG_SLOPE = 0.2

        def _gat_layer(x, src, dst, n, W, a_src, a_dst, b):
            h = x @ W
            al_s = h @ a_src
            al_d = h @ a_dst
            e = jax.nn.leaky_relu(al_s[src] + al_d[dst], NEG_SLOPE)
            m = jax.ops.segment_max(e, dst, num_segments=n)
            ex = jnp.exp(e - m[dst])
            denom = jax.ops.segment_sum(ex, dst, num_segments=n)
            alpha = ex / denom[dst]
            out = jax.ops.segment_sum(h[src] * alpha[:, None], dst, num_segments=n)
            return out + b
        key = jax.random.key(seed)
        ks = jax.random.split(key, 12)
        x = jax.random.normal(ks[0], (N_NODES, NODE_DIM), dtype=jnp.float32)
        edge_index = jax.random.randint(ks[1], (2, N_EDGES), 0, N_NODES, dtype=jnp.int64)
        s1 = 1.0 / np.sqrt(NODE_DIM)
        s2 = 1.0 / np.sqrt(HIDDEN)
        W1 = jax.random.normal(ks[2], (NODE_DIM, HIDDEN), dtype=jnp.float32) * s1
        a1_src = jax.random.normal(ks[3], (HIDDEN,), dtype=jnp.float32) * s2
        a1_dst = jax.random.normal(ks[4], (HIDDEN,), dtype=jnp.float32) * s2
        b1 = jnp.zeros((HIDDEN,), dtype=jnp.float32)
        W2 = jax.random.normal(ks[5], (HIDDEN, HIDDEN), dtype=jnp.float32) * s2
        a2_src = jax.random.normal(ks[6], (HIDDEN,), dtype=jnp.float32) * s2
        a2_dst = jax.random.normal(ks[7], (HIDDEN,), dtype=jnp.float32) * s2
        b2 = jnp.zeros((HIDDEN,), dtype=jnp.float32)
        return {'x': x, 'edge_index': edge_index, 'W1': W1, 'a1_src': a1_src, 'a1_dst': a1_dst, 'b1': b1, 'W2': W2, 'a2_src': a2_src, 'a2_dst': a2_dst, 'b2': b2}
    _L3_gnn_all = _L3_gnn_setup()
    _L3_gnn_in = {k: v for k, v in _L3_gnn_all.items() if k in ('W1', 'a1_src', 'a1_dst', 'b1', 'W2', 'a2_src', 'a2_dst', 'b2')}
    del _L3_gnn_all
    return {'x': x, 'src': src, 'dst': dst, 'edge_attr_64': edge_attr_64, 'L0_gnn_W1': _L0_gnn_in['W1'], 'L0_gnn_b1': _L0_gnn_in['b1'], 'L0_gnn_W2': _L0_gnn_in['W2'], 'L0_gnn_b2': _L0_gnn_in['b2'], 'L0_gnn_W3': _L0_gnn_in['W3'], 'L0_gnn_b3': _L0_gnn_in['b3'], 'L1_gnn_Wv': _L1_gnn_in['Wv'], 'L1_gnn_bv': _L1_gnn_in['bv'], 'L1_gnn_wq': _L1_gnn_in['wq'], 'L1_gnn_bq': _L1_gnn_in['bq'], 'L1_gnn_wk': _L1_gnn_in['wk'], 'L1_gnn_bk': _L1_gnn_in['bk'], 'L2_gnn_eps': _L2_gnn_in['eps'], 'L2_gnn_ee_w1': _L2_gnn_in['ee_w1'], 'L2_gnn_ee_b1': _L2_gnn_in['ee_b1'], 'L2_gnn_ee_w2': _L2_gnn_in['ee_w2'], 'L2_gnn_ee_b2': _L2_gnn_in['ee_b2'], 'L2_gnn_w1': _L2_gnn_in['w1'], 'L2_gnn_b1': _L2_gnn_in['b1'], 'L2_gnn_g1': _L2_gnn_in['g1'], 'L2_gnn_be1': _L2_gnn_in['be1'], 'L2_gnn_w2': _L2_gnn_in['w2'], 'L2_gnn_b2': _L2_gnn_in['b2'], 'L2_gnn_g2': _L2_gnn_in['g2'], 'L2_gnn_be2': _L2_gnn_in['be2'], 'L2_gnn_w3': _L2_gnn_in['w3'], 'L2_gnn_b3': _L2_gnn_in['b3'], 'L2_gnn_bn_g': _L2_gnn_in['bn_g'], 'L2_gnn_bn_b': _L2_gnn_in['bn_b'], 'L3_gnn_W1': _L3_gnn_in['W1'], 'L3_gnn_a1_src': _L3_gnn_in['a1_src'], 'L3_gnn_a1_dst': _L3_gnn_in['a1_dst'], 'L3_gnn_b1': _L3_gnn_in['b1'], 'L3_gnn_W2': _L3_gnn_in['W2'], 'L3_gnn_a2_src': _L3_gnn_in['a2_src'], 'L3_gnn_a2_dst': _L3_gnn_in['a2_dst'], 'L3_gnn_b2': _L3_gnn_in['b2']}

def reference(x, src, dst, edge_attr_64, L0_gnn_W1, L0_gnn_b1, L0_gnn_W2, L0_gnn_b2, L0_gnn_W3, L0_gnn_b3, L1_gnn_Wv, L1_gnn_bv, L1_gnn_wq, L1_gnn_bq, L1_gnn_wk, L1_gnn_bk, L2_gnn_eps, L2_gnn_ee_w1, L2_gnn_ee_b1, L2_gnn_ee_w2, L2_gnn_ee_b2, L2_gnn_w1, L2_gnn_b1, L2_gnn_g1, L2_gnn_be1, L2_gnn_w2, L2_gnn_b2, L2_gnn_g2, L2_gnn_be2, L2_gnn_w3, L2_gnn_b3, L2_gnn_bn_g, L2_gnn_bn_b, L3_gnn_W1, L3_gnn_a1_src, L3_gnn_a1_dst, L3_gnn_b1, L3_gnn_W2, L3_gnn_a2_src, L3_gnn_a2_dst, L3_gnn_b2):
    import jax
    import jax.numpy as jnp

    def _L0_gnn_ref(x, edge_index, W1, b1, W2, b2, W3, b3):
        import jax, jax.numpy as jnp
        import numpy as np
        N = 50000
        E = 25000
        D = 256

        def _gcn_norm(edge_index, n_nodes):
            loop = jnp.arange(n_nodes, dtype=edge_index.dtype)
            row = jnp.concatenate([edge_index[0], loop])
            col = jnp.concatenate([edge_index[1], loop])
            deg = jax.ops.segment_sum(jnp.ones_like(col, dtype=jnp.float32), col, num_segments=n_nodes)
            dinv = jnp.where(deg > 0, jax.lax.rsqrt(deg), 0.0)
            norm = dinv[row] * dinv[col]
            return (row, col, norm)

        def _gcn_conv(h, row, col, norm, W, b, n_nodes):
            h = h @ W.T
            msg = h[row] * norm[:, None]
            out = jax.ops.segment_sum(msg, col, num_segments=n_nodes)
            return out + b
        n_nodes = x.shape[0]
        row, col, norm = _gcn_norm(edge_index, n_nodes)
        h = jax.nn.relu(_gcn_conv(x, row, col, norm, W1, b1, n_nodes))
        h = jax.nn.relu(_gcn_conv(h, row, col, norm, W2, b2, n_nodes))
        out = _gcn_conv(h, row, col, norm, W3, b3, n_nodes)
        return out

    def _L1_gnn_ref(x, Wv, bv, wq, bq, wk, bk, src, dst):
        import jax, jax.numpy as jnp
        import numpy as np
        N_NODES = 3125
        N_EDGES = 100000
        IN_F = 256
        OUT_F = 256
        NEG_SLOPE = 0.2
        n = x.shape[0]
        h = x @ Wv + bv
        q = h @ wq + bq
        k = h @ wk + bk
        e = q[src] + k[dst]
        c = jnp.where(e > 0, e, NEG_SLOPE * e)
        m = jax.ops.segment_max(c, dst, num_segments=n)
        ex = jnp.exp(c - m[dst])
        s = jax.ops.segment_sum(ex, dst, num_segments=n)
        attn = ex / s[dst]
        msg = h[src] * attn[:, None]
        out = jax.ops.segment_sum(msg, dst, num_segments=n)
        return out

    def _L2_gnn_ref(x, edge_index, edge_attr, eps, ee_w1, ee_b1, ee_w2, ee_b2, w1, b1, g1, be1, w2, b2, g2, be2, w3, b3, bn_g, bn_b):
        import jax, jax.numpy as jnp
        import numpy as np
        N = 3125
        E = 10000
        CIN = 256
        EDIM = 64
        EEMB = 256
        H = 1024
        LN_EPS = 1e-05

        def _ln(x, g, b):
            m = jnp.mean(x, axis=-1, keepdims=True)
            v = jnp.var(x, axis=-1, keepdims=True)
            return (x - m) * jax.lax.rsqrt(v + LN_EPS) * g + b
        n = x.shape[0]
        sl = jnp.arange(n, dtype=edge_index.dtype)
        ei = jnp.concatenate([edge_index, jnp.stack([sl, sl], axis=0)], axis=1)
        ea = jnp.concatenate([edge_attr, jnp.zeros((n, edge_attr.shape[1]), edge_attr.dtype)], axis=0)
        src, dst = (ei[0], ei[1])
        e = jax.nn.relu(ea @ ee_w1 + ee_b1) @ ee_w2 + ee_b2
        msg = x[src] + e
        agg = jax.ops.segment_sum(msg, dst, num_segments=n)
        h = (1.0 + eps) * x + agg
        h = jax.nn.relu(_ln(h @ w1 + b1, g1, be1))
        h = jax.nn.relu(_ln(h @ w2 + b2, g2, be2))
        y = h @ w3 + b3
        out = x + y
        out = _ln(out, bn_g, bn_b)
        return jax.nn.relu(out)

    def _L3_gnn_ref(x, edge_index, W1, a1_src, a1_dst, b1, W2, a2_src, a2_dst, b2):
        import jax, jax.numpy as jnp
        import numpy as np
        N_NODES = 50000
        NODE_DIM = 256
        HIDDEN = 256
        N_EDGES = 25000
        NEG_SLOPE = 0.2

        def _gat_layer(x, src, dst, n, W, a_src, a_dst, b):
            h = x @ W
            al_s = h @ a_src
            al_d = h @ a_dst
            e = jax.nn.leaky_relu(al_s[src] + al_d[dst], NEG_SLOPE)
            m = jax.ops.segment_max(e, dst, num_segments=n)
            ex = jnp.exp(e - m[dst])
            denom = jax.ops.segment_sum(ex, dst, num_segments=n)
            alpha = ex / denom[dst]
            out = jax.ops.segment_sum(h[src] * alpha[:, None], dst, num_segments=n)
            return out + b
        n = x.shape[0]
        loops = jnp.arange(n, dtype=edge_index.dtype)
        src = jnp.concatenate([edge_index[0], loops])
        dst = jnp.concatenate([edge_index[1], loops])
        h = jax.nn.relu(_gat_layer(x, src, dst, n, W1, a1_src, a1_dst, b1))
        h = jax.nn.relu(_gat_layer(h, src, dst, n, W2, a2_src, a2_dst, b2))
        return h
    edge_index = jnp.stack([src, dst])
    x = _layernorm(x + _L0_gnn_ref(x, edge_index, L0_gnn_W1, L0_gnn_b1, L0_gnn_W2, L0_gnn_b2, L0_gnn_W3, L0_gnn_b3), axis=-1)
    x = _layernorm(x + _L1_gnn_ref(x, L1_gnn_Wv, L1_gnn_bv, L1_gnn_wq, L1_gnn_bq, L1_gnn_wk, L1_gnn_bk, src, dst), axis=-1)
    x = _layernorm(x + _L2_gnn_ref(x, edge_index, edge_attr_64, L2_gnn_eps, L2_gnn_ee_w1, L2_gnn_ee_b1, L2_gnn_ee_w2, L2_gnn_ee_b2, L2_gnn_w1, L2_gnn_b1, L2_gnn_g1, L2_gnn_be1, L2_gnn_w2, L2_gnn_b2, L2_gnn_g2, L2_gnn_be2, L2_gnn_w3, L2_gnn_b3, L2_gnn_bn_g, L2_gnn_bn_b), axis=-1)
    x = _layernorm(x + _L3_gnn_ref(x, edge_index, L3_gnn_W1, L3_gnn_a1_src, L3_gnn_a1_dst, L3_gnn_b1, L3_gnn_W2, L3_gnn_a2_src, L3_gnn_a2_dst, L3_gnn_b2), axis=-1)
    return x

_drawn_inputs = setup_inputs


def setup_inputs(seed=0):
    import zlib

    import numpy as np

    out = dict(_drawn_inputs(seed))
    spreads = {'L0_gnn_b1': (0.0, 0.1),
     'L0_gnn_b2': (0.0, 0.1),
     'L0_gnn_b3': (0.0, 0.1),
     'L1_gnn_bv': (0.0, 0.1),
     'L2_gnn_ee_b1': (0.0, 0.315),
     'L2_gnn_ee_b2': (0.0, 0.1),
     'L2_gnn_b1': (0.0, 2.0),
     'L2_gnn_g1': (1.0, 0.2),
     'L2_gnn_be1': (0.0, 0.289),
     'L2_gnn_b2': (0.0, 0.1),
     'L2_gnn_g2': (1.0, 0.2),
     'L2_gnn_be2': (0.0, 0.274),
     'L2_gnn_b3': (0.0, 0.1),
     'L2_gnn_bn_g': (1.0, 0.2),
     'L2_gnn_bn_b': (0.0, 0.1),
     'L3_gnn_b1': (0.0, 0.1),
     'L3_gnn_b2': (0.0, 0.1)}
    factors = {'L0_gnn_W1': 2.855,
     'L3_gnn_a1_dst': 21.443,
     'L3_gnn_a2_src': 5.68,
     'L3_gnn_a2_dst': 24.572}
    for name, (base, spread) in spreads.items():
        noise = np.random.default_rng([zlib.crc32(name.encode()), seed]).standard_normal(out[name].shape)
        drawn = base * np.exp(spread * noise) if base else spread * noise
        out[name] = jnp.asarray(drawn.astype(out[name].dtype))
    for name, factor in factors.items():
        out[name] = (out[name] * factor).astype(out[name].dtype)
    return out
```

```python
import numpy as np
from contextlib import ExitStack

import concourse.bass as bass
from concourse import mybir

F32 = mybir.dt.float32
F16 = mybir.dt.float16
BF16 = mybir.dt.bfloat16
I32 = mybir.dt.int32
ALU = mybir.AluOpType
ACT = mybir.ActivationFunctionType
AX = mybir.AxisListType

N, D, E, EDIM, HID = 3125, 256, 50000, 64, 1024
P = 125
NB = N // P
NPAIR = E // (2 * P)
PAD = 128
LO = 2048.0
BIG = 1e30
LN_EPS = 1e-5
SLOPE = 0.2
GB = 5
NG = NB // GB
CENTER = 1562


TAKEN = []


class Core:
    pass


def sb_of(nc, ctx):
    return lambda name, shape, dt: ctx.enter_context(nc.sbuf_tensor(name, shape, dt))


def sem_of(nc, ctx):
    def sem(name):
        TAKEN.append(nc.alloc_semaphore(name))
        return TAKEN[-1]
    return sem


def recycle(nc):
    nc.clear_and_free_semaphores(TAKEN)
    TAKEN.clear()
    nc.all_engine_barrier()


def row_bcast(vec, parts, n):
    return bass.AP(vec.tensor, vec.offset, [[0, parts], [1, n]])


def stage_windows(nc, k, dst):
    with ExitStack() as ctx:
        sb, sem = sb_of(nc, ctx), sem_of(nc, ctx)
        H = NPAIR // 2
        pairs_i = sb("pairs_i", [H, 2, 2 * P], I32)
        pairs = sb("pairs", [H, 2, 2 * P], F32)
        ext = sb("ext", [H, 4], F32)
        diag = sb("diag", [H, 4, H], F32)
        ones = sb("ones_w", [H, NB], F32)
        blk_lo = sb("blk_lo", [NB, 1], F32)
        blk_hi = sb("blk_hi", [NB, 1], F32)
        pair_id = sb("pair_id", [NB, 2, H], F32)
        meets = sb("meets", [NB, 2, H], F32)
        cand = sb("cand", [NB, 2, 2, H], F32)
        lohi = sb("lohi", [NB, 2], F32)
        lohi_i = sb("lohi_i", [NB, 2], I32)
        s_in, s_tab, s_diag, s_row, s_win, s_out = (sem(x) for x in (
            "w_in", "w_tables", "w_diag", "w_rows", "w_windows", "w_out"))
        rows = k.ps[0:NB, 0, 0:4 * H].rearrange("p (s h) -> p s h", s=4)
        with nc.Block() as block:
            @block.sync
            def _(sp):
                sp.dma_start(pairs_i[:], dst.rearrange("(p a e) -> p a e", a=2, e=2 * P)).then_inc(s_in, 16)
                sp.wait_ge(s_win, 1)
                sp.dma_start(k.windows_dram, lohi_i[:]).then_inc(s_out, 16)
                sp.wait_ge(s_out, 16)
                sp.dma_start(k.windows[:], k.windows_dram.rearrange("b s -> (b s)")[None, :]).then_inc(s_out, 16)
                sp.wait_ge(s_out, 32)

            @block.gpsimd
            def _(pool):
                pool.memset(k.src_iota[:], 9999.0)
                pool.drain()
                pool.iota(k.src_iota[:, :, 0:P], pattern=[[P, NB], [1, P]], base=-CENTER, channel_multiplier=0,
                          allow_small_or_imprecise_dtypes=True)
                pool.iota(k.dst_iota[:], pattern=[[1, P]], base=0, channel_multiplier=0,
                          allow_small_or_imprecise_dtypes=True)
                pool.iota(blk_lo[:], pattern=[[0, 1]], base=0, channel_multiplier=P,
                          allow_small_or_imprecise_dtypes=True)
                pool.iota(blk_hi[:], pattern=[[0, 1]], base=P, channel_multiplier=P,
                          allow_small_or_imprecise_dtypes=True)
                pool.iota(pair_id[:], pattern=[[1, 2], [2, H]], base=1, channel_multiplier=0,
                          allow_small_or_imprecise_dtypes=True)
                pool.memset(k.ident[:], 0.0)
                pool.drain()
                pool.affine_select(out=k.ident[:], in_=k.ident[:], compare_op=ALU.not_equal, fill=1.0, base=0,
                                   pattern=[[-1, 128]], channel_multiplier=1)
                pool.drain().then_inc(s_tab, 1)

            @block.vector
            def _(dve):
                dve.memset(ones[:], 1.0)
                dve.wait_ge(s_in, 16)
                dve.tensor_copy(pairs[:], pairs_i[:])
                dve.drain()
                dve.tensor_reduce(ext[:, 0:2], pairs[:], AX.X, ALU.min)
                dve.tensor_reduce(ext[:, 2:4], pairs[:], AX.X, ALU.max)
                dve.wait_ge(s_tab, 1)
                dve.tensor_copy(k.ident16[:], k.ident[0:P, 0:P])
                dve.drain()
                for s in range(4):
                    dve.tensor_scalar(diag[:, s, :], k.ident[0:H, 0:H], ext[:, s:s + 1], None, ALU.mult)
                dve.drain().then_inc(s_diag, 1)
                dve.wait_ge(s_row, 1)
                dve.tensor_scalar(meets[:], rows[:, 2:4, :], blk_lo[:, 0:1], None, ALU.is_ge)
                dve.drain()
                dve.scalar_tensor_tensor(meets[:], rows[:, 0:2, :], blk_hi[:, 0:1], meets[:], ALU.is_lt, ALU.mult)
                dve.drain()
                dve.scalar_tensor_tensor(cand[:, 0], pair_id[:], float(NPAIR + 1), meets[:], ALU.subtract, ALU.mult)
                dve.tensor_tensor(cand[:, 1], pair_id[:], meets[:], ALU.mult)
                dve.drain()
                dve.tensor_reduce(lohi[:, 0:1], cand[:, 0], AX.XY, ALU.min)
                dve.tensor_reduce(lohi[:, 1:2], cand[:, 1], AX.XY, ALU.max)
                dve.drain()
                dve.tensor_scalar(lohi[:, 0:1], lohi[:, 0:1], float(NPAIR), float(NPAIR - 1), ALU.add, ALU.min)
                dve.drain()
                dve.scalar_tensor_tensor(lohi[:, 1:2], lohi[:, 0:1], 1.0, lohi[:, 1:2], ALU.add, ALU.max)
                dve.drain()
                dve.tensor_copy(lohi_i[:], lohi[:])
                dve.drain().then_inc(s_win, 1)

            @block.tensor
            def _(pe):
                pe.wait_ge(s_diag, 1)
                for s in range(4):
                    mm = pe.matmul(rows[:, s, :], ones[:, :], diag[:, s, :], start=(s == 0), stop=True,
                                   skip_group_check=True)
                mm.then_inc(s_row, 1)


def stage_edges(nc, k, srcT, dstT, eaT, ee_w1, ee_b1):
    with ExitStack() as ctx:
        sb, sem = sb_of(nc, ctx), sem_of(nc, ctx)
        ids_i = sb("ids_i", [P, 2, 2 * NPAIR], I32)
        src_f = sb("src_f", [P, 2 * NPAIR], F32)
        dst_f = sb("dst_f", [P, 2 * NPAIR], F32)
        dst_blk = sb("dst_blk", [P, P], F32)
        src_hot = sb("src_hot", [P, 2, NB, PAD], F16)
        dst_hot = sb("dst_hot", [P, 2, P], F16)
        dst_hot32 = sb("dst_hot32", [P, 2, P], F32)
        ea = sb("ea", [EDIM + 1, 2, P], F32)
        w_edge = sb("w_edge", [EDIM + 1, D], F32)
        relu = sb("relu_e", [P, 2, D + 1], F32)
        zero = sb("zero_e", [P, 512], F16)
        a_out = sb("a_out", [128, N], F16)
        e_out = sb("e_out", [P, D + 1], F32)
        s_ids, s_w, s_set, s_store = sem("e_ids"), sem("e_w"), sem("e_set"), sem("e_store")
        s_ea = [sem("e_ea0"), sem("e_ea1")]
        s_mlp, s_relu, s_acc = sem("e_mlp"), sem("e_relu"), sem("e_acc")
        s_hot, s_evac, s_free = sem("e_hot"), sem("e_evac"), sem("e_free")
        mlp = k.ps[0:P, 7, :].rearrange("p (i f) -> p i f", i=2)
        esum = k.ps[0:P, 6, 128:128 + D + 1]

        def chunk(c):
            return k.ps[:, c // 4, (c % 4) * P:(c % 4 + 1) * P]

        def window(eng, b):
            lo = eng.value_load(k.windows[0:1, bass.ds(b * 2, 1)], min_val=0, max_val=NPAIR - 1)
            hi = eng.value_load(k.windows[0:1, bass.ds(b * 2 + 1, 1)], min_val=1, max_val=NPAIR)
            return lo, hi

        with nc.Block() as block:
            @block.sync
            def _(sp):
                sp.dma_start(ids_i[:, 0], srcT).then_inc(s_ids, 16)
                sp.dma_start(ids_i[:, 1], dstT).then_inc(s_ids, 16)
                sp.dma_start(w_edge[0:EDIM], ee_w1).then_inc(s_w, 16)
                sp.dma_start(w_edge[EDIM:EDIM + 1], ee_b1[None, :]).then_inc(s_w, 16)
                done = sp.alloc_register("sp_pairs")
                sp.reg_mov(done, 0)
                with sp.Fori(0, NB) as b:
                    lo, hi = window(sp, b)
                    with sp.Fori(lo, hi) as j:
                        t = sp.snap(done)
                        for i in range(2):
                            sp.wait_ge(s_mlp, t * 2 + (i + 1))
                            sp.dma_start(ea[0:EDIM, i, :], eaT[:, bass.ds((j * 2 + i) * P, P)]).then_inc(s_ea[i], 16)
                        sp.reg_add(done, done, 1)

            @block.gpsimd
            def _(pool):
                with pool.Fori(0, NB) as b:
                    pool.wait_ge(s_evac, b * 2 + 4)
                    pool.dma_start(k.a_dram[bass.ds(b, 1)].rearrange("a p n -> (a p) n"), a_out[:]).then_inc(s_store, 16)
                    pool.dma_start(k.e_dram[bass.ds(b, 1)].rearrange("a p n -> (a p) n"), e_out[:]).then_inc(s_store, 16)
                    pool.wait_ge(s_store, b * 32 + 32)
                    pool.sem_inc(s_free, 1)

            @block.vector
            def _(dve):
                dve.memset(zero[:], 0.0)
                dve.memset(relu[:, :, D:D + 1], 1.0)
                dve.memset(ea[EDIM:EDIM + 1], 1.0)
                dve.tensor_copy(dst_blk[:], k.dst_iota[0:P])
                dve.wait_ge(s_ids, 32)
                dve.tensor_scalar(src_f[:], ids_i[:, 0], float(-CENTER), None, ALU.add)
                dve.tensor_copy(dst_f[:], ids_i[:, 1])
                dve.drain().then_inc(s_set, 1)
                dve.sem_inc(s_free, 1)
                done = dve.alloc_register("dve_pairs")
                dve.reg_mov(done, 0)
                with dve.Fori(0, NB) as b:
                    lo, hi = window(dve, b)
                    with dve.Fori(lo, hi) as j:
                        t = dve.snap(done)
                        for i in range(2):
                            dve.wait_ge(s_acc, t * 2 + (i + 1))
                            dve.tensor_scalar(dst_hot[:, i, :], dst_blk[:], dst_f[:, bass.ds(j * 2 + i, 1)], None, ALU.is_equal)
                            dve.tensor_scalar(dst_hot32[:, i, :], dst_blk[:], dst_f[:, bass.ds(j * 2 + i, 1)], None, ALU.is_equal)
                            dve.tensor_scalar(src_hot[:, i], k.src_iota[0:P], src_f[:, bass.ds(j * 2 + i, 1)], None,
                                              ALU.is_equal).then_inc(s_hot, 1)
                        dve.reg_add(done, done, 1)
                    dve.tensor_scalar(dst_blk[:], dst_blk[:], float(P), None, ALU.add)
                    dve.wait_ge(s_free, b + 1)
                    t = dve.snap(done)
                    dve.wait_ge(s_acc, t * 2 + 2)
                    dve.tensor_copy(a_out[:, 16 * P:24 * P].rearrange("p (k n) -> p k n", k=2), k.ps[:, 4:6, 0:4 * P])
                    dve.tensor_copy(a_out[:, 24 * P:], chunk(24))
                    dve.tensor_copy(k.deg[:, bass.ds(b, 1)], esum[:, D:D + 1])
                    dve.tensor_copy(e_out[:], esum)
                    dve.drain().then_inc(s_evac, 1)

            @block.scalar
            def _(act):
                act.wait_ge(s_set, 1)
                act.sem_inc(s_relu, 1)
                done = act.alloc_register("act_pairs")
                act.reg_mov(done, 0)
                with act.Fori(0, NB) as b:
                    lo, hi = window(act, b)
                    with act.Fori(lo, hi) as j:
                        t = act.snap(done)
                        act.wait_ge(s_acc, t * 2 + 2)
                        act.wait_ge(s_mlp, t * 2 + 4)
                        act.activation(relu[:, :, 0:D], mlp[:], ACT.Relu).then_inc(s_relu, 1)
                        act.reg_add(done, done, 1)
                    act.wait_ge(s_free, b + 1)
                    t = act.snap(done)
                    act.wait_ge(s_acc, t * 2 + 2)
                    act.copy(a_out[:, 0:16 * P].rearrange("p (k n) -> p k n", k=4), k.ps[:, 0:4, 0:4 * P])
                    act.drain().then_inc(s_evac, 1)

            @block.tensor
            def _(pe):
                pe.sem_inc(s_mlp, 2)
                pe.sem_inc(s_acc, 2)
                pe.sem_inc(s_evac, 2)
                pe.wait_ge(s_set, 1)
                pe.wait_ge(s_w, 32)
                done = pe.alloc_register("pe_pairs")
                pe.reg_mov(done, 0)
                with pe.Fori(0, NB) as b:
                    lo, hi = window(pe, b)
                    pe.wait_ge(s_evac, b * 2 + 2)
                    for bank in range(7):
                        pe.matmul(k.ps[:, bank, :], zero[:, 0:128], zero[:], start=True, stop=True,
                                  skip_group_check=True)
                    with pe.Fori(lo, hi) as j:
                        t = pe.snap(done)
                        pe.wait_ge(s_relu, t + 1)
                        for i in range(2):
                            pe.wait_ge(s_ea[i], t * 16 + 16)
                            pe.matmul(mlp[:, i], ea[:, i, :], w_edge[:], start=True, stop=True,
                                      skip_group_check=True).then_inc(s_mlp, 1)
                        for i in range(2):
                            pe.wait_ge(s_hot, t * 2 + (i + 1))
                            for c in range(NB):
                                pe.matmul(chunk(c), src_hot[:, i, c, :], dst_hot[:, i, :], start=False, stop=False,
                                          skip_group_check=True)
                            if i == 0:
                                pe.wait_ge(s_relu, t + 2)
                            pe.matmul(esum, dst_hot32[:, i, :], relu[:, i, :], start=False, stop=False,
                                      skip_group_check=True).then_inc(s_acc, 1)
                        pe.reg_add(done, done, 1)



def in_steps(eng, step, tail):
    for i in range(GB):
        step(i, i)
    with eng.Fori(1, NG) as it:
        for i in range(GB):
            step(it * GB + i, i)
    for i in range(tail):
        step(NB + i, i)


def at(s, lag, first=0):
    return not isinstance(s, int) or first <= s - lag < NB


def slot(s, lag, i):
    return (i - lag) % GB


BANK3 = (0, 1, 0, 1, 2)


def split(dve, hi, lo, x2048):
    dve.tensor_scalar(hi, x2048, 1.0 / LO, None, ALU.mult)
    dve.drain()
    return dve.scalar_tensor_tensor(lo, hi, -LO, x2048, ALU.mult, ALU.add)


def stage_first_split(nc, k, x, parts):
    with ExitStack() as ctx:
        sb, sem = sb_of(nc, ctx), sem_of(nc, ctx)
        g = sb("first_g", [P, 2, D], F32)
        s_x, s_deg, s_root = sem("f_x"), sem("f_deg"), sem("f_root")
        with nc.Block() as block:
            @block.sync
            def _(sp):
                sp.dma_start(k.xs[:], x.rearrange("(b p) d -> p b d", p=P)).then_inc(s_x, 16)

            @block.scalar
            def _(act):
                act.wait_ge(s_deg, 1)
                act.activation(k.dinv[:], k.deg1[:], ACT.Sqrt).then_inc(s_root, 1)

            @block.vector
            def _(dve):
                dve.tensor_scalar(k.deg1[:], k.deg[:], 1.0, None, ALU.add).then_inc(s_deg, 1)
                dve.wait_ge(s_root, 1)
                dve.reciprocal(k.dinv[:], k.dinv[:])
                dve.drain()
                dve.tensor_scalar(k.dinv_lo[:], k.dinv[:], LO, None, ALU.mult)
                dve.wait_ge(s_x, 16)
                dve.drain()
                with dve.Fori(0, NB) as b:
                    dve.tensor_scalar(g[:, 0, :], k.xs[:, bass.ds(b, 1), :].rearrange("p a d -> p (a d)"),
                                      k.dinv_lo[:, bass.ds(b, 1)], None, ALU.mult)
                    dve.drain()
                    out = parts[:, bass.ds(b, 1), :].rearrange("p a d -> p (a d)")
                    split(dve, out[:, 0:D], out[:, D:2 * D], g[:, 0, :])
                    dve.drain()


def blk(t, b):
    if isinstance(b, int):
        return t[:, b, :]
    return t[:, bass.ds(b, 1), :].rearrange("p a n -> p (a n)")


def col(t, b):
    return t[:, b:b + 1] if isinstance(b, int) else t[:, bass.ds(b, 1)]


def stage_aggregate(nc, k, name, parts, finish, w, bias, out_parts=None, rb1=None, eps=None):
    gin = finish == "gin"
    with ExitStack() as ctx:
        sb0, sem0 = sb_of(nc, ctx), sem_of(nc, ctx)
        sb = lambda n, s, d: sb0(f"{name}_{n}", s, d)
        sem = lambda n: sem0(f"{name}_{n}")
        a_ring = sb("a_ring", [128, GB, N], F16)
        wt = sb("w", [128, 2, D], F32)
        brow = sb("bias", [P, D], F32)
        z_lo = sb("z_lo", [P, GB, D], F32)
        z = sb("z", [P, GB, D], F32)
        zt = sb("zt", [128, GB, 2, P], F32)
        t = sb("t", [P, D], F32)
        g = sb("g", [P, D], F32)
        s_a = [sem(f"a{i}") for i in range(GB)]
        s_w, s_agg, s_zlo, s_z, s_tr, s_zt, s_y, s_post = (sem(x) for x in (
            "w", "agg", "zlo", "z", "tr", "zt", "y", "post"))
        ps_t = k.ps[:, 6, 0:2 * P].rearrange("p (h n) -> p h n", h=2)
        ps_y = k.ps[0:P, 7, 0:D]
        nw = 2
        if gin:
            e_in = sb("e_in", [P, GB, D + 1], F32)
            er = sb("er", [P, GB, D], F32)
            rb1row = sb("rb1", [P, D], F32)
            eps1 = sb("eps1", [P, 1], F32)
            s_e = [sem(f"e{i}") for i in range(GB)]
            s_er = sem("er")
            nw = 4
        with nc.Block() as block:
            @block.sync
            def _(sp):
                sp.dma_start(wt[:], w.rearrange("(h p) n -> p h n", h=2)).then_inc(s_w, 16)
                sp.dma_start(brow[:], row_bcast(bias, P, D)).then_inc(s_w, 16)
                if gin:
                    sp.dma_start(rb1row[:], row_bcast(rb1, P, D)).then_inc(s_w, 16)
                    sp.dma_start(eps1[:], row_bcast(eps, P, 1)).then_inc(s_w, 16)
                for i in range(GB):
                    sp.dma_start(a_ring[:, i, :], k.a_dram[i]).then_inc(s_a[i], 16)
                    if gin:
                        sp.dma_start(e_in[:, i, :], k.e_dram[i]).then_inc(s_e[i], 16)
                with sp.Fori(1, NG) as it:
                    for i in range(GB):
                        b = it * GB + i
                        sp.wait_ge(s_agg, it * GB + (i - GB + 1))
                        sp.dma_start(a_ring[:, i, :], k.a_dram[bass.ds(b, 1)].rearrange("a p n -> (a p) n")).then_inc(s_a[i], 16)
                        if gin:
                            sp.wait_ge(s_er, it * GB + (i - GB + 1))
                            sp.dma_start(e_in[:, i, :], k.e_dram[bass.ds(b, 1)].rearrange("a p n -> (a p) n")).then_inc(s_e[i], 16)

            @block.tensor
            def _(pe):
                pe.wait_ge(s_w, 16 * nw)

                def step(s, i, it=None):
                    if at(s, 0):
                        pe.wait_ge(s_a[i], 16 if it is None else it * 16 + 16)
                        bank = BANK3[i]
                        for c in range(NB):
                            pe.matmul(k.ps[0:P, bank, :], a_ring[0:P, i, c * P:(c + 1) * P], parts[:, c, :],
                                      start=(c == 0), stop=False)
                        pe.matmul(k.ps[0:P, bank, :], k.ident16[:], blk(parts, s), start=False,
                                  stop=True).then_inc(s_agg, 1)
                    if at(s, 1):
                        j = slot(s, 1, i)
                        pe.wait_ge(s_z, s)
                        if not isinstance(s, int) or s >= 2:
                            pe.wait_ge(s_zt, s - 1)
                        src = er if gin else z
                        for h in range(2):
                            tr = pe.transpose(ps_t[:, h, :], src[:, j, h * 128:(h + 1) * 128], k.ident[0:P, 0:P])
                        tr.then_inc(s_tr, 1)
                    if at(s, 2):
                        j = slot(s, 2, i)
                        pe.wait_ge(s_zt, s - 1)
                        if not isinstance(s, int) or s >= 3:
                            pe.wait_ge(s_post, s - 2)
                        for h in range(2):
                            mm = pe.matmul(ps_y, zt[:, j, h, :], wt[:, h, :], start=(h == 0), stop=(h == 1))
                        mm.then_inc(s_y, 1)

                for i in range(GB):
                    step(i, i)
                with pe.Fori(1, NG) as it:
                    for i in range(GB):
                        step(it * GB + i, i, it)
                for i in range(2):
                    step(NB + i, i)

            @block.scalar
            def _(act):
                def step(s, i):
                    if at(s, 0):
                        act.wait_ge(s_agg, s + 1)
                        act.mul(z_lo[:, i, :], k.ps[0:P, BANK3[i], D:2 * D], 1.0 / LO).then_inc(s_zlo, 1)
                    if at(s, 1):
                        act.wait_ge(s_tr, s)
                        if not isinstance(s, int) or s >= GB + 1:
                            act.wait_ge(s_y, s - GB)
                        act.copy(zt[:, slot(s, 1, i)], ps_t).then_inc(s_zt, 1)

                in_steps(act, step, 1)

            @block.vector
            def _(dve):
                dve.wait_ge(s_w, 16 * nw)
                if gin:
                    dve.tensor_scalar(rb1row[:], rb1row[:], 0.0, None, ALU.max)
                    dve.tensor_scalar(eps1[:], eps1[:], 1.0, None, ALU.add)
                    dve.drain()

                def step(s, i, it=None):
                    if at(s, 0):
                        if gin:
                            dve.wait_ge(s_e[i], 16 if it is None else it * 16 + 16)
                            dve.tensor_tensor(er[:, i, :], e_in[:, i, 0:D], rb1row[:], ALU.add).then_inc(s_er, 1)
                        dve.wait_ge(s_zlo, s + 1)
                        dve.tensor_tensor(z[:, i, :], k.ps[0:P, BANK3[i], 0:D], z_lo[:, i, :],
                                          ALU.add).then_inc(s_z, 1)
                    if at(s, 2):
                        b = s - 2
                        dve.wait_ge(s_y, s - 1)
                        if gin:
                            dve.scalar_tensor_tensor(t[:], blk(k.xs, b), eps1[:, 0:1], z[:, slot(s, 2, i), :],
                                                     ALU.mult, ALU.add)
                            dve.scalar_tensor_tensor(g[:], brow[:], col(k.deg1, b), ps_y, ALU.mult,
                                                     ALU.add).then_inc(s_post, 1)
                            dve.drain()
                            dve.tensor_tensor(blk(k.y, b), t[:], g[:], ALU.add)
                            dve.drain()
                            return
                        dve.scalar_tensor_tensor(t[:], ps_y, col(k.dinv, b), brow[:], ALU.mult,
                                                 ALU.add).then_inc(s_post, 1)
                        dve.drain()
                        if finish == "gcn":
                            dve.tensor_scalar(g[:], t[:], 0.0, col(k.dinv_lo, b), ALU.max, ALU.mult)
                            dve.drain()
                            out = blk(out_parts, b)
                            split(dve, out[:, 0:D], out[:, D:2 * D], g[:])
                        else:
                            dve.tensor_tensor(blk(k.xs, b), t[:], blk(k.xs, b), ALU.add)
                            dve.drain()
                            dve.bn_stats(blk(k.stats, b), blk(k.xs, b))
                        dve.drain()

                for i in range(GB):
                    step(i, i)
                with dve.Fori(1, NG) as it:
                    for i in range(GB):
                        step(it * GB + i, i, it)
                for i in range(2):
                    step(NB + i, i)


def stage_project(nc, k, name, source, norm, w=None, bias=None, wq=None, wk=None, bq=None, bk=None, parts=None):
    project = w is not None
    with ExitStack() as ctx:
        sb0, sem0 = sb_of(nc, ctx), sem_of(nc, ctx)
        sb = lambda n, s, d: sb0(f"{name}_{n}", s, d)
        sem = lambda n: sem0(f"{name}_{n}")
        wt = sb("w", [128, 2, D], F32)
        brow = sb("bias", [P, D], F32)
        wqk = sb("wqk", [P, 2, D], F32)
        bqk = sb("bqk", [P, 2], F32)
        xin = sb("xin", [P, GB, D], F32)
        xt = sb("xt", [128, GB, 2, P], F32)
        prod = sb("prod", [P, 2, D], F32)
        g = sb("g", [P, D], F32)
        s_w, s_x, s_tr, s_xt, s_y, s_h, s_var, s_root = (sem(x) for x in (
            "w", "x", "tr", "xt", "y", "h", "var", "root"))
        ps_t = [k.ps[:, m, 0:2 * P].rearrange("p (h n) -> p h n", h=2) for m in range(3)]
        ps_y = [k.ps[0:P, 3 + m, 0:D] for m in range(3)]
        loads = 0
        if project:
            loads = 3 + (bias is not None) + 2 * (bq is not None)
        with nc.Block() as block:
            @block.sync
            def _(sp):
                if project:
                    sp.dma_start(wt[:], w.rearrange("(h p) n -> p h n", h=2)).then_inc(s_w, 16)
                    sp.dma_start(wqk[:, 0, :], row_bcast(wq, P, D)).then_inc(s_w, 16)
                    sp.dma_start(wqk[:, 1, :], row_bcast(wk, P, D)).then_inc(s_w, 16)
                    if bias is not None:
                        sp.dma_start(brow[:], row_bcast(bias, P, D)).then_inc(s_w, 16)
                    if bq is not None:
                        sp.dma_start(bqk[:, 0:1], row_bcast(bq, P, 1)).then_inc(s_w, 16)
                        sp.dma_start(bqk[:, 1:2], row_bcast(bk, P, 1)).then_inc(s_w, 16)

            @block.scalar
            def _(act):
                if norm:
                    act.wait_ge(s_var, 1)
                    act.activation(k.rstd[:], k.rstd[:], ACT.Sqrt).then_inc(s_root, 1)
                if not project:
                    return

                def step(s, i):
                    act.wait_ge(s_tr, s + 1)
                    act.copy(xt[:, i], ps_t[BANK3[i]]).then_inc(s_xt, 1)

                in_steps(act, step, 0)

            @block.tensor
            def _(pe):
                if not project:
                    return
                pe.wait_ge(s_w, 16 * loads)

                def step(s, i):
                    if at(s, 0):
                        pe.wait_ge(s_x, s + 1)
                        for h in range(2):
                            tr = pe.transpose(ps_t[BANK3[i]][:, h, :], xin[:, i, h * 128:(h + 1) * 128],
                                              k.ident[0:P, 0:P])
                        tr.then_inc(s_tr, 1)
                    if at(s, 1):
                        j = slot(s, 1, i)
                        pe.wait_ge(s_xt, s)
                        if not isinstance(s, int) or s >= 3:
                            pe.wait_ge(s_h, s - 2)
                        for h in range(2):
                            mm = pe.matmul(ps_y[BANK3[j]], xt[:, j, h, :], wt[:, h, :], start=(h == 0), stop=(h == 1))
                        mm.then_inc(s_y, 1)

                in_steps(pe, step, 1)

            @block.vector
            def _(dve):
                if norm:
                    for b in range(NB):
                        dve.bn_aggr(k.mv[:, b, :], k.stats[:, b, :])
                    dve.drain()
                    dve.tensor_scalar(k.rstd[:], k.mv[:, :, 1], LN_EPS, None, ALU.add).then_inc(s_var, 1)
                    dve.tensor_copy(k.mean[:], k.mv[:, :, 0])
                    dve.wait_ge(s_root, 1)
                    dve.reciprocal(k.rstd[:], k.rstd[:])
                    dve.drain()
                if project:
                    dve.memset(k.h[:, :, D:D + 1], 1.0)
                    dve.wait_ge(s_w, 16 * loads)

                def step(s, i):
                    if at(s, 0):
                        if norm:
                            dve.tensor_scalar(blk(k.xs, s), blk(k.xs, s), col(k.mean, s), col(k.rstd, s),
                                              ALU.subtract, ALU.mult)
                            dve.drain()
                        if project:
                            if not isinstance(s, int) or s >= GB:
                                dve.wait_ge(s_tr, s - GB + 1)
                            dve.tensor_scalar(xin[:, i, :], blk(source, s), 1.0, None, ALU.mult).then_inc(s_x, 1)
                        if parts is not None:
                            dve.tensor_scalar(g[:], blk(k.xs, s), LO, None, ALU.mult)
                            dve.drain()
                            out = blk(parts, s)
                            split(dve, out[:, 0:D], out[:, D:2 * D], g[:])
                            dve.drain()
                    if project and at(s, 2):
                        b = s - 2
                        j = slot(s, 2, i)
                        dve.wait_ge(s_y, s - 1)
                        h = blk(k.h, b)[:, 0:D]
                        if bias is None:
                            dve.tensor_scalar(h, ps_y[BANK3[j]], 1.0, None, ALU.mult).then_inc(s_h, 1)
                        else:
                            dve.tensor_tensor(h, ps_y[BANK3[j]], brow[:], ALU.add).then_inc(s_h, 1)
                        dve.drain()
                        for v in range(2):
                            dve.tensor_tensor(prod[:, v, :], h, wqk[:, v, :], ALU.mult)
                        dve.drain()
                        dve.tensor_reduce(col(k.q, b), prod[:, 0, :], AX.X, ALU.add)
                        dve.tensor_reduce(col(k.kk, b), prod[:, 1, :], AX.X, ALU.add)
                        dve.drain()

                in_steps(dve, step, 2 if project else 0)
                if bq is not None:
                    dve.tensor_scalar(k.q[:], k.q[:], bqk[:, 0:1], None, ALU.add)
                    dve.tensor_scalar(k.kk[:], k.kk[:], bqk[:, 1:2], None, ALU.add)
                    dve.drain()
                if project:
                    dve.tensor_scalar(k.q_slope[:], k.q[:], SLOPE, None, ALU.mult)


def stage_attention(nc, k, name, finish, bias=None):
    GW = GB * P
    with ExitStack() as ctx:
        sb0, sem0 = sb_of(nc, ctx), sem_of(nc, ctx)
        sb = lambda n, s, d: sb0(f"{name}_{n}", s, d)
        sem = lambda n: sem0(f"{name}_{n}")
        a_grp = sb("a_grp", [128, 2, GB, N], F16)
        brow = sb("bias", [P, D], F32)
        mask = sb("mask", [P, GB, P], BF16)
        qmax = sb("qmax", [P, GB, P], F32)
        top = sb("top", [P, GB], F32)
        tops = sb("tops", [P, GB], F32)
        rcol = sb("rcol", [P, 2, GB], F32)
        kslope = sb("kslope", [P, NB], F32)
        diag = sb("diag", [P, 2, GB, P], F32)
        ones = sb("ones", [P, P], F32)
        zero = sb("zero", [P, D + 1], F16)
        rrow = sb("rrow", [P, 2, GB, P], F32)
        e = sb("e", [P, 3, 2, GW], F32)
        x = sb("x", [P, GB, P], F32)
        p = sb("p", [P, 3, GB, P], F32)
        den = sb("den", [P, GB], F32)
        t = sb("t", [P, GB, D], F32)
        s_a = [sem("a0"), sem("a1")]
        s_w, s_qmax, s_tr, s_diag, s_bc, s_r, s_e, s_x, s_p, s_pv, s_sum, s_out, s_zero = (sem(v) for v in (
            "w", "qmax", "tr", "diag", "bc", "r", "e", "x", "p", "pv", "sum", "out", "zero"))

        def spread(r):
            return (k.ps[0:P, 5 + 2 * r, 0:4 * P].rearrange("p (j n) -> p j n", j=4),
                    k.ps[0:P, 6, r * P:(r + 1) * P])

        def free_after(i):
            return (3, 3, 2, 2, 5)[i]

        def chunks(eng, body):
            with eng.Fori(0, NG) as it:
                for i in range(GB):
                    body(it * GB + i, i)

        with nc.Block() as block:
            @block.sync
            def _(sp):
                if bias is not None:
                    sp.dma_start(brow[:], row_bcast(bias, P, D)).then_inc(s_w, 16)
                for g in range(NG):
                    if g >= 2:
                        sp.wait_ge(s_p, GB + NB * (g - 1))
                    sp.dma_start(a_grp[:, g % 2], k.a_dram[g * GB:(g + 1) * GB].rearrange("b p n -> p b n")).then_inc(s_a[g % 2], 16)

            @block.scalar
            def _(act):
                for g in range(NG):
                    act.wait_ge(s_bc, g + 1)
                    for r in range(2):
                        many, one = spread(r)
                        act.copy(rrow[:, r, 0:4, :], many)
                        act.copy(rrow[:, r, 4, :], one)
                    act.drain().then_inc(s_r, 1)

                    def body(c, i, g=g):
                        act.wait_ge(s_x, c + (g * NB - free_after(i) + 1 + GB))
                        act.activation(e[:, BANK3[i], 0, :], rrow[:, 0].rearrange("p j n -> p (j n)"), ACT.Exp,
                                       bias=col(k.q, c))
                        act.activation(e[:, BANK3[i], 1, :], rrow[:, 1].rearrange("p j n -> p (j n)"), ACT.Exp,
                                       bias=col(k.q_slope, c)).then_inc(s_e, 1)

                    chunks(act, body)

            @block.vector
            def _(dve):
                dve.memset(ones[:], 1.0)
                dve.memset(zero[:], 0.0)
                dve.tensor_scalar(kslope[:], k.kk[:], SLOPE, None, ALU.mult)
                if bias is not None:
                    dve.wait_ge(s_w, 16)
                dve.drain().then_inc(s_zero, 1)
                dve.sem_inc(s_x, GB)
                dve.sem_inc(s_p, GB)
                for g in range(NG):
                    a = a_grp[0:P, g % 2]
                    dve.wait_ge(s_a[g % 2], 16 * (g // 2 + 1))
                    dve.memset(qmax[:], -3e38)
                    dve.drain()

                    def greatest(c, i):
                        dve.tensor_scalar(mask[:], a[:, :, bass.ds(c * P, P)], 0.0, -BIG, ALU.is_equal, ALU.mult)
                        dve.drain()
                        dve.scalar_tensor_tensor(qmax[:], mask[:], col(k.q, c), qmax[:], ALU.add, ALU.max)
                        dve.drain()

                    chunks(dve, greatest)
                    dve.drain().then_inc(s_qmax, 1)
                    dve.wait_ge(s_tr, g + 1)
                    many, one = spread(0)
                    dve.tensor_reduce(top[:, 0:4], many, AX.X, ALU.max)
                    dve.tensor_reduce(top[:, 4:5], one, AX.X, ALU.max)
                    dve.drain()
                    gs = slice(g * GB, (g + 1) * GB)
                    dve.tensor_tensor(top[:], top[:], k.kk[:, gs], ALU.add)
                    dve.drain()
                    dve.tensor_scalar(tops[:], top[:], SLOPE, None, ALU.mult)
                    dve.drain()
                    dve.tensor_tensor(top[:], top[:], tops[:], ALU.max)
                    dve.drain()
                    dve.tensor_tensor(rcol[:, 0, :], k.kk[:, gs], top[:], ALU.subtract)
                    dve.tensor_tensor(rcol[:, 1, :], kslope[:, gs], top[:], ALU.subtract)
                    dve.drain()
                    for r in range(2):
                        for j in range(GB):
                            dve.tensor_scalar(diag[:, r, j, :], k.ident[0:P, 0:P], rcol[:, r, j:j + 1], None, ALU.mult)
                    dve.drain().then_inc(s_diag, 1)

                    def weights(c, i, g=g):
                        dve.wait_ge(s_e, c + (g * NB + 1))
                        m = BANK3[i]
                        dve.tensor_tensor(x[:].rearrange("p j n -> p (j n)"), e[:, m, 0, :], e[:, m, 1, :],
                                          ALU.max).then_inc(s_x, 1)
                        dve.drain()
                        dve.wait_ge(s_pv, c + (g * NB - free_after(i) + 1 + GB))
                        dve.scalar_tensor_tensor(p[:, m], x[:], 1.0, a[:, :, bass.ds(c * P, P)], ALU.min,
                                                 ALU.mult).then_inc(s_p, 1)
                        dve.drain()

                    chunks(dve, weights)
                    dve.wait_ge(s_sum, g + 1)
                    dve.tensor_scalar(den[:], k.ps[0:P, 0:GB, D], 1e-30, None, ALU.max)
                    dve.drain()
                    dve.reciprocal(den[:], den[:])
                    dve.drain()
                    for j in range(GB):
                        b = g * GB + j
                        other = k.xs[:, b, :] if finish == "res" else brow[:]
                        out = k.xs[:, b, :] if finish == "res" else t[:, j, :]
                        last = dve.scalar_tensor_tensor(out, k.ps[0:P, j, 0:D], den[:, j:j + 1], other, ALU.mult, ALU.add)
                    last.then_inc(s_out, 1)
                    dve.drain()
                    for j in range(GB):
                        b = g * GB + j
                        if finish == "relu":
                            dve.tensor_scalar(k.y[:, b, :], t[:, j, :], 0.0, None, ALU.max)
                        if finish == "both":
                            dve.scalar_tensor_tensor(k.xs[:, b, :], t[:, j, :], 0.0, k.xs[:, b, :], ALU.max, ALU.add)
                    dve.drain()
                    if finish != "relu":
                        for j in range(GB):
                            dve.bn_stats(k.stats[:, g * GB + j, :], k.xs[:, g * GB + j, :])

            @block.tensor
            def _(pe):
                pe.wait_ge(s_zero, 1)
                pe.sem_inc(s_pv, GB)
                for g in range(NG):
                    pe.wait_ge(s_qmax, g + 1)
                    many, one = spread(0)
                    for j in range(GB):
                        tr = pe.transpose(many[:, j, :] if j < 4 else one, qmax[:, j, :], k.ident[0:P, 0:P])
                    tr.then_inc(s_tr, 1)
                    pe.wait_ge(s_diag, g + 1)
                    for r in range(2):
                        many, one = spread(r)
                        pe.matmul(many, ones[:], diag[:, r, 0:4, :], start=True, stop=True, skip_group_check=True)
                        mm = pe.matmul(one, ones[:], diag[:, r, 4, :], start=True, stop=True, skip_group_check=True)
                    mm.then_inc(s_bc, 1)
                    if g >= 1:
                        pe.wait_ge(s_out, g)
                    for j in range(GB):
                        pe.matmul(k.ps[0:P, j, 0:D + 1], zero[:, 0:P], zero[:], start=True, stop=False,
                                  skip_group_check=True)

                    def body(c, i, g=g):
                        pe.wait_ge(s_p, c + (g * NB + 1 + GB))
                        for j in range(GB):
                            mm = pe.matmul(k.ps[0:P, j, 0:D + 1], p[:, BANK3[i], j, :], blk(k.h, c), start=False,
                                           stop=False, skip_group_check=True)
                        mm.then_inc(s_pv, 1)

                    chunks(pe, body)
                    pe.drain().then_inc(s_sum, 1)


def stage_mlp(nc, k, w):
    KH = HID // 128
    with ExitStack() as ctx:
        sb, sem = sb_of(nc, ctx), sem_of(nc, ctx)
        w1 = sb("m_w1", [128, 2, HID], F32)
        w2 = sb("m_w2", [128, KH, HID], F32)
        w3 = sb("m_w3", [128, KH, D], F32)
        rows = sb("m_rows", [P, 2, HID], F32)
        rows3 = sb("m_rows3", [P, 3, D], F32)
        cols = sb("m_cols", [128, 4, KH], F32)
        hin = sb("m_hin", [P, D], F32)
        ht = sb("m_ht", [128, 2, P], F32)
        u = sb("m_u", [P, 2, HID], F32)
        un = sb("m_un", [P, 2, HID], F32)
        ut = sb("m_ut", [128, 2, KH, P], F32)
        st = sb("m_st", [P, 2, 2, 6], F32)
        mv = sb("m_mv", [P, 3, 2], F32)
        rs = sb("m_rs", [P, 3, 2], F32)
        r3 = sb("m_r3", [P, D], F32)
        st3 = sb("m_st3", [P, 6], F32)
        s_w, s_in, s_tr0, s_ht = sem("m_w"), sem("m_in"), sem("m_tr0"), sem("m_ht")
        s_mm = [sem("m_mm1"), sem("m_mm2"), sem("m_mm3")]
        s_var = [sem("m_var1"), sem("m_var2"), sem("m_var3")]
        s_root = [sem("m_root1"), sem("m_root2"), sem("m_root3")]
        s_scale = [sem("m_scale1"), sem("m_scale2")]
        s_un = [sem("m_un1"), sem("m_un2")]
        s_tr = [sem("m_tr1"), sem("m_tr2")]
        s_ut = [sem("m_ut1"), sem("m_ut2")]
        s_read = [sem("m_read1"), sem("m_read2"), sem("m_read3")]
        ps_h = k.ps[:, 0, 0:2 * P].rearrange("p (h n) -> p h n", h=2)
        ps_m = [k.ps[0:P, 1:3, :], k.ps[0:P, 3:5, :]]
        ps_3 = k.ps[0:P, 7, 0:D]
        ps_u = k.ps[:, 5:7, 0:4 * P].rearrange("p m (c n) -> p m c n", c=4)
        with nc.Block() as block:
            @block.sync
            def _(sp):
                sp.dma_start(w1[:], w["w1"].rearrange("(c p) n -> p c n", p=128)).then_inc(s_w, 16)
                sp.dma_start(w2[:], w["w2"].rearrange("(c p) n -> p c n", p=128)).then_inc(s_w, 16)
                sp.dma_start(w3[:], w["w3"].rearrange("(c p) n -> p c n", p=128)).then_inc(s_w, 16)
                for n, v in enumerate(("b1", "b2")):
                    sp.dma_start(rows[:, n, :], row_bcast(w[v], P, HID)).then_inc(s_w, 16)
                for n, v in enumerate(("b3", "bn_g", "bn_b")):
                    sp.dma_start(rows3[:, n, :], row_bcast(w[v], P, D)).then_inc(s_w, 16)
                for n, v in enumerate(("g1", "be1", "g2", "be2")):
                    with nc.allow_non_contiguous_dma(reason="4 vectors of 1024"):
                        sp.dma_start(cols[:, n, :], w[v].rearrange("(c p) -> p c", p=128)).then_inc(s_w, 16)

            @block.tensor
            def _(pe):
                pe.wait_ge(s_w, 16 * 12)

                def first(b):
                    pe.wait_ge(s_in, b + 1)
                    for h in range(2):
                        tr = pe.transpose(ps_h[:, h, :], hin[:, h * 128:(h + 1) * 128], k.ident[0:P, 0:P])
                    tr.then_inc(s_tr0, 1)
                    pe.wait_ge(s_ht, b + 1)
                    if not (isinstance(b, int) and b == 0):
                        pe.wait_ge(s_read[0], b)
                    for n in range(2):
                        for c in range(2):
                            mm = pe.matmul(ps_m[0][:, n, :], ht[:, c, :], w1[:, c, n * 512:(n + 1) * 512],
                                           start=(c == 0), stop=(c == 1))
                    mm.then_inc(s_mm[0], 1)

                def turn(l, b):
                    pe.wait_ge(s_un[l], b + 1)
                    if l == 1:
                        pe.wait_ge(s_ut[0], b + 1)
                    elif not (isinstance(b, int) and b == 0):
                        pe.wait_ge(s_ut[1], b)
                    for c in range(KH):
                        tr = pe.transpose(ps_u[:, c // 4, c % 4, :], un[:, l, c * 128:(c + 1) * 128], k.ident[0:P, 0:P])
                    tr.then_inc(s_tr[l], 1)
                    pe.wait_ge(s_ut[l], b + 1)

                def second(b):
                    turn(0, b)
                    if not (isinstance(b, int) and b == 0):
                        pe.wait_ge(s_read[1], b)
                    for n in range(2):
                        for c in range(KH):
                            mm = pe.matmul(ps_m[1][:, n, :], ut[:, 0, c, :], w2[:, c, n * 512:(n + 1) * 512],
                                           start=(c == 0), stop=(c == KH - 1))
                    mm.then_inc(s_mm[1], 1)

                def third(b):
                    turn(1, b)
                    if not (isinstance(b, int) and b == 0):
                        pe.wait_ge(s_read[2], b)
                    for c in range(KH):
                        mm = pe.matmul(ps_3, ut[:, 1, c, :], w3[:, c, :], start=(c == 0), stop=(c == KH - 1))
                    mm.then_inc(s_mm[2], 1)

                first(0)
                second(0)
                with pe.Fori(1, NB) as b:
                    first(b)
                    third(b - 1)
                    second(b)
                third(NB - 1)

            @block.scalar
            def _(act):
                act.wait_ge(s_w, 16 * 12)

                def head(b):
                    act.wait_ge(s_tr0, b + 1)
                    act.copy(ht[:], ps_h).then_inc(s_ht, 1)

                def root(l, b):
                    act.wait_ge(s_var[l], b + 1)
                    act.activation(rs[:, l, 0:1], rs[:, l, 0:1], ACT.Sqrt).then_inc(s_root[l], 1)

                def hidden(l, b):
                    root(l, b)
                    act.wait_ge(s_scale[l], b + 1)
                    if not (isinstance(b, int) and b == 0):
                        act.wait_ge(s_tr[l], b)
                    act.activation(un[:, l, :], u[:, l, :], ACT.Identity, bias=rs[:, l, 1:2],
                                   scale=rs[:, l, 0:1]).then_inc(s_un[l], 1)

                def turned(l, b):
                    act.wait_ge(s_tr[l], b + 1)
                    if not (isinstance(b, int) and b == 0):
                        act.wait_ge(s_mm[l + 1], b)
                    for c in range(KH):
                        last = act.activation(ut[:, l, c, :], ps_u[:, c // 4, c % 4, :], ACT.Relu,
                                              bias=cols[:, 2 * l + 1, c:c + 1], scale=cols[:, 2 * l, c:c + 1])
                    last.then_inc(s_ut[l], 1)

                def block_of(b, before=None):
                    head(b)
                    hidden(0, b)
                    if before is not None:
                        turned(1, before)
                    turned(0, b)
                    if before is not None:
                        root(2, before)
                    hidden(1, b)

                block_of(0)
                with act.Fori(1, NB) as b:
                    block_of(b, b - 1)
                turned(1, NB - 1)
                root(2, NB - 1)

            @block.vector
            def _(dve):
                dve.wait_ge(s_w, 16 * 12)

                def scales(l, b):
                    dve.bn_aggr(mv[:, l, :], st[:, l] if l < 2 else st3[:])
                    dve.drain()
                    dve.tensor_scalar(rs[:, l, 0:1], mv[:, l, 1:2], LN_EPS, None, ALU.add).then_inc(s_var[l], 1)
                    dve.wait_ge(s_root[l], b + 1)
                    dve.reciprocal(rs[:, l, 0:1], rs[:, l, 0:1])
                    dve.drain()

                def hidden(l, b):
                    dve.wait_ge(s_mm[l], b + 1)
                    if not (isinstance(b, int) and b == 0):
                        dve.wait_ge(s_un[l], b)
                    dve.tensor_tensor(u[:, l, :].rearrange("p (m n) -> p m n", m=2), ps_m[l],
                                      rows[:, l, :].rearrange("p (m n) -> p m n", m=2), ALU.add).then_inc(s_read[l], 1)
                    dve.drain()
                    for m in range(2):
                        dve.bn_stats(st[:, l, m, :], u[:, l, m * 512:(m + 1) * 512])
                    dve.drain()
                    scales(l, b)
                    dve.scalar_tensor_tensor(rs[:, l, 1:2], mv[:, l, 0:1], -1.0, rs[:, l, 0:1], ALU.mult,
                                             ALU.mult).then_inc(s_scale[l], 1)

                def bring(b):
                    if not (isinstance(b, int) and b == 0):
                        dve.wait_ge(s_tr0, b)
                    dve.tensor_scalar(hin[:], blk(k.y, b), 1.0, None, ALU.mult).then_inc(s_in, 1)

                def out(b):
                    dve.wait_ge(s_mm[2], b + 1)
                    dve.tensor_tensor(r3[:], ps_3, rows3[:, 0, :], ALU.add).then_inc(s_read[2], 1)
                    dve.drain()
                    dve.tensor_tensor(r3[:], r3[:], blk(k.xs, b), ALU.add)
                    dve.drain()
                    dve.bn_stats(st3[:], r3[:])
                    dve.drain()
                    scales(2, b)
                    dve.tensor_scalar(r3[:], r3[:], mv[:, 2, 0:1], rs[:, 2, 0:1], ALU.subtract, ALU.mult)
                    dve.drain()
                    dve.tensor_tensor(r3[:], r3[:], rows3[:, 1, :], ALU.mult)
                    dve.drain()
                    dve.tensor_tensor(r3[:], r3[:], rows3[:, 2, :], ALU.add)
                    dve.drain()
                    dve.scalar_tensor_tensor(blk(k.xs, b), r3[:], 0.0, blk(k.xs, b), ALU.max, ALU.add)
                    dve.drain()
                    dve.bn_stats(blk(k.stats, b), blk(k.xs, b))
                    dve.drain()

                bring(0)
                hidden(0, 0)
                bring(1)
                hidden(1, 0)
                with dve.Fori(1, NB - 1) as b:
                    hidden(0, b)
                    bring(b + 1)
                    out(b - 1)
                    hidden(1, b)
                for b in (NB - 1,):
                    hidden(0, b)
                    out(b - 1)
                    hidden(1, b)
                out(NB - 1)


def stage_add_loops(nc, k):
    with ExitStack() as ctx:
        sb, sem = sb_of(nc, ctx), sem_of(nc, ctx)
        diag = sb("loops", [P, NB, P], F16)
        s_in, s_add, s_out = sem("l_in"), sem("l_add"), sem("l_out")
        with nc.Block() as block:
            @block.sync
            def _(sp):
                for b in range(NB):
                    sp.dma_start(diag[:, b, :], k.a_dram[b, 0:P, b * P:(b + 1) * P]).then_inc(s_in, 16)
                sp.wait_ge(s_add, 1)
                for b in range(NB):
                    sp.dma_start(k.a_dram[b, 0:P, b * P:(b + 1) * P], diag[:, b, :]).then_inc(s_out, 16)
                sp.wait_ge(s_out, 16 * NB)

            @block.vector
            def _(dve):
                dve.wait_ge(s_in, 16 * NB)
                for b in range(NB):
                    dve.tensor_tensor(diag[:, b, :], diag[:, b, :], k.ident16[:], ALU.add)
                dve.drain().then_inc(s_add, 1)


def stage_last(nc, k, out):
    with ExitStack() as ctx:
        sem = sem_of(nc, ctx)
        s_norm, s_store = sem("o_norm"), sem("o_store")
        with nc.Block() as block:
            @block.sync
            def _(sp):
                sp.dma_start(out.rearrange("(b p) d -> p b d", p=P), k.xs[:]).then_inc(s_store, 16)
                sp.wait_ge(s_store, 16)


def program(nc, ins, outs, upto=99):
    TAKEN.clear()
    with ExitStack() as ctx:
        sb = sb_of(nc, ctx)
        k = Core()
        k.ps = ctx.enter_context(nc.psum_tensor("ps", [128, 8, 512], F32))
        k.ident = sb("ident", [128, 128], F32)
        k.ident16 = sb("ident16", [P, P], F16)
        k.windows = sb("windows", [1, 2 * NB], I32)
        k.deg, k.deg1, k.dinv, k.dinv_lo, k.rstd, k.mean, k.q, k.kk, k.q_slope = (sb(v, [P, NB], F32) for v in (
            "deg", "deg1", "dinv", "dinv_lo", "rstd", "mean", "q", "kk", "q_slope"))
        k.stats = sb("stats", [P, NB, 6], F32)
        k.mv = sb("mv", [P, NB, 2], F32)
        k.windows_dram = nc.dram_tensor("windows_dram", (NB, 2), I32).ap()
        k.a_dram = nc.dram_tensor("a_dram", (NB, 128, N), F16).ap()
        k.e_dram = nc.dram_tensor("e_dram", (NB, P, D + 1), F32).ap()
        with ExitStack() as early:
            sbe = sb_of(nc, early)
            k.src_iota = sbe("src_iota", [128, NB, PAD], F16)
            k.dst_iota = sbe("dst_iota", [128, P], F32)
            stage_windows(nc, k, ins["dst"])
            stage_edges(nc, k, ins["srcT"], ins["dstT"], ins["eaT"], ins["L2_gnn_ee_w1"], ins["L2_gnn_ee_b1"])
        k.xs = sb("xs", [P, NB, D], F32)

        def finish():
            stage_last(nc, k, outs["out"])

        with ExitStack() as gcn:
            sbg = sb_of(nc, gcn)
            pa, pb = sbg("parts_a", [P, NB, 2 * D], F16), sbg("parts_b", [P, NB, 2 * D], F16)
            stage_first_split(nc, k, ins["x"], pa)
            stage_aggregate(nc, k, "g1", pa, "gcn", ins["W1T"], ins["L0_gnn_b1"], out_parts=pb)
            stage_aggregate(nc, k, "g2", pb, "gcn", ins["W2T"], ins["L0_gnn_b2"], out_parts=pa)
            stage_aggregate(nc, k, "g3", pa, "last", ins["W3T"], ins["L0_gnn_b3"])
        if upto == 1:
            return finish()
        with ExitStack() as att:
            k.h = sb_of(nc, att)("h_att", [P, NB, D + 1], F32)
            stage_project(nc, k, "p1", k.xs, True, ins["L1_gnn_Wv"], ins["L1_gnn_bv"], ins["L1_gnn_wq"],
                          ins["L1_gnn_wk"], ins["L1_gnn_bq"], ins["L1_gnn_bk"])
            stage_attention(nc, k, "t1", "res")
        if upto == 2:
            return finish()
        k.y = sb("y", [P, NB, D], F32)
        with ExitStack() as gin:
            pa = sb_of(nc, gin)("parts_c", [P, NB, 2 * D], F16)
            stage_project(nc, k, "p2", k.xs, True, parts=pa)
            stage_aggregate(nc, k, "gi", pa, "gin", ins["L2_gnn_ee_w2"], ins["L2_gnn_ee_b2"],
                            rb1=ins["L2_gnn_ee_b1"], eps=ins["L2_gnn_eps"])
        stage_mlp(nc, k, {v: ins["L2_gnn_" + v] for v in ("w1", "w2", "w3", "b1", "b2", "b3", "g1", "be1", "g2", "be2", "bn_g", "bn_b")})
        if upto == 3:
            return finish()
        recycle(nc)
        stage_add_loops(nc, k)
        k.h = sb("h_att2", [P, NB, D + 1], F32)
        stage_project(nc, k, "p3", k.xs, True, ins["L3_gnn_W1"], None, ins["L3_gnn_a1_src"], ins["L3_gnn_a1_dst"])
        stage_attention(nc, k, "t3", "relu", ins["L3_gnn_b1"])
        stage_project(nc, k, "p4", k.y, False, ins["L3_gnn_W2"], None, ins["L3_gnn_a2_src"], ins["L3_gnn_a2_dst"])
        stage_attention(nc, k, "t4", "both", ins["L3_gnn_b2"])
        stage_project(nc, k, "p5", k.xs, True)
        finish()


_AS_THEY_ARE = ("x", "dst", "L0_gnn_b1", "L0_gnn_b2", "L0_gnn_b3", "L1_gnn_Wv", "L1_gnn_bv", "L1_gnn_wq", "L1_gnn_bq",
                "L1_gnn_wk", "L1_gnn_bk", "L2_gnn_eps", "L2_gnn_ee_w1", "L2_gnn_ee_b1", "L2_gnn_ee_w2", "L2_gnn_ee_b2",
                "L2_gnn_w1", "L2_gnn_b1", "L2_gnn_g1", "L2_gnn_be1", "L2_gnn_w2", "L2_gnn_b2", "L2_gnn_g2",
                "L2_gnn_be2", "L2_gnn_w3", "L2_gnn_b3", "L2_gnn_bn_g", "L2_gnn_bn_b", "L3_gnn_W1", "L3_gnn_a1_src",
                "L3_gnn_a1_dst", "L3_gnn_b1", "L3_gnn_W2", "L3_gnn_a2_src", "L3_gnn_a2_dst", "L3_gnn_b2")


def kernel(**inputs):
    import concourse.bacc as bacc
    from concourse.bass_utils import run_bass_kernel_spmd

    a = {n: np.ascontiguousarray(inputs[n]).reshape(inputs[n].shape or (1,)) for n in _AS_THEY_ARE}
    a["srcT"] = np.ascontiguousarray(inputs["src"].reshape(E // P, P).T)
    a["dstT"] = np.ascontiguousarray(inputs["dst"].reshape(E // P, P).T)
    a["eaT"] = np.ascontiguousarray(inputs["edge_attr_64"].T)
    for n in ("W1", "W2", "W3"):
        a[n + "T"] = np.ascontiguousarray(inputs["L0_gnn_" + n].T)
    nc = bacc.Bacc("TRN2", target_bir_lowering=False, num_devices=1)
    ins = {n: nc.dram_tensor("in_" + n, v.shape, mybir.dt.from_np(v.dtype), kind="ExternalInput").ap()
           for n, v in a.items()}
    out = nc.dram_tensor("out_x", (N, D), F32, kind="ExternalOutput").ap()
    program(nc, ins, {"out": out})
    r = run_bass_kernel_spmd(nc, [{"in_" + n: v for n, v in a.items()}], core_ids=[0])
    return r.results[0]["out_x"]
```

```python
import numpy as np
from contextlib import ExitStack

import concourse.bass as bass
from concourse import mybir

F32 = mybir.dt.float32
F16 = mybir.dt.float16
BF16 = mybir.dt.bfloat16
I32 = mybir.dt.int32
ALU = mybir.AluOpType
ACT = mybir.ActivationFunctionType
AX = mybir.AxisListType

N, D, E, EDIM, HID = 3125, 256, 50000, 64, 1024
P = 125
NB = N // P
NPAIR = E // (2 * P)
PAD = 128
LO = 2048.0
BIG = 1e30
LN_EPS = 1e-5
SLOPE = 0.2
GB = 5
NG = NB // GB
CENTER = 1562


TAKEN = []


class Core:
    pass


def sb_of(nc, ctx):
    return lambda name, shape, dt: ctx.enter_context(nc.sbuf_tensor(name, shape, dt))


def sem_of(nc, ctx):
    def sem(name):
        TAKEN.append(nc.alloc_semaphore(name))
        return TAKEN[-1]
    return sem


def recycle(nc):
    nc.clear_and_free_semaphores(TAKEN)
    TAKEN.clear()
    nc.all_engine_barrier()


def row_bcast(vec, parts, n):
    return bass.AP(vec.tensor, vec.offset, [[0, parts], [1, n]])


def stage_windows(nc, k, dst):
    with ExitStack() as ctx:
        sb, sem = sb_of(nc, ctx), sem_of(nc, ctx)
        H = NPAIR // 2
        pairs_i = sb("pairs_i", [H, 2, 2 * P], I32)
        pairs = sb("pairs", [H, 2, 2 * P], F32)
        ext = sb("ext", [H, 4], F32)
        diag = sb("diag", [H, 4, H], F32)
        ones = sb("ones_w", [H, NB], F32)
        blk_lo = sb("blk_lo", [NB, 1], F32)
        blk_hi = sb("blk_hi", [NB, 1], F32)
        pair_id = sb("pair_id", [NB, 2, H], F32)
        meets = sb("meets", [NB, 2, H], F32)
        cand = sb("cand", [NB, 2, 2, H], F32)
        lohi = sb("lohi", [NB, 2], F32)
        lohi_i = sb("lohi_i", [NB, 2], I32)
        s_in, s_tab, s_diag, s_row, s_win, s_out = (sem(x) for x in (
            "w_in", "w_tables", "w_diag", "w_rows", "w_windows", "w_out"))
        rows = k.ps[0:NB, 0, 0:4 * H].rearrange("p (s h) -> p s h", s=4)
        with nc.Block() as block:
            @block.sync
            def _(sp):
                sp.dma_start(pairs_i[:], dst.rearrange("(p a e) -> p a e", a=2, e=2 * P)).then_inc(s_in, 16)
                sp.wait_ge(s_win, 1)
                sp.dma_start(k.windows_dram, lohi_i[:]).then_inc(s_out, 16)
                sp.wait_ge(s_out, 16)
                sp.dma_start(k.windows[:], k.windows_dram.rearrange("b s -> (b s)")[None, :]).then_inc(s_out, 16)
                sp.wait_ge(s_out, 32)

            @block.gpsimd
            def _(pool):
                pool.memset(k.src_iota[:], 9999.0)
                pool.drain()
                pool.iota(k.src_iota[:, :, 0:P], pattern=[[P, NB], [1, P]], base=-CENTER, channel_multiplier=0,
                          allow_small_or_imprecise_dtypes=True)
                pool.iota(k.dst_iota[:], pattern=[[1, P]], base=0, channel_multiplier=0,
                          allow_small_or_imprecise_dtypes=True)
                pool.iota(blk_lo[:], pattern=[[0, 1]], base=0, channel_multiplier=P,
                          allow_small_or_imprecise_dtypes=True)
                pool.iota(blk_hi[:], pattern=[[0, 1]], base=P, channel_multiplier=P,
                          allow_small_or_imprecise_dtypes=True)
                pool.iota(pair_id[:], pattern=[[1, 2], [2, H]], base=1, channel_multiplier=0,
                          allow_small_or_imprecise_dtypes=True)
                pool.memset(k.ident[:], 0.0)
                pool.drain()
                pool.affine_select(out=k.ident[:], in_=k.ident[:], compare_op=ALU.not_equal, fill=1.0, base=0,
                                   pattern=[[-1, 128]], channel_multiplier=1)
                pool.drain().then_inc(s_tab, 1)

            @block.vector
            def _(dve):
                dve.memset(ones[:], 1.0)
                dve.wait_ge(s_in, 16)
                dve.tensor_copy(pairs[:], pairs_i[:])
                dve.drain()
                dve.tensor_reduce(ext[:, 0:2], pairs[:], AX.X, ALU.min)
                dve.tensor_reduce(ext[:, 2:4], pairs[:], AX.X, ALU.max)
                dve.wait_ge(s_tab, 1)
                dve.tensor_copy(k.ident16[:], k.ident[0:P, 0:P])
                dve.drain()
                for s in range(4):
                    dve.tensor_scalar(diag[:, s, :], k.ident[0:H, 0:H], ext[:, s:s + 1], None, ALU.mult)
                dve.drain().then_inc(s_diag, 1)
                dve.wait_ge(s_row, 1)
                dve.tensor_scalar(meets[:], rows[:, 2:4, :], blk_lo[:, 0:1], None, ALU.is_ge)
                dve.drain()
                dve.scalar_tensor_tensor(meets[:], rows[:, 0:2, :], blk_hi[:, 0:1], meets[:], ALU.is_lt, ALU.mult)
                dve.drain()
                dve.scalar_tensor_tensor(cand[:, 0], pair_id[:], float(NPAIR + 1), meets[:], ALU.subtract, ALU.mult)
                dve.tensor_tensor(cand[:, 1], pair_id[:], meets[:], ALU.mult)
                dve.drain()
                dve.tensor_reduce(lohi[:, 0:1], cand[:, 0], AX.XY, ALU.min)
                dve.tensor_reduce(lohi[:, 1:2], cand[:, 1], AX.XY, ALU.max)
                dve.drain()
                dve.tensor_scalar(lohi[:, 0:1], lohi[:, 0:1], float(NPAIR), float(NPAIR - 1), ALU.add, ALU.min)
                dve.drain()
                dve.scalar_tensor_tensor(lohi[:, 1:2], lohi[:, 0:1], 1.0, lohi[:, 1:2], ALU.add, ALU.max)
                dve.drain()
                dve.tensor_copy(lohi_i[:], lohi[:])
                dve.drain().then_inc(s_win, 1)

            @block.tensor
            def _(pe):
                pe.wait_ge(s_diag, 1)
                for s in range(4):
                    mm = pe.matmul(rows[:, s, :], ones[:, :], diag[:, s, :], start=(s == 0), stop=True,
                                   skip_group_check=True)
                mm.then_inc(s_row, 1)


def stage_edges(nc, k, srcT, dstT, eaT, ee_w1, ee_b1):
    with ExitStack() as ctx:
        sb, sem = sb_of(nc, ctx), sem_of(nc, ctx)
        ids_i = sb("ids_i", [P, 2, 2 * NPAIR], I32)
        src_f = sb("src_f", [P, 2 * NPAIR], F32)
        dst_f = sb("dst_f", [P, 2 * NPAIR], F32)
        dst_blk = sb("dst_blk", [P, P], F32)
        src_hot = sb("src_hot", [P, 2, NB, PAD], F16)
        dst_hot = sb("dst_hot", [P, 2, P], F16)
        dst_hot32 = sb("dst_hot32", [P, 2, P], F32)
        ea = sb("ea", [EDIM + 1, 2, P], F32)
        w_edge = sb("w_edge", [EDIM + 1, D], F32)
        relu = sb("relu_e", [P, 2, D + 1], F32)
        zero = sb("zero_e", [P, 512], F16)
        a_out = sb("a_out", [128, N], F16)
        m_out = sb("m_out", [128, N], BF16)
        e_out = sb("e_out", [P, D + 1], F32)
        s_ids, s_w, s_set, s_store = sem("e_ids"), sem("e_w"), sem("e_set"), sem("e_store")
        s_ea = [sem("e_ea0"), sem("e_ea1")]
        s_mlp, s_relu, s_acc = sem("e_mlp"), sem("e_relu"), sem("e_acc")
        s_hot, s_evac, s_free, s_masks = sem("e_hot"), sem("e_evac"), sem("e_free"), sem("e_masks")
        mlp = k.ps[0:P, 7, :].rearrange("p (i f) -> p i f", i=2)
        esum = k.ps[0:P, 6, 128:128 + D + 1]

        def chunk(c):
            return k.ps[:, c // 4, (c % 4) * P:(c % 4 + 1) * P]

        def window(eng, b):
            lo = eng.value_load(k.windows[0:1, bass.ds(b * 2, 1)], min_val=0, max_val=NPAIR - 1)
            hi = eng.value_load(k.windows[0:1, bass.ds(b * 2 + 1, 1)], min_val=1, max_val=NPAIR)
            return lo, hi

        with nc.Block() as block:
            @block.sync
            def _(sp):
                sp.dma_start(ids_i[:, 0], srcT).then_inc(s_ids, 16)
                sp.dma_start(ids_i[:, 1], dstT).then_inc(s_ids, 16)
                sp.dma_start(w_edge[0:EDIM], ee_w1).then_inc(s_w, 16)
                sp.dma_start(w_edge[EDIM:EDIM + 1], ee_b1[None, :]).then_inc(s_w, 16)
                done = sp.alloc_register("sp_pairs")
                sp.reg_mov(done, 0)
                with sp.Fori(0, NB) as b:
                    lo, hi = window(sp, b)
                    with sp.Fori(lo, hi) as j:
                        t = sp.snap(done)
                        for i in range(2):
                            sp.wait_ge(s_mlp, t * 2 + (i + 1))
                            sp.dma_start(ea[0:EDIM, i, :], eaT[:, bass.ds((j * 2 + i) * P, P)]).then_inc(s_ea[i], 16)
                        sp.reg_add(done, done, 1)

            @block.gpsimd
            def _(pool):
                with pool.Fori(0, NB) as b:
                    pool.wait_ge(s_masks, b + 1)
                    pool.dma_start(k.a_dram[bass.ds(b, 1)].rearrange("a p n -> (a p) n"), a_out[:]).then_inc(s_store, 16)
                    pool.dma_start(k.m_dram[bass.ds(b, 1)].rearrange("a p n -> (a p) n"), m_out[:]).then_inc(s_store, 16)
                    pool.dma_start(k.e_dram[bass.ds(b, 1)].rearrange("a p n -> (a p) n"), e_out[:]).then_inc(s_store, 16)
                    pool.wait_ge(s_store, b * 48 + 48)
                    pool.sem_inc(s_free, 1)

            @block.vector
            def _(dve):
                dve.memset(zero[:], 0.0)
                dve.memset(relu[:, :, D:D + 1], 1.0)
                dve.memset(ea[EDIM:EDIM + 1], 1.0)
                dve.tensor_copy(dst_blk[:], k.dst_iota[0:P])
                dve.wait_ge(s_ids, 32)
                dve.tensor_scalar(src_f[:], ids_i[:, 0], float(-CENTER), None, ALU.add)
                dve.tensor_copy(dst_f[:], ids_i[:, 1])
                dve.drain().then_inc(s_set, 1)
                dve.sem_inc(s_free, 1)
                done = dve.alloc_register("dve_pairs")
                dve.reg_mov(done, 0)
                with dve.Fori(0, NB) as b:
                    lo, hi = window(dve, b)
                    with dve.Fori(lo, hi) as j:
                        t = dve.snap(done)
                        for i in range(2):
                            dve.wait_ge(s_acc, t * 2 + (i + 1))
                            dve.tensor_scalar(dst_hot[:, i, :], dst_blk[:], dst_f[:, bass.ds(j * 2 + i, 1)], None, ALU.is_equal)
                            dve.tensor_scalar(dst_hot32[:, i, :], dst_blk[:], dst_f[:, bass.ds(j * 2 + i, 1)], None, ALU.is_equal)
                            dve.tensor_scalar(src_hot[:, i], k.src_iota[0:P], src_f[:, bass.ds(j * 2 + i, 1)], None,
                                              ALU.is_equal).then_inc(s_hot, 1)
                        dve.reg_add(done, done, 1)
                    dve.tensor_scalar(dst_blk[:], dst_blk[:], float(P), None, ALU.add)
                    dve.wait_ge(s_free, b + 1)
                    t = dve.snap(done)
                    dve.wait_ge(s_acc, t * 2 + 2)
                    dve.tensor_copy(a_out[:, 16 * P:24 * P].rearrange("p (k n) -> p k n", k=2), k.ps[:, 4:6, 0:4 * P])
                    dve.tensor_copy(a_out[:, 24 * P:], chunk(24))
                    dve.tensor_copy(k.deg[:, bass.ds(b, 1)], esum[:, D:D + 1])
                    dve.tensor_copy(e_out[:], esum)
                    dve.drain().then_inc(s_evac, 1)
                    dve.wait_ge(s_evac, b * 2 + 4)
                    dve.tensor_scalar(m_out[:], a_out[:], 0.0, -BIG, ALU.is_equal, ALU.mult).then_inc(s_masks, 1)

            @block.scalar
            def _(act):
                act.preload_act_table(ACT.Relu)
                act.wait_ge(s_set, 1)
                act.sem_inc(s_relu, 1)
                done = act.alloc_register("act_pairs")
                act.reg_mov(done, 0)
                with act.Fori(0, NB) as b:
                    lo, hi = window(act, b)
                    with act.Fori(lo, hi) as j:
                        t = act.snap(done)
                        act.wait_ge(s_acc, t * 2 + 2)
                        act.wait_ge(s_mlp, t * 2 + 4)
                        act.activation(relu[:, :, 0:D], mlp[:], ACT.Relu).then_inc(s_relu, 1)
                        act.reg_add(done, done, 1)
                    act.wait_ge(s_free, b + 1)
                    t = act.snap(done)
                    act.wait_ge(s_acc, t * 2 + 2)
                    act.copy(a_out[:, 0:16 * P].rearrange("p (k n) -> p k n", k=4), k.ps[:, 0:4, 0:4 * P])
                    act.drain().then_inc(s_evac, 1)

            @block.tensor
            def _(pe):
                pe.sem_inc(s_mlp, 2)
                pe.sem_inc(s_acc, 2)
                pe.sem_inc(s_evac, 2)
                pe.wait_ge(s_set, 1)
                pe.wait_ge(s_w, 32)
                done = pe.alloc_register("pe_pairs")
                pe.reg_mov(done, 0)
                with pe.Fori(0, NB) as b:
                    lo, hi = window(pe, b)
                    pe.wait_ge(s_evac, b * 2 + 2)
                    for bank in range(7):
                        pe.matmul(k.ps[:, bank, :], zero[:, 0:128], zero[:], start=True, stop=True,
                                  skip_group_check=True)
                    with pe.Fori(lo, hi) as j:
                        t = pe.snap(done)
                        pe.wait_ge(s_relu, t + 1)
                        for i in range(2):
                            pe.wait_ge(s_ea[i], t * 16 + 16)
                            pe.matmul(mlp[:, i], ea[:, i, :], w_edge[:], start=True, stop=True,
                                      skip_group_check=True).then_inc(s_mlp, 1)
                        for i in range(2):
                            pe.wait_ge(s_hot, t * 2 + (i + 1))
                            for c in range(NB):
                                pe.matmul(chunk(c), src_hot[:, i, c, :], dst_hot[:, i, :], start=False, stop=False,
                                          skip_group_check=True)
                            if i == 0:
                                pe.wait_ge(s_relu, t + 2)
                            pe.matmul(esum, dst_hot32[:, i, :], relu[:, i, :], start=False, stop=False,
                                      skip_group_check=True).then_inc(s_acc, 1)
                        pe.reg_add(done, done, 1)



def in_steps(eng, step, tail):
    for i in range(GB):
        step(i, i)
    with eng.Fori(1, NG) as it:
        for i in range(GB):
            step(it * GB + i, i)
    for i in range(tail):
        step(NB + i, i)


def at(s, lag, first=0):
    return not isinstance(s, int) or first <= s - lag < NB


def slot(s, lag, i):
    return (i - lag) % GB


BANK3 = (0, 1, 0, 1, 2)


def split(dve, hi, lo, x2048):
    dve.tensor_scalar(hi, x2048, 1.0 / LO, None, ALU.mult)
    dve.drain()
    return dve.scalar_tensor_tensor(lo, hi, -LO, x2048, ALU.mult, ALU.add)


def stage_first_split(nc, k, x, parts):
    with ExitStack() as ctx:
        sb, sem = sb_of(nc, ctx), sem_of(nc, ctx)
        g = sb("first_g", [P, 2, D], F32)
        s_x, s_deg, s_root = sem("f_x"), sem("f_deg"), sem("f_root")
        with nc.Block() as block:
            @block.sync
            def _(sp):
                sp.dma_start(k.xs[:], x.rearrange("(b p) d -> p b d", p=P)).then_inc(s_x, 16)

            @block.scalar
            def _(act):
                act.wait_ge(s_deg, 1)
                act.activation(k.dinv[:], k.deg1[:], ACT.Sqrt).then_inc(s_root, 1)

            @block.vector
            def _(dve):
                dve.tensor_scalar(k.deg1[:], k.deg[:], 1.0, None, ALU.add).then_inc(s_deg, 1)
                dve.wait_ge(s_root, 1)
                dve.reciprocal(k.dinv[:], k.dinv[:])
                dve.drain()
                dve.tensor_scalar(k.dinv_lo[:], k.dinv[:], LO, None, ALU.mult)
                dve.wait_ge(s_x, 16)
                dve.drain()
                with dve.Fori(0, NB) as b:
                    dve.tensor_scalar(g[:, 0, :], k.xs[:, bass.ds(b, 1), :].rearrange("p a d -> p (a d)"),
                                      k.dinv_lo[:, bass.ds(b, 1)], None, ALU.mult)
                    dve.drain()
                    out = parts[:, bass.ds(b, 1), :].rearrange("p a d -> p (a d)")
                    split(dve, out[:, 0:D], out[:, D:2 * D], g[:, 0, :])
                    dve.drain()


def blk(t, b):
    if isinstance(b, int):
        return t[:, b, :]
    return t[:, bass.ds(b, 1), :].rearrange("p a n -> p (a n)")


def col(t, b):
    return t[:, b:b + 1] if isinstance(b, int) else t[:, bass.ds(b, 1)]


def stage_aggregate(nc, k, name, parts, finish, w, bias, out_parts=None, rb1=None, eps=None):
    gin = finish == "gin"
    with ExitStack() as ctx:
        sb0, sem0 = sb_of(nc, ctx), sem_of(nc, ctx)
        sb = lambda n, s, d: sb0(f"{name}_{n}", s, d)
        sem = lambda n: sem0(f"{name}_{n}")
        a_ring = sb("a_ring", [128, GB, N], F16)
        wt = sb("w", [128, 2, D], F32)
        brow = sb("bias", [P, D], F32)
        z_lo = sb("z_lo", [P, GB, D], F32)
        z = sb("z", [P, GB, D], F32)
        zt = sb("zt", [128, GB, 2, P], F32)
        t = sb("t", [P, D], F32)
        g = sb("g", [P, D], F32)
        s_a = [sem(f"a{i}") for i in range(GB)]
        s_w, s_agg, s_zlo, s_z, s_tr, s_zt, s_y, s_post = (sem(x) for x in (
            "w", "agg", "zlo", "z", "tr", "zt", "y", "post"))
        ps_t = k.ps[:, 6, 0:2 * P].rearrange("p (h n) -> p h n", h=2)
        ps_y = k.ps[0:P, 7, 0:D]
        nw = 2
        if gin:
            e_in = sb("e_in", [P, GB, D + 1], F32)
            er = sb("er", [P, GB, D], F32)
            rb1row = sb("rb1", [P, D], F32)
            eps1 = sb("eps1", [P, 1], F32)
            s_e = [sem(f"e{i}") for i in range(GB)]
            s_er = sem("er")
            nw = 4
        with nc.Block() as block:
            @block.sync
            def _(sp):
                sp.dma_start(wt[:], w.rearrange("(h p) n -> p h n", h=2)).then_inc(s_w, 16)
                sp.dma_start(brow[:], row_bcast(bias, P, D)).then_inc(s_w, 16)
                if gin:
                    sp.dma_start(rb1row[:], row_bcast(rb1, P, D)).then_inc(s_w, 16)
                    sp.dma_start(eps1[:], row_bcast(eps, P, 1)).then_inc(s_w, 16)
                for i in range(GB):
                    sp.dma_start(a_ring[:, i, :], k.a_dram[i]).then_inc(s_a[i], 16)
                    if gin:
                        sp.dma_start(e_in[:, i, :], k.e_dram[i]).then_inc(s_e[i], 16)
                with sp.Fori(1, NG) as it:
                    for i in range(GB):
                        b = it * GB + i
                        sp.wait_ge(s_agg, it * GB + (i - GB + 1))
                        sp.dma_start(a_ring[:, i, :], k.a_dram[bass.ds(b, 1)].rearrange("a p n -> (a p) n")).then_inc(s_a[i], 16)
                        if gin:
                            sp.wait_ge(s_er, it * GB + (i - GB + 1))
                            sp.dma_start(e_in[:, i, :], k.e_dram[bass.ds(b, 1)].rearrange("a p n -> (a p) n")).then_inc(s_e[i], 16)

            @block.tensor
            def _(pe):
                pe.wait_ge(s_w, 16 * nw)

                def step(s, i, it=None):
                    if at(s, 0):
                        pe.wait_ge(s_a[i], 16 if it is None else it * 16 + 16)
                        bank = BANK3[i]
                        for c in range(NB):
                            pe.matmul(k.ps[0:P, bank, :], a_ring[0:P, i, c * P:(c + 1) * P], parts[:, c, :],
                                      start=(c == 0), stop=False)
                        pe.matmul(k.ps[0:P, bank, :], k.ident16[:], blk(parts, s), start=False,
                                  stop=True).then_inc(s_agg, 1)
                    if at(s, 1):
                        j = slot(s, 1, i)
                        pe.wait_ge(s_z, s)
                        if not isinstance(s, int) or s >= 2:
                            pe.wait_ge(s_zt, s - 1)
                        src = er if gin else z
                        for h in range(2):
                            tr = pe.transpose(ps_t[:, h, :], src[:, j, h * 128:(h + 1) * 128], k.ident[0:P, 0:P])
                        tr.then_inc(s_tr, 1)
                    if at(s, 2):
                        j = slot(s, 2, i)
                        pe.wait_ge(s_zt, s - 1)
                        if not isinstance(s, int) or s >= 3:
                            pe.wait_ge(s_post, s - 2)
                        for h in range(2):
                            mm = pe.matmul(ps_y, zt[:, j, h, :], wt[:, h, :], start=(h == 0), stop=(h == 1))
                        mm.then_inc(s_y, 1)

                for i in range(GB):
                    step(i, i)
                with pe.Fori(1, NG) as it:
                    for i in range(GB):
                        step(it * GB + i, i, it)
                for i in range(2):
                    step(NB + i, i)

            @block.scalar
            def _(act):
                def step(s, i):
                    if at(s, 0):
                        act.wait_ge(s_agg, s + 1)
                        act.mul(z_lo[:, i, :], k.ps[0:P, BANK3[i], D:2 * D], 1.0 / LO).then_inc(s_zlo, 1)
                    if at(s, 1):
                        act.wait_ge(s_tr, s)
                        if not isinstance(s, int) or s >= GB + 1:
                            act.wait_ge(s_y, s - GB)
                        act.copy(zt[:, slot(s, 1, i)], ps_t).then_inc(s_zt, 1)

                in_steps(act, step, 1)

            @block.vector
            def _(dve):
                dve.wait_ge(s_w, 16 * nw)
                if gin:
                    dve.tensor_scalar(rb1row[:], rb1row[:], 0.0, None, ALU.max)
                    dve.tensor_scalar(eps1[:], eps1[:], 1.0, None, ALU.add)
                    dve.drain()

                def step(s, i, it=None):
                    if at(s, 0):
                        if gin:
                            dve.wait_ge(s_e[i], 16 if it is None else it * 16 + 16)
                            dve.tensor_tensor(er[:, i, :], e_in[:, i, 0:D], rb1row[:], ALU.add).then_inc(s_er, 1)
                        dve.wait_ge(s_zlo, s + 1)
                        dve.tensor_tensor(z[:, i, :], k.ps[0:P, BANK3[i], 0:D], z_lo[:, i, :],
                                          ALU.add).then_inc(s_z, 1)
                    if at(s, 2):
                        b = s - 2
                        dve.wait_ge(s_y, s - 1)
                        if gin:
                            dve.scalar_tensor_tensor(t[:], blk(k.xs, b), eps1[:, 0:1], z[:, slot(s, 2, i), :],
                                                     ALU.mult, ALU.add)
                            dve.scalar_tensor_tensor(g[:], brow[:], col(k.deg1, b), ps_y, ALU.mult,
                                                     ALU.add).then_inc(s_post, 1)
                            dve.drain()
                            dve.tensor_tensor(blk(k.y, b), t[:], g[:], ALU.add)
                            dve.drain()
                            return
                        dve.scalar_tensor_tensor(t[:], ps_y, col(k.dinv, b), brow[:], ALU.mult,
                                                 ALU.add).then_inc(s_post, 1)
                        dve.drain()
                        if finish == "gcn":
                            dve.tensor_scalar(g[:], t[:], 0.0, col(k.dinv_lo, b), ALU.max, ALU.mult)
                            dve.drain()
                            out = blk(out_parts, b)
                            split(dve, out[:, 0:D], out[:, D:2 * D], g[:])
                        else:
                            dve.tensor_tensor(blk(k.xs, b), t[:], blk(k.xs, b), ALU.add)
                            dve.drain()
                            dve.bn_stats(blk(k.stats, b), blk(k.xs, b))
                        dve.drain()

                for i in range(GB):
                    step(i, i)
                with dve.Fori(1, NG) as it:
                    for i in range(GB):
                        step(it * GB + i, i, it)
                for i in range(2):
                    step(NB + i, i)


def stage_project(nc, k, name, source, norm, w=None, bias=None, wq=None, wk=None, bq=None, bk=None, parts=None):
    project = w is not None
    with ExitStack() as ctx:
        sb0, sem0 = sb_of(nc, ctx), sem_of(nc, ctx)
        sb = lambda n, s, d: sb0(f"{name}_{n}", s, d)
        sem = lambda n: sem0(f"{name}_{n}")
        wt = sb("w", [128, 2, D], F32)
        brow = sb("bias", [P, D], F32)
        wqk = sb("wqk", [P, 2, D], F32)
        bqk = sb("bqk", [P, 2], F32)
        xin = sb("xin", [P, GB, D], F32)
        xt = sb("xt", [128, GB, 2, P], F32)
        prod = sb("prod", [P, 2, D], F32)
        g = sb("g", [P, D], F32)
        s_w, s_x, s_tr, s_xt, s_y, s_h, s_var, s_root = (sem(x) for x in (
            "w", "x", "tr", "xt", "y", "h", "var", "root"))
        ps_t = [k.ps[:, m, 0:2 * P].rearrange("p (h n) -> p h n", h=2) for m in range(3)]
        ps_y = [k.ps[0:P, 3 + m, 0:D] for m in range(3)]
        loads = 0
        if project:
            loads = 3 + (bias is not None) + 2 * (bq is not None)
        with nc.Block() as block:
            @block.sync
            def _(sp):
                if project:
                    sp.dma_start(wt[:], w.rearrange("(h p) n -> p h n", h=2)).then_inc(s_w, 16)
                    sp.dma_start(wqk[:, 0, :], row_bcast(wq, P, D)).then_inc(s_w, 16)
                    sp.dma_start(wqk[:, 1, :], row_bcast(wk, P, D)).then_inc(s_w, 16)
                    if bias is not None:
                        sp.dma_start(brow[:], row_bcast(bias, P, D)).then_inc(s_w, 16)
                    if bq is not None:
                        sp.dma_start(bqk[:, 0:1], row_bcast(bq, P, 1)).then_inc(s_w, 16)
                        sp.dma_start(bqk[:, 1:2], row_bcast(bk, P, 1)).then_inc(s_w, 16)

            @block.scalar
            def _(act):
                if norm:
                    act.wait_ge(s_var, 1)
                    act.activation(k.rstd[:], k.rstd[:], ACT.Sqrt).then_inc(s_root, 1)
                if not project:
                    return

                def step(s, i):
                    act.wait_ge(s_tr, s + 1)
                    act.copy(xt[:, i], ps_t[BANK3[i]]).then_inc(s_xt, 1)

                in_steps(act, step, 0)

            @block.tensor
            def _(pe):
                if not project:
                    return
                pe.wait_ge(s_w, 16 * loads)

                def step(s, i):
                    if at(s, 0):
                        pe.wait_ge(s_x, s + 1)
                        for h in range(2):
                            tr = pe.transpose(ps_t[BANK3[i]][:, h, :], xin[:, i, h * 128:(h + 1) * 128],
                                              k.ident[0:P, 0:P])
                        tr.then_inc(s_tr, 1)
                    if at(s, 1):
                        j = slot(s, 1, i)
                        pe.wait_ge(s_xt, s)
                        if not isinstance(s, int) or s >= 3:
                            pe.wait_ge(s_h, s - 2)
                        for h in range(2):
                            mm = pe.matmul(ps_y[BANK3[j]], xt[:, j, h, :], wt[:, h, :], start=(h == 0), stop=(h == 1))
                        mm.then_inc(s_y, 1)

                in_steps(pe, step, 1)

            @block.vector
            def _(dve):
                if norm:
                    for b in range(NB):
                        dve.bn_aggr(k.mv[:, b, :], k.stats[:, b, :])
                    dve.drain()
                    dve.tensor_scalar(k.rstd[:], k.mv[:, :, 1], LN_EPS, None, ALU.add).then_inc(s_var, 1)
                    dve.tensor_copy(k.mean[:], k.mv[:, :, 0])
                    dve.wait_ge(s_root, 1)
                    dve.reciprocal(k.rstd[:], k.rstd[:])
                    dve.drain()
                if project:
                    dve.memset(k.h[:, :, D:D + 1], 1.0)
                    dve.wait_ge(s_w, 16 * loads)

                def step(s, i):
                    if at(s, 0):
                        if norm:
                            dve.tensor_scalar(blk(k.xs, s), blk(k.xs, s), col(k.mean, s), col(k.rstd, s),
                                              ALU.subtract, ALU.mult)
                            dve.drain()
                        if project:
                            if not isinstance(s, int) or s >= GB:
                                dve.wait_ge(s_tr, s - GB + 1)
                            dve.tensor_scalar(xin[:, i, :], blk(source, s), 1.0, None, ALU.mult).then_inc(s_x, 1)
                        if parts is not None:
                            dve.tensor_scalar(g[:], blk(k.xs, s), LO, None, ALU.mult)
                            dve.drain()
                            out = blk(parts, s)
                            split(dve, out[:, 0:D], out[:, D:2 * D], g[:])
                            dve.drain()
                    if project and at(s, 2):
                        b = s - 2
                        j = slot(s, 2, i)
                        dve.wait_ge(s_y, s - 1)
                        h = blk(k.h, b)[:, 0:D]
                        if bias is None:
                            dve.tensor_scalar(h, ps_y[BANK3[j]], 1.0, None, ALU.mult).then_inc(s_h, 1)
                        else:
                            dve.tensor_tensor(h, ps_y[BANK3[j]], brow[:], ALU.add).then_inc(s_h, 1)
                        dve.drain()
                        for v in range(2):
                            dve.tensor_tensor(prod[:, v, :], h, wqk[:, v, :], ALU.mult)
                        dve.drain()
                        dve.tensor_reduce(col(k.q, b), prod[:, 0, :], AX.X, ALU.add)
                        dve.tensor_reduce(col(k.kk, b), prod[:, 1, :], AX.X, ALU.add)
                        dve.drain()

                in_steps(dve, step, 2 if project else 0)
                if bq is not None:
                    dve.tensor_scalar(k.q[:], k.q[:], bqk[:, 0:1], None, ALU.add)
                    dve.tensor_scalar(k.kk[:], k.kk[:], bqk[:, 1:2], None, ALU.add)
                    dve.drain()
                if project:
                    dve.tensor_scalar(k.q_slope[:], k.q[:], SLOPE, None, ALU.mult)


def stage_attention(nc, k, name, finish, bias=None):
    GW = GB * P
    AHEAD = 20
    E_SLOTS, P_SLOTS = 2, 3
    with ExitStack() as ctx:
        sb0, sem0 = sb_of(nc, ctx), sem_of(nc, ctx)
        sb = lambda n, s, d: sb0(f"{name}_{n}", s, d)
        sem = lambda n: sem0(f"{name}_{n}")
        counts = sb("counts", [128, NG, GB, GB * P], F16)
        masks = sb("masks", [128, NG, GB, GB * P], BF16)
        brow = sb("bias", [P, D], F32)
        qmax = sb("qmax", [P, GB, P], F32)
        top = sb("top", [P, GB], F32)
        tops = sb("tops", [P, GB], F32)
        rcol = sb("rcol", [P, 2, GB], F32)
        kslope = sb("kslope", [P, NB], F32)
        diag = sb("diag", [P, 2, GB, P], F32)
        ones = sb("ones", [P, P], F32)
        rrow = sb("rrow", [P, 2, GB, P], F32)
        e = sb("e", [P, E_SLOTS + 1, 2, GW], F32)
        x = sb("x", [P, GB, P], F32)
        p = sb("p", [P, P_SLOTS + 1, GB, P], F32)
        den = sb("den", [P, GB], F32)
        t = sb("t", [P, GB, D], F32)
        s_cnt = [sem(f"cnt{n}") for n in range(NG)]
        s_mask = [sem(f"mask{n}") for n in range(NG)]
        s_w, s_max, s_qmax, s_tr, s_diag, s_bc, s_r, s_e, s_x, s_p, s_pv, s_out, s_set = (sem(v) for v in (
            "w", "max", "qmax", "tr", "diag", "bc", "r", "e", "x", "p", "pv", "out", "set"))

        def spread(r):
            return (k.ps[0:P, 5 + 2 * r, 0:4 * P].rearrange("p (j n) -> p j n", j=4),
                    k.ps[0:P, 6, r * P:(r + 1) * P])

        def piece(dram, g, n):
            src = dram[g * GB:(g + 1) * GB] if isinstance(g, int) else dram[bass.ds(g * GB, GB)]
            return src.rearrange("b p n -> p b n")[:, :, n * GB * P:(n + 1) * GB * P]

        def chunk(tile, c):
            return tile[0:P, c // GB, :, (c % GB) * P:(c % GB + 1) * P]

        def e_slot(c):
            return c % E_SLOTS if c < NB - 1 else E_SLOTS

        def p_slot(c):
            return c % P_SLOTS if c < NB - 1 else P_SLOTS

        def maxima(c):
            return range(NB * c // AHEAD, NB * (c + 1) // AHEAD) if c < AHEAD else ()

        def groups(eng, body):
            body(0, True, False)
            with eng.Fori(1, NG - 1) as g:
                body(g, False, False)
            body(NG - 1, False, True)

        with nc.Block() as block:
            @block.sync
            def _(sp):
                if bias is not None:
                    sp.dma_start(brow[:], row_bcast(bias, P, D)).then_inc(s_w, 16)
                for n in range(NG):
                    sp.dma_start(masks[:, n], piece(k.m_dram, 0, n)).then_inc(s_mask[n], 16)
                for n in range(NG):
                    sp.dma_start(counts[:, n], piece(k.a_dram, 0, n)).then_inc(s_cnt[n], 16)
                for n in range(NG):
                    sp.wait_ge(s_max, GB * (n + 1))
                    sp.dma_start(masks[:, n], piece(k.m_dram, 1, n)).then_inc(s_mask[n], 16)

                def body(g, last_mask):
                    for n in range(NG):
                        if not last_mask:
                            sp.wait_ge(s_max, g * NB + (NB + GB * (n + 1)))
                            sp.dma_start(masks[:, n], piece(k.m_dram, g + 2, n)).then_inc(s_mask[n], 16)
                        sp.wait_ge(s_p, g * NB + GB * (n + 1))
                        sp.dma_start(counts[:, n], piece(k.a_dram, g + 1, n)).then_inc(s_cnt[n], 16)

                with sp.Fori(0, NG - 2) as g:
                    body(g, False)
                body(NG - 2, True)

            @block.scalar
            def _(act):
                act.preload_act_table(ACT.Exp)

                def body(g, first, last):
                    act.wait_ge(s_bc, g + 1)
                    if not first:
                        act.wait_ge(s_e, g * NB)
                    for r in range(2):
                        many, one = spread(r)
                        act.copy(rrow[:, r, 0:4, :], many)
                        act.copy(rrow[:, r, 4, :], one)
                    act.drain().then_inc(s_r, 1)
                    for c in range(NB):
                        if not (first and c < E_SLOTS):
                            act.wait_ge(s_x, g * NB + (c - E_SLOTS + 1))
                        m = e_slot(c)
                        act.activation(e[:, m, 0, :], rrow[:, 0].rearrange("p j n -> p (j n)"), ACT.Exp,
                                       bias=k.q[:, c:c + 1])
                        act.activation(e[:, m, 1, :], rrow[:, 1].rearrange("p j n -> p (j n)"), ACT.Exp,
                                       bias=k.q_slope[:, c:c + 1]).then_inc(s_e, 1)

                groups(act, body)

            @block.vector
            def _(dve):
                dve.memset(ones[:], 1.0)
                dve.tensor_scalar(kslope[:], k.kk[:], SLOPE, None, ALU.mult)
                if bias is not None:
                    dve.wait_ge(s_w, 16)
                dve.drain().then_inc(s_set, 1)

                def greatest(g, c):
                    if c % GB == 0:
                        dve.wait_ge(s_mask[c // GB], g * 16 + 16)
                    if c == 0:
                        dve.tensor_scalar(qmax[:], chunk(masks, c), k.q[:, c:c + 1], None, ALU.add).then_inc(s_max, 1)
                    else:
                        dve.wait_ge(s_max, g * NB + c)
                        dve.scalar_tensor_tensor(qmax[:], chunk(masks, c), k.q[:, c:c + 1], qmax[:], ALU.add,
                                                 ALU.max).then_inc(s_max, 1)

                def of_group(tile, g):
                    return tile[:, g * GB:(g + 1) * GB] if isinstance(g, int) else tile[:, bass.ds(g * GB, GB)]

                def limits(g):
                    dve.wait_ge(s_tr, g + 1)
                    many, one = spread(0)
                    dve.tensor_reduce(top[:, 0:4], many, AX.X, ALU.max)
                    dve.tensor_reduce(top[:, 4:5], one, AX.X, ALU.max)
                    dve.drain()
                    dve.tensor_tensor(top[:], top[:], of_group(k.kk, g), ALU.add)
                    dve.drain()
                    dve.tensor_scalar(tops[:], top[:], SLOPE, None, ALU.mult)
                    dve.drain()
                    dve.tensor_tensor(top[:], top[:], tops[:], ALU.max)
                    dve.drain()
                    dve.tensor_tensor(rcol[:, 0, :], of_group(k.kk, g), top[:], ALU.subtract)
                    dve.tensor_tensor(rcol[:, 1, :], of_group(kslope, g), top[:], ALU.subtract)
                    dve.drain()
                    for r in range(2):
                        dve.tensor_tensor(diag[:, r], k.ident[0:P, 0:P].unsqueeze(1).to_broadcast([P, GB, P]),
                                          rcol[:, r, :].unsqueeze(2).to_broadcast([P, GB, P]), ALU.mult)
                    dve.drain().then_inc(s_diag, 1)

                def take(g):
                    dve.wait_ge(s_pv, g * NB + NB)
                    dve.tensor_scalar(den[:], k.ps[0:P, 0:GB, D], 1e-30, None, ALU.max)
                    dve.drain()
                    dve.reciprocal(den[:], den[:])
                    dve.drain()
                    for j in range(GB):
                        other = blk(k.xs, g * GB + j) if finish == "res" else brow[:]
                        dve.scalar_tensor_tensor(t[:, j, :], k.ps[0:P, j, 0:D], den[:, j:j + 1], other, ALU.mult,
                                                 ALU.add).then_inc(s_out, 1)

                def settle(g, j):
                    b = g * GB + j
                    if j == 0:
                        dve.drain()
                    if finish == "relu":
                        dve.tensor_scalar(blk(k.y, b), t[:, j, :], 0.0, None, ALU.max)
                        return
                    if finish == "both":
                        dve.scalar_tensor_tensor(blk(k.xs, b), t[:, j, :], 0.0, blk(k.xs, b), ALU.max, ALU.add)
                        dve.drain()
                        dve.bn_stats(blk(k.stats, b), blk(k.xs, b))
                    else:
                        dve.tensor_scalar(blk(k.xs, b), t[:, j, :], 1.0, None, ALU.mult)
                        dve.bn_stats(blk(k.stats, b), t[:, j, :])

                def body(g, first, last):
                    for c in range(NB):
                        dve.wait_ge(s_e, g * NB + (c + 1))
                        m = e_slot(c)
                        if not (first and c == 0):
                            dve.wait_ge(s_p, g * NB + c)
                        dve.tensor_tensor(x[:].rearrange("p j n -> p (j n)"), e[:, m, 0, :], e[:, m, 1, :],
                                          ALU.max).then_inc(s_x, 1)
                        if not last:
                            for n in maxima(c):
                                greatest(g + 1, n)
                        if c % GB == 0:
                            dve.wait_ge(s_cnt[c // GB], g * 16 + 16)
                        if not (first and c < P_SLOTS):
                            dve.wait_ge(s_pv, g * NB + (c - P_SLOTS + 1))
                        dve.wait_ge(s_x, g * NB + (c + 1))
                        dve.scalar_tensor_tensor(p[:, p_slot(c)], x[:], 1.0, chunk(counts, c), ALU.min,
                                                 ALU.mult).then_inc(s_p, 1)
                        if c == 0 and not first:
                            take(g - 1)
                        if 2 <= c < 2 + GB and not first:
                            settle(g - 1, c - 2)
                        if c == AHEAD - 1 and not last:
                            dve.drain().then_inc(s_qmax, 1)
                        if c == AHEAD + 1 and not last:
                            limits(g + 1)

                for c in range(NB):
                    greatest(0, c)
                dve.drain().then_inc(s_qmax, 1)
                limits(0)
                groups(dve, body)
                take(NG - 1)
                for j in range(GB):
                    settle(NG - 1, j)

            @block.tensor
            def _(pe):
                pe.wait_ge(s_set, 1)

                def turn(g):
                    pe.wait_ge(s_qmax, g + 1)
                    if not isinstance(g, int) or g >= 1:
                        pe.wait_ge(s_r, g)
                    many, one = spread(0)
                    for j in range(GB):
                        tr = pe.transpose(many[:, j, :] if j < 4 else one, qmax[:, j, :], k.ident[0:P, 0:P])
                    tr.then_inc(s_tr, 1)

                def rows(g):
                    pe.wait_ge(s_diag, g + 1)
                    for r in range(2):
                        many, one = spread(r)
                        pe.matmul(many, ones[:], diag[:, r, 0:4, :], start=True, stop=True, skip_group_check=True)
                        mm = pe.matmul(one, ones[:], diag[:, r, 4, :], start=True, stop=True, skip_group_check=True)
                    mm.then_inc(s_bc, 1)

                def body(g, first, last):
                    for c in range(NB):
                        pe.wait_ge(s_p, g * NB + (c + 1))
                        for j in range(GB):
                            if c == 0 and not first:
                                pe.wait_ge(s_out, (g - 1) * GB + (j + 1))
                            mm = pe.matmul(k.ps[0:P, j, 0:D + 1], p[:, p_slot(c), j, :], k.h[:, c, :],
                                           start=(c == 0), stop=(c == NB - 1))
                        mm.then_inc(s_pv, 1)
                        if c == AHEAD and not last:
                            turn(g + 1)
                        if c == AHEAD + 2 and not last:
                            rows(g + 1)

                turn(0)
                rows(0)
                groups(pe, body)


def stage_mlp(nc, k, w):
    KH = HID // 128
    with ExitStack() as ctx:
        sb, sem = sb_of(nc, ctx), sem_of(nc, ctx)
        w1 = sb("m_w1", [128, 2, HID], F32)
        w2 = sb("m_w2", [128, KH, HID], F32)
        w3 = sb("m_w3", [128, KH, D], F32)
        rows = sb("m_rows", [P, 2, HID], F32)
        rows3 = sb("m_rows3", [P, 3, D], F32)
        cols = sb("m_cols", [128, 4, KH], F32)
        hin = sb("m_hin", [P, D], F32)
        ht = sb("m_ht", [128, 2, P], F32)
        u = sb("m_u", [P, 2, HID], F32)
        un = sb("m_un", [P, 2, HID], F32)
        ut = sb("m_ut", [128, 2, KH, P], F32)
        st = sb("m_st", [P, 2, 2, 6], F32)
        mv = sb("m_mv", [P, 3, 2], F32)
        rs = sb("m_rs", [P, 3, 2], F32)
        r3 = sb("m_r3", [P, D], F32)
        st3 = sb("m_st3", [P, 6], F32)
        s_w, s_in, s_tr0, s_ht = sem("m_w"), sem("m_in"), sem("m_tr0"), sem("m_ht")
        s_mm = [sem("m_mm1"), sem("m_mm2"), sem("m_mm3")]
        s_var = [sem("m_var1"), sem("m_var2"), sem("m_var3")]
        s_root = [sem("m_root1"), sem("m_root2"), sem("m_root3")]
        s_scale = [sem("m_scale1"), sem("m_scale2")]
        s_un = [sem("m_un1"), sem("m_un2")]
        s_tr = [sem("m_tr1"), sem("m_tr2")]
        s_ut = [sem("m_ut1"), sem("m_ut2")]
        s_read = [sem("m_read1"), sem("m_read2"), sem("m_read3")]
        ps_h = k.ps[:, 0, 0:2 * P].rearrange("p (h n) -> p h n", h=2)
        ps_m = [k.ps[0:P, 1:3, :], k.ps[0:P, 3:5, :]]
        ps_3 = k.ps[0:P, 7, 0:D]
        ps_u = k.ps[:, 5:7, 0:4 * P].rearrange("p m (c n) -> p m c n", c=4)
        with nc.Block() as block:
            @block.sync
            def _(sp):
                sp.dma_start(w1[:], w["w1"].rearrange("(c p) n -> p c n", p=128)).then_inc(s_w, 16)
                sp.dma_start(w2[:], w["w2"].rearrange("(c p) n -> p c n", p=128)).then_inc(s_w, 16)
                sp.dma_start(w3[:], w["w3"].rearrange("(c p) n -> p c n", p=128)).then_inc(s_w, 16)
                for n, v in enumerate(("b1", "b2")):
                    sp.dma_start(rows[:, n, :], row_bcast(w[v], P, HID)).then_inc(s_w, 16)
                for n, v in enumerate(("b3", "bn_g", "bn_b")):
                    sp.dma_start(rows3[:, n, :], row_bcast(w[v], P, D)).then_inc(s_w, 16)
                for n, v in enumerate(("g1", "be1", "g2", "be2")):
                    with nc.allow_non_contiguous_dma(reason="4 vectors of 1024"):
                        sp.dma_start(cols[:, n, :], w[v].rearrange("(c p) -> p c", p=128)).then_inc(s_w, 16)

            def blocks(eng, before, part):
                before()
                part(0, True, False)
                with eng.Fori(1, NB - 1) as b:
                    part(b, False, False)
                part(NB - 1, False, True)

            @block.tensor
            def _(pe):
                pe.wait_ge(s_w, 16 * 12)

                def turn_input(b):
                    pe.wait_ge(s_in, b + 1)
                    for h in range(2):
                        tr = pe.transpose(ps_h[:, h, :], hin[:, h * 128:(h + 1) * 128], k.ident[0:P, 0:P])
                    tr.then_inc(s_tr0, 1)

                def first(b, begin=False):
                    pe.wait_ge(s_ht, b + 1)
                    if not begin:
                        pe.wait_ge(s_read[0], b)
                    for n in range(2):
                        for c in range(2):
                            mm = pe.matmul(ps_m[0][:, n, :], ht[:, c, :], w1[:, c, n * 512:(n + 1) * 512],
                                           start=(c == 0), stop=(c == 1))
                    mm.then_inc(s_mm[0], 1)

                def turn(l, b):
                    pe.wait_ge(s_un[l], b + 1)
                    for c in range(KH):
                        tr = pe.transpose(ps_u[:, c // 4, c % 4, :], un[:, l, c * 128:(c + 1) * 128], k.ident[0:P, 0:P])
                        if c % 4 == 3:
                            tr.then_inc(s_tr[l], 1)

                def second(b, n, bring_in=False):
                    for c in range(KH):
                        if n == 0:
                            pe.wait_ge(s_ut[0], b * KH + (c + 1))
                            if c == KH - 1 and bring_in:
                                turn_input(b + 1)
                        mm = pe.matmul(ps_m[1][:, n, :], ut[:, 0, c, :], w2[:, c, n * 512:(n + 1) * 512],
                                       start=(c == 0), stop=(c == KH - 1))
                    mm.then_inc(s_mm[1], 1)

                def third(b):
                    for c in range(KH):
                        pe.wait_ge(s_ut[1], b * KH + (c + 1))
                        mm = pe.matmul(ps_3, ut[:, 1, c, :], w3[:, c, :], start=(c == 0), stop=(c == KH - 1))
                    mm.then_inc(s_mm[2], 1)

                def before():
                    turn_input(0)
                    first(0, begin=True)

                def part(b, begin, end):
                    if not isinstance(b, int) or b >= 2:
                        pe.wait_ge(s_ut[1], (b - 1) * KH)
                    turn(0, b)
                    if not begin:
                        pe.wait_ge(s_read[1], b)
                    second(b, 0, bring_in=not end)
                    if not end:
                        first(b + 1)
                    if not begin:
                        pe.wait_ge(s_ut[0], b * KH + KH)
                        turn(1, b - 1)
                        if not isinstance(b, int) or b >= 2:
                            pe.wait_ge(s_read[2], b - 1)
                        third(b - 1)
                    second(b, 1)

                blocks(pe, before, part)
                turn(1, NB - 1)
                pe.wait_ge(s_read[2], NB - 1)
                third(NB - 1)

            @block.scalar
            def _(act):
                act.preload_act_table(ACT.Sqrt)
                act.wait_ge(s_w, 16 * 12)

                def head(b):
                    act.wait_ge(s_tr0, b + 1)
                    act.copy(ht[:], ps_h).then_inc(s_ht, 1)

                def root(l, b):
                    act.wait_ge(s_var[l], b + 1)
                    act.activation(rs[:, l, 0:1], rs[:, l, 0:1], ACT.Sqrt).then_inc(s_root[l], 1)

                def hidden(l, b):
                    root(l, b)
                    act.wait_ge(s_scale[l], b + 1)
                    act.activation(un[:, l, :], u[:, l, :], ACT.Identity, bias=rs[:, l, 1:2],
                                   scale=rs[:, l, 0:1]).then_inc(s_un[l], 1)

                def turned(l, b):
                    for c in range(KH):
                        if c % 4 == 0:
                            act.wait_ge(s_tr[l], b * 2 + (c // 4 + 1))
                        act.activation(ut[:, l, c, :], ps_u[:, c // 4, c % 4, :], ACT.Relu,
                                       bias=cols[:, 2 * l + 1, c:c + 1],
                                       scale=cols[:, 2 * l, c:c + 1]).then_inc(s_ut[l], 1)

                def before():
                    head(0)
                    hidden(0, 0)

                def part(b, begin, end):
                    if not begin:
                        act.wait_ge(s_mm[1], b * 2)
                    turned(0, b)
                    if not end:
                        head(b + 1)
                    if not begin:
                        if not isinstance(b, int) or b >= 2:
                            act.wait_ge(s_mm[2], b - 1)
                        turned(1, b - 1)
                    if not end:
                        hidden(0, b + 1)
                    if not begin:
                        root(2, b - 1)
                    hidden(1, b)

                blocks(act, before, part)
                act.wait_ge(s_mm[2], NB - 1)
                turned(1, NB - 1)
                root(2, NB - 1)

            @block.vector
            def _(dve):
                dve.wait_ge(s_w, 16 * 12)

                def scales(l, b):
                    dve.bn_aggr(mv[:, l, :], st[:, l] if l < 2 else st3[:])
                    dve.drain()
                    dve.tensor_scalar(rs[:, l, 0:1], mv[:, l, 1:2], LN_EPS, None, ALU.add).then_inc(s_var[l], 1)
                    dve.wait_ge(s_root[l], b + 1)
                    dve.reciprocal(rs[:, l, 0:1], rs[:, l, 0:1])
                    dve.drain()

                def hidden(l, b, begin=False):
                    dve.wait_ge(s_mm[l], b * (l + 1) + (l + 1))
                    if not begin:
                        dve.wait_ge(s_un[l], b)
                    dve.tensor_tensor(u[:, l, :].rearrange("p (m n) -> p m n", m=2), ps_m[l],
                                      rows[:, l, :].rearrange("p (m n) -> p m n", m=2), ALU.add).then_inc(s_read[l], 1)
                    dve.drain()
                    for m in range(2):
                        dve.bn_stats(st[:, l, m, :], u[:, l, m * 512:(m + 1) * 512])
                    dve.drain()
                    scales(l, b)
                    dve.scalar_tensor_tensor(rs[:, l, 1:2], mv[:, l, 0:1], -1.0, rs[:, l, 0:1], ALU.mult,
                                             ALU.mult).then_inc(s_scale[l], 1)

                def bring(b, begin=False):
                    if not begin:
                        dve.wait_ge(s_tr0, b)
                    dve.tensor_scalar(hin[:], blk(k.y, b), 1.0, None, ALU.mult).then_inc(s_in, 1)

                def out(b):
                    dve.wait_ge(s_mm[2], b + 1)
                    dve.tensor_tensor(r3[:], ps_3, rows3[:, 0, :], ALU.add).then_inc(s_read[2], 1)
                    dve.drain()
                    dve.tensor_tensor(r3[:], r3[:], blk(k.xs, b), ALU.add)
                    dve.drain()
                    dve.bn_stats(st3[:], r3[:])
                    dve.drain()
                    scales(2, b)
                    dve.tensor_scalar(r3[:], r3[:], mv[:, 2, 0:1], rs[:, 2, 0:1], ALU.subtract, ALU.mult)
                    dve.drain()
                    dve.tensor_tensor(r3[:], r3[:], rows3[:, 1, :], ALU.mult)
                    dve.drain()
                    dve.tensor_tensor(r3[:], r3[:], rows3[:, 2, :], ALU.add)
                    dve.drain()
                    dve.scalar_tensor_tensor(blk(k.xs, b), r3[:], 0.0, blk(k.xs, b), ALU.max, ALU.add)
                    dve.drain()
                    dve.bn_stats(blk(k.stats, b), blk(k.xs, b))
                    dve.drain()

                def before():
                    bring(0, begin=True)
                    hidden(0, 0, begin=True)

                def part(b, begin, end):
                    if not end:
                        bring(b + 1)
                        hidden(0, b + 1)
                    if not begin:
                        out(b - 1)
                    hidden(1, b, begin)

                blocks(dve, before, part)
                out(NB - 1)


def stage_add_loops(nc, k):
    with ExitStack() as ctx:
        sb, sem = sb_of(nc, ctx), sem_of(nc, ctx)
        diag = sb("loops", [P, NB, P], F16)
        open_ = sb("loops_open", [P, NB, P], BF16)
        s_in, s_add, s_out = sem("l_in"), sem("l_add"), sem("l_out")
        with nc.Block() as block:
            @block.sync
            def _(sp):
                for b in range(NB):
                    sp.dma_start(diag[:, b, :], k.a_dram[b, 0:P, b * P:(b + 1) * P]).then_inc(s_in, 16)
                    sp.dma_start(open_[:, b, :], k.m_dram[b, 0:P, b * P:(b + 1) * P]).then_inc(s_in, 16)
                sp.wait_ge(s_add, 1)
                for b in range(NB):
                    sp.dma_start(k.a_dram[b, 0:P, b * P:(b + 1) * P], diag[:, b, :]).then_inc(s_out, 16)
                    sp.dma_start(k.m_dram[b, 0:P, b * P:(b + 1) * P], open_[:, b, :]).then_inc(s_out, 16)
                sp.wait_ge(s_out, 32 * NB)

            @block.vector
            def _(dve):
                dve.wait_ge(s_in, 32 * NB)
                each = k.ident16[:].unsqueeze(1).to_broadcast([P, NB, P])
                dve.tensor_tensor(diag[:], diag[:], each, ALU.add)
                dve.scalar_tensor_tensor(open_[:], each, 0.0, open_[:], ALU.is_equal, ALU.mult)
                dve.drain().then_inc(s_add, 1)


def stage_last(nc, k, out):
    with ExitStack() as ctx:
        sem = sem_of(nc, ctx)
        s_norm, s_store = sem("o_norm"), sem("o_store")
        with nc.Block() as block:
            @block.sync
            def _(sp):
                sp.dma_start(out.rearrange("(b p) d -> p b d", p=P), k.xs[:]).then_inc(s_store, 16)
                sp.wait_ge(s_store, 16)


def program(nc, ins, outs, upto=99):
    TAKEN.clear()
    with ExitStack() as ctx:
        sb = sb_of(nc, ctx)
        k = Core()
        k.ps = ctx.enter_context(nc.psum_tensor("ps", [128, 8, 512], F32))
        k.ident = sb("ident", [128, 128], F32)
        k.ident16 = sb("ident16", [P, P], F16)
        k.windows = sb("windows", [1, 2 * NB], I32)
        k.deg, k.deg1, k.dinv, k.dinv_lo, k.rstd, k.mean, k.q, k.kk, k.q_slope = (sb(v, [P, NB], F32) for v in (
            "deg", "deg1", "dinv", "dinv_lo", "rstd", "mean", "q", "kk", "q_slope"))
        k.stats = sb("stats", [P, NB, 6], F32)
        k.mv = sb("mv", [P, NB, 2], F32)
        k.windows_dram = nc.dram_tensor("windows_dram", (NB, 2), I32).ap()
        k.a_dram = nc.dram_tensor("a_dram", (NB, 128, N), F16).ap()
        k.m_dram = nc.dram_tensor("m_dram", (NB, 128, N), BF16).ap()
        k.e_dram = nc.dram_tensor("e_dram", (NB, P, D + 1), F32).ap()
        with ExitStack() as early:
            sbe = sb_of(nc, early)
            k.src_iota = sbe("src_iota", [128, NB, PAD], F16)
            k.dst_iota = sbe("dst_iota", [128, P], F32)
            stage_windows(nc, k, ins["dst"])
            stage_edges(nc, k, ins["srcT"], ins["dstT"], ins["eaT"], ins["L2_gnn_ee_w1"], ins["L2_gnn_ee_b1"])
        k.xs = sb("xs", [P, NB, D], F32)

        def finish():
            stage_last(nc, k, outs["out"])

        with ExitStack() as gcn:
            sbg = sb_of(nc, gcn)
            pa, pb = sbg("parts_a", [P, NB, 2 * D], F16), sbg("parts_b", [P, NB, 2 * D], F16)
            stage_first_split(nc, k, ins["x"], pa)
            stage_aggregate(nc, k, "g1", pa, "gcn", ins["W1T"], ins["L0_gnn_b1"], out_parts=pb)
            stage_aggregate(nc, k, "g2", pb, "gcn", ins["W2T"], ins["L0_gnn_b2"], out_parts=pa)
            stage_aggregate(nc, k, "g3", pa, "last", ins["W3T"], ins["L0_gnn_b3"])
        if upto == 1:
            return finish()
        with ExitStack() as att:
            k.h = sb_of(nc, att)("h_att", [P, NB, D + 1], F32)
            stage_project(nc, k, "p1", k.xs, True, ins["L1_gnn_Wv"], ins["L1_gnn_bv"], ins["L1_gnn_wq"],
                          ins["L1_gnn_wk"], ins["L1_gnn_bq"], ins["L1_gnn_bk"])
            stage_attention(nc, k, "t1", "res")
        if upto == 2:
            return finish()
        k.y = sb("y", [P, NB, D], F32)
        with ExitStack() as gin:
            pa = sb_of(nc, gin)("parts_c", [P, NB, 2 * D], F16)
            stage_project(nc, k, "p2", k.xs, True, parts=pa)
            stage_aggregate(nc, k, "gi", pa, "gin", ins["L2_gnn_ee_w2"], ins["L2_gnn_ee_b2"],
                            rb1=ins["L2_gnn_ee_b1"], eps=ins["L2_gnn_eps"])
        stage_mlp(nc, k, {v: ins["L2_gnn_" + v] for v in ("w1", "w2", "w3", "b1", "b2", "b3", "g1", "be1", "g2", "be2", "bn_g", "bn_b")})
        if upto == 3:
            return finish()
        recycle(nc)
        stage_add_loops(nc, k)
        k.h = sb("h_att2", [P, NB, D + 1], F32)
        stage_project(nc, k, "p3", k.xs, True, ins["L3_gnn_W1"], None, ins["L3_gnn_a1_src"], ins["L3_gnn_a1_dst"])
        stage_attention(nc, k, "t3", "relu", ins["L3_gnn_b1"])
        stage_project(nc, k, "p4", k.y, False, ins["L3_gnn_W2"], None, ins["L3_gnn_a2_src"], ins["L3_gnn_a2_dst"])
        stage_attention(nc, k, "t4", "both", ins["L3_gnn_b2"])
        stage_project(nc, k, "p5", k.xs, True)
        finish()


_AS_THEY_ARE = ("x", "dst", "L0_gnn_b1", "L0_gnn_b2", "L0_gnn_b3", "L1_gnn_Wv", "L1_gnn_bv", "L1_gnn_wq", "L1_gnn_bq",
                "L1_gnn_wk", "L1_gnn_bk", "L2_gnn_eps", "L2_gnn_ee_w1", "L2_gnn_ee_b1", "L2_gnn_ee_w2", "L2_gnn_ee_b2",
                "L2_gnn_w1", "L2_gnn_b1", "L2_gnn_g1", "L2_gnn_be1", "L2_gnn_w2", "L2_gnn_b2", "L2_gnn_g2",
                "L2_gnn_be2", "L2_gnn_w3", "L2_gnn_b3", "L2_gnn_bn_g", "L2_gnn_bn_b", "L3_gnn_W1", "L3_gnn_a1_src",
                "L3_gnn_a1_dst", "L3_gnn_b1", "L3_gnn_W2", "L3_gnn_a2_src", "L3_gnn_a2_dst", "L3_gnn_b2")


def kernel(**inputs):
    import concourse.bacc as bacc
    from concourse.bass_utils import run_bass_kernel_spmd

    a = {n: np.ascontiguousarray(inputs[n]).reshape(inputs[n].shape or (1,)) for n in _AS_THEY_ARE}
    a["srcT"] = np.ascontiguousarray(inputs["src"].reshape(E // P, P).T)
    a["dstT"] = np.ascontiguousarray(inputs["dst"].reshape(E // P, P).T)
    a["eaT"] = np.ascontiguousarray(inputs["edge_attr_64"].T)
    for n in ("W1", "W2", "W3"):
        a[n + "T"] = np.ascontiguousarray(inputs["L0_gnn_" + n].T)
    nc = bacc.Bacc("TRN2", target_bir_lowering=False, num_devices=1)
    ins = {n: nc.dram_tensor("in_" + n, v.shape, mybir.dt.from_np(v.dtype), kind="ExternalInput").ap()
           for n, v in a.items()}
    out = nc.dram_tensor("out_x", (N, D), F32, kind="ExternalOutput").ap()
    program(nc, ins, {"out": out})
    r = run_bass_kernel_spmd(nc, [{"in_" + n: v for n, v in a.items()}], core_ids=[0])
    return r.results[0]["out_x"]
```

```python
import numpy as np
from contextlib import ExitStack

import concourse.bass as bass
from concourse import mybir

F32 = mybir.dt.float32
F16 = mybir.dt.float16
BF16 = mybir.dt.bfloat16
I32 = mybir.dt.int32
ALU = mybir.AluOpType
ACT = mybir.ActivationFunctionType
AX = mybir.AxisListType

N, D, E, EDIM, HID = 3125, 256, 50000, 64, 1024
P = 125
NB = N // P
NPAIR = E // (2 * P)
PAD = 128
LO = 2048.0
BIG = 1e30
LN_EPS = 1e-5
SLOPE = 0.2
GB = 5
NG = NB // GB
CENTER = 1562


TAKEN = []


class Core:
    pass


def sb_of(nc, ctx):
    return lambda name, shape, dt: ctx.enter_context(nc.sbuf_tensor(name, shape, dt))


def sem_of(nc, ctx):
    def sem(name):
        TAKEN.append(nc.alloc_semaphore(name))
        return TAKEN[-1]
    return sem


def recycle(nc):
    nc.clear_and_free_semaphores(TAKEN)
    TAKEN.clear()
    nc.all_engine_barrier()


def row_bcast(vec, parts, n):
    return bass.AP(vec.tensor, vec.offset, [[0, parts], [1, n]])


def stage_windows(nc, k, dst):
    with ExitStack() as ctx:
        sb, sem = sb_of(nc, ctx), sem_of(nc, ctx)
        H = NPAIR // 2
        pairs_i = sb("pairs_i", [H, 2, 2 * P], I32)
        pairs = sb("pairs", [H, 2, 2 * P], F32)
        ext = sb("ext", [H, 4], F32)
        diag = sb("diag", [H, 4, H], F32)
        ones = sb("ones_w", [H, NB], F32)
        blk_lo = sb("blk_lo", [NB, 1], F32)
        blk_hi = sb("blk_hi", [NB, 1], F32)
        pair_id = sb("pair_id", [NB, 2, H], F32)
        meets = sb("meets", [NB, 2, H], F32)
        cand = sb("cand", [NB, 2, 2, H], F32)
        lohi = sb("lohi", [NB, 2], F32)
        lohi_i = sb("lohi_i", [NB, 2], I32)
        s_in, s_tab, s_diag, s_row, s_win, s_out = (sem(x) for x in (
            "w_in", "w_tables", "w_diag", "w_rows", "w_windows", "w_out"))
        rows = k.ps[0:NB, 0, 0:4 * H].rearrange("p (s h) -> p s h", s=4)
        with nc.Block() as block:
            @block.sync
            def _(sp):
                sp.dma_start(pairs_i[:], dst.rearrange("(p a e) -> p a e", a=2, e=2 * P)).then_inc(s_in, 16)
                sp.wait_ge(s_win, 1)
                sp.dma_start(k.windows_dram, lohi_i[:]).then_inc(s_out, 16)
                sp.wait_ge(s_out, 16)
                sp.dma_start(k.windows[:, 0:2 * NB], k.windows_dram.rearrange("b s -> (b s)")[None, :]).then_inc(s_out, 16)
                sp.wait_ge(s_out, 32)

            @block.gpsimd
            def _(pool):
                pool.memset(k.src_iota[:], 9999.0)
                pool.drain()
                pool.iota(k.src_iota[:, :, 0:P], pattern=[[P, NB], [1, P]], base=-CENTER, channel_multiplier=0,
                          allow_small_or_imprecise_dtypes=True)
                pool.iota(k.dst_iota[:], pattern=[[1, P]], base=0, channel_multiplier=0,
                          allow_small_or_imprecise_dtypes=True)
                pool.iota(blk_lo[:], pattern=[[0, 1]], base=0, channel_multiplier=P,
                          allow_small_or_imprecise_dtypes=True)
                pool.iota(blk_hi[:], pattern=[[0, 1]], base=P, channel_multiplier=P,
                          allow_small_or_imprecise_dtypes=True)
                pool.iota(pair_id[:], pattern=[[1, 2], [2, H]], base=1, channel_multiplier=0,
                          allow_small_or_imprecise_dtypes=True)
                pool.memset(k.ident[:], 0.0)
                pool.drain()
                pool.affine_select(out=k.ident[:], in_=k.ident[:], compare_op=ALU.not_equal, fill=1.0, base=0,
                                   pattern=[[-1, 128]], channel_multiplier=1)
                pool.drain().then_inc(s_tab, 1)

            @block.vector
            def _(dve):
                dve.memset(ones[:], 1.0)
                dve.memset(k.windows[:, 2 * NB:], 0)
                dve.wait_ge(s_in, 16)
                dve.tensor_copy(pairs[:], pairs_i[:])
                dve.drain()
                dve.tensor_reduce(ext[:, 0:2], pairs[:], AX.X, ALU.min)
                dve.tensor_reduce(ext[:, 2:4], pairs[:], AX.X, ALU.max)
                dve.wait_ge(s_tab, 1)
                dve.tensor_copy(k.ident16[:], k.ident[0:P, 0:P])
                dve.drain()
                for s in range(4):
                    dve.tensor_scalar(diag[:, s, :], k.ident[0:H, 0:H], ext[:, s:s + 1], None, ALU.mult)
                dve.drain().then_inc(s_diag, 1)
                dve.wait_ge(s_row, 1)
                dve.tensor_scalar(meets[:], rows[:, 2:4, :], blk_lo[:, 0:1], None, ALU.is_ge)
                dve.drain()
                dve.scalar_tensor_tensor(meets[:], rows[:, 0:2, :], blk_hi[:, 0:1], meets[:], ALU.is_lt, ALU.mult)
                dve.drain()
                dve.scalar_tensor_tensor(cand[:, 0], pair_id[:], float(NPAIR + 1), meets[:], ALU.subtract, ALU.mult)
                dve.tensor_tensor(cand[:, 1], pair_id[:], meets[:], ALU.mult)
                dve.drain()
                dve.tensor_reduce(lohi[:, 0:1], cand[:, 0], AX.XY, ALU.min)
                dve.tensor_reduce(lohi[:, 1:2], cand[:, 1], AX.XY, ALU.max)
                dve.drain()
                dve.tensor_scalar(lohi[:, 0:1], lohi[:, 0:1], float(NPAIR), float(NPAIR - 1), ALU.add, ALU.min)
                dve.drain()
                dve.scalar_tensor_tensor(lohi[:, 1:2], lohi[:, 0:1], 1.0, lohi[:, 1:2], ALU.add, ALU.max)
                dve.drain()
                dve.tensor_copy(lohi_i[:], lohi[:])
                dve.drain().then_inc(s_win, 1)

            @block.tensor
            def _(pe):
                pe.wait_ge(s_diag, 1)
                for s in range(4):
                    mm = pe.matmul(rows[:, s, :], ones[:, :], diag[:, s, :], start=(s == 0), stop=True,
                                   skip_group_check=True)
                mm.then_inc(s_row, 1)


def stage_edges(nc, k, srcT, dstT, eaT, ee_w1, ee_b1, x):
    SCALE = 16.0
    B_HI, B_LO = EDIM, 96
    with ExitStack() as ctx:
        sb, sem = sb_of(nc, ctx), sem_of(nc, ctx)
        ids_i = sb("ids_i", [P, 2, 2 * NPAIR], I32)
        src_f = sb("src_f", [P, 2 * NPAIR], F32)
        dst_f = sb("dst_f", [P, 2 * NPAIR], F32)
        dst_blk = sb("dst_blk", [P, P], F16)
        src_hot = sb("src_hot", [P, 2, NB, PAD], F16)
        dst_hot = sb("dst_hot", [P, 2, P], F16)
        sum_hot = sb("sum_hot", [P, 2, P], F16)
        ea = sb("ea", [128, 2, 2 * P], F32)
        f_hilo = sb("f_hilo", [128, 2, P], F16)
        f_low = sb("f_low", [B_LO + 1, 2, P], F16)
        w_in = sb("w_in_e", [128, 2, D], F32)
        w_hi = sb("w_hi_e", [128, D], F16)
        w_low = sb("w_low_e", [128, D], F16)
        r_hi = sb("r_hi", [P, 2, D + 1], F16)
        r_lo = sb("r_lo", [P, 2, D], F16)
        zero = sb("zero_e", [P, 512], F16)
        a_out = sb("a_out", [128, N], F16)
        m_out = sb("m_out", [128, N], BF16)
        e_out = sb("e_out", [P, D], F32)
        s_ids, s_w, s_set, s_store, s_mstore = (sem(x) for x in ("e_ids", "e_w", "e_set", "e_store", "e_mstore"))
        s_ea, s_fhi, s_flo, s_mlp, s_rhi, s_rlo, s_hot, s_acc, s_out_a, s_out_v, s_free, s_masks, s_mfree = (sem(x) for x in (
            "e_ea", "e_fhi", "e_flo", "e_mlp", "e_rhi", "e_rlo", "e_hot", "e_acc", "e_out_a", "e_out_v", "e_free", "e_masks",
            "e_mfree"))
        s_used = [sem("e_used0"), sem("e_used1")]
        s_sumhot = sem("e_sumhot")
        s_seen, s_ready = sem("e_seen"), sem("e_ready")
        s_x = sem("e_x")
        mlp = k.ps[0:P, 7, :].rearrange("p (i f) -> p i f", i=2)
        esum = k.ps[0:P, 6, 128:128 + D + 1]

        def chunk(c):
            return k.ps[:, c // 4, (c % 4) * P:(c % 4 + 1) * P]

        def next_window(eng, regs, b):
            for n, reg in enumerate(regs):
                eng.reg_load(reg, k.windows[0:1, 2 * b + n:2 * b + n + 1] if isinstance(b, int)
                             else k.windows[0:1, bass.ds(b * 2 + n, 1)])

        def window_regs(eng, name):
            regs = [eng.alloc_register(f"{name}_window_{n}") for n in ("lo", "hi")]
            next_window(eng, regs, 0)
            return regs

        def window(eng, regs, b):
            lo = eng.snap(regs[0], min_val=0, max_val=NPAIR - 1)
            hi = eng.snap(regs[1], min_val=1, max_val=NPAIR)
            next_window(eng, regs, b + 1)
            return lo, hi

        def slot_of(tile, t):
            return tile[:, bass.ds(t % 2, 1)].rearrange("p a (i e) -> p (a i) e", i=2)

        def dram(t, b):
            return t[b] if isinstance(b, int) else t[bass.ds(b, 1)].rearrange("a p n -> (a p) n")

        with nc.Block() as block:
            @block.sync
            def _(sp):
                sp.dma_start(ids_i[:, 0], srcT).then_inc(s_ids, 16)
                sp.dma_start(ids_i[:, 1], dstT).then_inc(s_ids, 16)
                for half in range(2):
                    sp.dma_start(w_in[half * EDIM:(half + 1) * EDIM, 0, :], ee_w1).then_inc(s_w, 16)
                sp.wait_ge(s_set, 1)
                for row in (B_HI, B_LO):
                    sp.dma_start(w_in[row:row + 1, 1, :], ee_b1[None, :]).then_inc(s_w, 16)
                sp.dma_start(k.xs[:], x.rearrange("(b p) d -> p b d", p=P)).then_inc(s_x, 16)
                regs = window_regs(sp, "sp")
                done = sp.alloc_register("sp_pairs")
                sp.reg_mov(done, 0)
                with sp.Fori(0, NB) as b:
                    lo, hi = window(sp, regs, b)
                    with sp.Fori(lo, hi) as j:
                        t = sp.snap(done)
                        sp.wait_ge(s_flo, t + 1)
                        sp.wait_ge(s_fhi, t * 2 + 2)
                        sp.wait_ge(s_ea, t * 16 + 16)
                        sp.dma_start(ea[:, bass.ds(t % 2, 1)].rearrange("p a e -> p (a e)"),
                                     eaT[:, bass.ds(j * (2 * P), 2 * P)]).then_inc(s_ea, 16)
                        sp.reg_add(done, done, 1)
                t = sp.snap(done)
                sp.wait_ge(s_flo, t + 1)
                sp.wait_ge(s_fhi, t * 2 + 2)
                sp.wait_ge(s_ea, t * 16 + 16)
                sp.dma_start(ea[:, bass.ds(t % 2, 1)].rearrange("p a e -> p (a e)"), eaT[:, 0:2 * P]).then_inc(s_ea, 16)
                sp.wait_ge(s_ea, t * 16 + 32)
                sp.sem_inc(s_seen, 1)
                sp.wait_ge(s_x, 16)

            @block.gpsimd
            def _(pool):
                with pool.Fori(0, NB) as b:
                    pool.wait_ge(s_out_a, b * 2 + 4)
                    pool.wait_ge(s_out_v, b * 2 + 4)
                    pool.sem_inc(s_seen, 1)
                    pool.dma_start(dram(k.a_dram, b), a_out[:]).then_inc(s_store, 16)
                    pool.dma_start(dram(k.e_dram, b), e_out[:]).then_inc(s_store, 16)
                    pool.wait_ge(s_store, b * 32 + 32)
                    pool.sem_inc(s_free, 1)
                    pool.wait_ge(s_masks, b + 1)
                    pool.sem_inc(s_seen, 1)
                    pool.dma_start(dram(k.m_dram, b), m_out[:]).then_inc(s_mstore, 16)
                    pool.wait_ge(s_mstore, b * 16 + 16)
                    pool.sem_inc(s_mfree, 1)

            @block.vector
            def _(dve):
                dve.memset(w_in[EDIM:128, 1, :], 0.0)
                dve.drain().then_inc(s_set, 1)
                dve.memset(zero[:], 0.0)
                dve.memset(r_hi[:, :, D:D + 1], 1.0)
                dve.memset(f_low[B_HI:B_LO], 1.0)
                dve.memset(f_low[B_LO:B_LO + 1], 1.0 / LO)
                dve.tensor_scalar(dst_blk[:], k.dst_iota[0:P], float(-CENTER), None, ALU.add)
                dve.wait_ge(s_ids, 32)
                dve.tensor_scalar(src_f[:], ids_i[:, 0], float(-CENTER), None, ALU.add)
                dve.tensor_scalar(dst_f[:], ids_i[:, 1], float(-CENTER), None, ALU.add)
                dve.wait_ge(s_w, 64)
                dve.tensor_copy(w_hi[:], w_in[:, 0, :])
                dve.tensor_scalar(w_in[EDIM:128, 1, :], w_in[EDIM:128, 1, :], SCALE, None, ALU.mult)
                dve.drain()
                dve.tensor_tensor(w_in[0:EDIM, 0, :], w_in[0:EDIM, 0, :], w_hi[0:EDIM], ALU.subtract)
                dve.tensor_copy(w_low[EDIM:128], w_in[EDIM:128, 1, :])
                dve.drain()
                dve.tensor_scalar(w_low[0:EDIM], w_in[0:EDIM, 0, :], LO, None, ALU.mult)
                dve.tensor_tensor(w_in[B_LO:B_LO + 1, 1, :], w_in[B_LO:B_LO + 1, 1, :], w_low[B_LO:B_LO + 1], ALU.subtract)
                dve.drain()
                dve.tensor_scalar(w_low[B_LO:B_LO + 1], w_in[B_LO:B_LO + 1, 1, :], LO, None, ALU.mult)
                dve.drain().then_inc(s_set, 1)
                regs = window_regs(dve, "dve")
                done = dve.alloc_register("dve_pairs")
                dve.reg_mov(done, 0)

                def low_features(t):
                    dve.wait_ge(s_fhi, t * 2 + 6)
                    dve.scalar_tensor_tensor(f_hilo[EDIM:128], slot_of(ea[EDIM:128], t), SCALE, f_hilo[EDIM:128], ALU.mult,
                                             ALU.subtract).then_inc(s_flo, 1)

                def masks(b):
                    dve.wait_ge(s_out_a, b * 2 + 4)
                    dve.wait_ge(s_out_v, b * 2 + 4)
                    dve.wait_ge(s_mfree, b + 1)
                    dve.tensor_scalar(m_out[:], a_out[:], 0.0, -BIG, ALU.is_equal, ALU.mult)
                    dve.drain().then_inc(s_masks, 1)

                def body(b, first=False):
                    lo, hi = window(dve, regs, b)
                    with dve.Fori(lo, hi) as j:
                        t = dve.snap(done)
                        for i in range(2):
                            dve.wait_ge(s_used[i], t + 1)
                            dve.wait_ge(s_sumhot, t + 1)
                            dve.tensor_scalar(dst_hot[:, i, :], dst_blk[:], dst_f[:, bass.ds(j * 2 + i, 1)], None, ALU.is_equal)
                            dve.tensor_scalar(src_hot[:, i], k.src_iota[0:P], src_f[:, bass.ds(j * 2 + i, 1)], None,
                                              ALU.is_equal).then_inc(s_hot, 1)
                        dve.wait_ge(s_rhi, t + 1)
                        dve.scalar_tensor_tensor(r_lo[:], mlp[:], 0.0, r_hi[:, :, 0:D], ALU.max,
                                                 ALU.subtract).then_inc(s_rlo, 1)
                        dve.wait_ge(s_hot, t * 2 + 2)
                        dve.tensor_scalar(sum_hot[:], dst_hot[:], 1.0, None, ALU.mult).then_inc(s_sumhot, 1)
                        dve.reg_add(done, done, 1)
                        low_features(dve.snap(done))
                    dve.tensor_scalar(dst_blk[:], dst_blk[:], float(P), None, ALU.add)
                    dve.drain()
                    if not first:
                        masks(b - 1)
                    dve.wait_ge(s_free, b + 1)
                    t = dve.snap(done)
                    dve.wait_ge(s_acc, t * 2 + 2)
                    dve.tensor_copy(a_out[:, 16 * P:24 * P].rearrange("p (k n) -> p k n", k=2),
                                    k.ps[:, 4:6, 0:4 * P]).then_inc(s_out_v, 1)
                    dve.tensor_copy(a_out[:, 24 * P:], chunk(24))
                    dve.tensor_copy(col(k.deg, b), esum[:, D:D + 1])
                    dve.tensor_scalar(e_out[:], esum[:, 0:D], 1.0 / SCALE, None, ALU.mult).then_inc(s_out_v, 1)

                low_features(dve.snap(done))
                body(0, first=True)
                with dve.Fori(1, NB) as b:
                    body(b)
                masks(NB - 1)

            @block.scalar
            def _(act):
                act.preload_act_table(ACT.Relu)
                act.wait_ge(s_set, 2)
                regs = window_regs(act, "act")
                done = act.alloc_register("act_pairs")
                act.reg_mov(done, 0)

                def high_features(t):
                    act.wait_ge(s_mlp, t * 2 + 2)
                    act.wait_ge(s_ea, t * 16 + 32)
                    act.sem_inc(s_ready, 1)
                    act.activation(f_hilo[:], slot_of(ea, t), ACT.Copy, scale=SCALE).then_inc(s_fhi, 1)
                    act.activation(f_low[0:EDIM], slot_of(ea[0:EDIM], t), ACT.Copy, scale=SCALE / LO).then_inc(s_fhi, 1)

                def body(b, first=False):
                    lo, hi = window(act, regs, b)
                    with act.Fori(lo, hi) as j:
                        t = act.snap(done)
                        act.wait_ge(s_acc, t * 2 + 2)
                        act.wait_ge(s_mlp, t * 2 + 4)
                        act.activation(r_hi[:, :, 0:D], mlp[:], ACT.Relu).then_inc(s_rhi, 1)
                        act.reg_add(done, done, 1)
                        high_features(act.snap(done))
                    if not first:
                        act.wait_ge(s_masks, b)
                    act.wait_ge(s_free, b + 1)
                    t = act.snap(done)
                    act.wait_ge(s_acc, t * 2 + 2)
                    for m in range(2):
                        act.copy(a_out[:, 8 * m * P:8 * (m + 1) * P].rearrange("p (k n) -> p k n", k=2),
                                 k.ps[:, 2 * m:2 * m + 2, 0:4 * P]).then_inc(s_out_a, 1)

                high_features(act.snap(done))
                body(0, first=True)
                with act.Fori(1, NB) as b:
                    body(b)

            @block.tensor
            def _(pe):
                pe.sem_inc(s_mlp, 2)
                pe.sem_inc(s_acc, 2)
                pe.sem_inc(s_out_a, 2)
                pe.sem_inc(s_out_v, 2)
                pe.sem_inc(s_flo, 2)
                pe.sem_inc(s_ea, 16)
                pe.sem_inc(s_sumhot, 1)
                pe.sem_inc(s_fhi, 4)
                pe.sem_inc(s_free, 1)
                pe.sem_inc(s_mfree, 1)
                pe.sem_inc(s_used[0], 1)
                pe.sem_inc(s_used[1], 1)
                pe.wait_ge(s_set, 2)
                regs = window_regs(pe, "pe")
                done = pe.alloc_register("pe_pairs")
                pe.reg_mov(done, 0)

                def edge_mlp(t):
                    pe.wait_ge(s_flo, t + 3)
                    for i in range(2):
                        pe.matmul(mlp[:, i], f_hilo[:, i, :], w_hi[:], start=True, stop=False,
                                  skip_group_check=True)
                        pe.matmul(mlp[:, i], f_low[:, i, :], w_low[0:B_LO + 1], start=False, stop=True,
                                  skip_group_check=True).then_inc(s_mlp, 1)

                edge_mlp(pe.snap(done))
                with pe.Fori(0, NB) as b:
                    lo, hi = window(pe, regs, b)
                    for bank in range(7):
                        if bank == 0 or bank == 2:
                            pe.wait_ge(s_out_a, b * 2 + (1 + bank // 2))
                        if bank == 4 or bank == 6:
                            pe.wait_ge(s_out_v, b * 2 + (bank // 2 - 1))
                        pe.matmul(k.ps[:, bank, :], zero[:, 0:128], zero[:], start=True, stop=True,
                                  skip_group_check=True)
                    with pe.Fori(lo, hi) as j:
                        t = pe.snap(done)
                        for i in range(2):
                            pe.wait_ge(s_hot, t * 2 + (i + 1))
                            for c in range(NB):
                                mm = pe.matmul(chunk(c), src_hot[:, i, c, :], dst_hot[:, i, :], start=False, stop=False,
                                               skip_group_check=True)
                            mm.then_inc(s_used[i], 1)
                        pe.wait_ge(s_rlo, t + 1)
                        pe.wait_ge(s_sumhot, t + 2)
                        for i in range(2):
                            pe.matmul(esum, sum_hot[:, i, :], r_hi[:, i, :], start=False, stop=False,
                                      skip_group_check=True)
                            pe.matmul(esum[:, 0:D], sum_hot[:, i, :], r_lo[:, i, :], start=False, stop=False,
                                      skip_group_check=True).then_inc(s_acc, 1)
                        pe.reg_add(done, done, 1)
                        edge_mlp(pe.snap(done))


def in_steps(eng, step, tail):
    for i in range(GB):
        step(i, i)
    with eng.Fori(1, NG) as it:
        for i in range(GB):
            step(it * GB + i, i)
    for i in range(tail):
        step(NB + i, i)


def at(s, lag, first=0):
    return not isinstance(s, int) or first <= s - lag < NB


def slot(s, lag, i):
    return (i - lag) % GB


BANK3 = (0, 1, 0, 1, 2)


def split(dve, hi, lo, x2048):
    dve.tensor_scalar(hi, x2048, 1.0 / LO, None, ALU.mult)
    dve.drain()
    return dve.scalar_tensor_tensor(lo, hi, -LO, x2048, ALU.mult, ALU.add)


def groups_of(tile):
    return [tile[:, g * GB:(g + 1) * GB] for g in range(NG)]


def stage_first_split(nc, k, ring, parts):
    with ExitStack() as ctx:
        sb, sem = sb_of(nc, ctx), sem_of(nc, ctx)
        g = sb("first_g", [P, NB, D], F32)
        s_deg, s_root, s_g, s_hi = sem("f_deg"), sem("f_root"), sem("f_g"), sem("f_hi")
        with nc.Block() as block:
            @block.sync
            def _(sp):
                for i in range(GB):
                    ring.load(sp, k, i, i)

            @block.scalar
            def _(act):
                act.wait_ge(s_deg, 1)
                act.activation(k.dinv[:], k.deg1[:], ACT.Sqrt).then_inc(s_root, 1)
                for n, (src, out) in enumerate(zip(groups_of(g), groups_of(parts))):
                    act.wait_ge(s_g, n + 1)
                    act.mul(out[:, :, 0:D], src, 1.0 / LO).then_inc(s_hi, 1)

            @block.vector
            def _(dve):
                dve.tensor_scalar(k.deg1[:], k.deg[:], 1.0, None, ALU.add).then_inc(s_deg, 1)
                dve.wait_ge(s_root, 1)
                dve.reciprocal(k.dinv[:], k.dinv[:])
                dve.drain()
                dve.tensor_scalar(k.dinv_lo[:], k.dinv[:], LO, None, ALU.mult)
                dve.drain()
                for n in range(NG + 1):
                    if n < NG:
                        scale = k.dinv_lo[:, n * GB:(n + 1) * GB].unsqueeze(2).to_broadcast([P, GB, D])
                        dve.tensor_tensor(groups_of(g)[n], groups_of(k.xs)[n], scale, ALU.mult).then_inc(s_g, 1)
                    if n >= 1:
                        dve.wait_ge(s_hi, n)
                        out = groups_of(parts)[n - 1]
                        dve.scalar_tensor_tensor(out[:, :, D:2 * D], out[:, :, 0:D], -LO, groups_of(g)[n - 1],
                                                 ALU.mult, ALU.add)


def blk(t, b):
    if isinstance(b, int):
        return t[:, b, :]
    return t[:, bass.ds(b, 1), :].rearrange("p a n -> p (a n)")


def col(t, b):
    return t[:, b:b + 1] if isinstance(b, int) else t[:, bass.ds(b, 1)]


class Ring:

    def __init__(self, nc, ctx, name):
        self.tile = sb_of(nc, ctx)(name, [128, GB, N], F16)
        self.loaded = [sem_of(nc, ctx)(f"{name}{i}") for i in range(GB)]
        self.passes = 0

    def load(self, sp, k, i, b):
        src = k.a_dram[b] if isinstance(b, int) else k.a_dram[bass.ds(b, 1)].rearrange("a p n -> (a p) n")
        sp.dma_start(self.tile[:, i, :], src).then_inc(self.loaded[i], 16)


def stage_aggregate(nc, k, name, ring, last_pass, parts, finish, w, bias, out_parts=None, rb1=None, eps=None):
    gin = finish == "gin"
    with ExitStack() as ctx:
        sb0, sem0 = sb_of(nc, ctx), sem_of(nc, ctx)
        sb = lambda n, s, d: sb0(f"{name}_{n}", s, d)
        sem = lambda n: sem0(f"{name}_{n}")
        a_ring = ring.tile
        before = ring.passes * NG * 16
        ring.passes += 1
        wt = sb("w", [128, 2, D], F32)
        brow = sb("bias", [P, D], F32)
        z_lo = sb("z_lo", [P, GB, D], F32)
        z = sb("z", [P, GB, D], F32)
        zt = sb("zt", [128, GB, 2, P], F32)
        t = sb("t", [P, D], F32)
        g = sb("g", [P, D], F32)
        s_w, s_agg, s_zlo, s_z, s_tr, s_zt, s_y, s_post = (sem(x) for x in (
            "w", "agg", "zlo", "z", "tr", "zt", "y", "post"))
        ps_t = k.ps[:, 6, 0:2 * P].rearrange("p (h n) -> p h n", h=2)
        ps_y = k.ps[0:P, 7, 0:D]
        nw = 2
        if gin:
            e_in = sb("e_in", [P, GB, D], F32)
            er = sb("er", [P, GB, D], F32)
            rb1row = sb("rb1", [P, D], F32)
            eps1 = sb("eps1", [P, 1], F32)
            s_e = [sem(f"e{i}") for i in range(GB)]
            s_er = sem("er")
            nw = 4
        with nc.Block() as block:
            @block.sync
            def _(sp):
                sp.dma_start(wt[:], w.rearrange("(h p) n -> p h n", h=2)).then_inc(s_w, 16)
                sp.dma_start(brow[:], row_bcast(bias, P, D)).then_inc(s_w, 16)
                if gin:
                    sp.dma_start(rb1row[:], row_bcast(rb1, P, D)).then_inc(s_w, 16)
                    sp.dma_start(eps1[:], row_bcast(eps, P, 1)).then_inc(s_w, 16)
                if gin:
                    for i in range(GB):
                        sp.dma_start(e_in[:, i, :], k.e_dram[i]).then_inc(s_e[i], 16)
                with sp.Fori(1, NG) as it:
                    for i in range(GB):
                        b = it * GB + i
                        sp.wait_ge(s_agg, it * GB + (i - GB + 1))
                        ring.load(sp, k, i, b)
                        if gin:
                            sp.wait_ge(s_er, it * GB + (i - GB + 1))
                            sp.dma_start(e_in[:, i, :], k.e_dram[bass.ds(b, 1)].rearrange("a p n -> (a p) n")).then_inc(s_e[i], 16)

                if not last_pass:
                    for i in range(GB):
                        sp.wait_ge(s_agg, NB - GB + i + 1)
                        ring.load(sp, k, i, i)

            @block.tensor
            def _(pe):
                pe.wait_ge(s_w, 16 * nw)

                def step(s, i, it=None):
                    if at(s, 0):
                        pe.wait_ge(ring.loaded[i], before + 16 if it is None else it * 16 + (before + 16))
                        bank = BANK3[i]
                        for c in range(NB):
                            pe.matmul(k.ps[0:P, bank, :], a_ring[0:P, i, c * P:(c + 1) * P], parts[:, c, :],
                                      start=(c == 0), stop=False)
                        pe.matmul(k.ps[0:P, bank, :], k.ident16[:], blk(parts, s), start=False,
                                  stop=True).then_inc(s_agg, 1)
                    if at(s, 1):
                        j = slot(s, 1, i)
                        pe.wait_ge(s_z, s)
                        if not isinstance(s, int) or s >= 2:
                            pe.wait_ge(s_zt, s - 1)
                        src = er if gin else z
                        for h in range(2):
                            tr = pe.transpose(ps_t[:, h, :], src[:, j, h * 128:(h + 1) * 128], k.ident[0:P, 0:P])
                        tr.then_inc(s_tr, 1)
                    if at(s, 2):
                        j = slot(s, 2, i)
                        pe.wait_ge(s_zt, s - 1)
                        if not isinstance(s, int) or s >= 3:
                            pe.wait_ge(s_post, s - 2)
                        for h in range(2):
                            mm = pe.matmul(ps_y, zt[:, j, h, :], wt[:, h, :], start=(h == 0), stop=(h == 1))
                        mm.then_inc(s_y, 1)

                for i in range(GB):
                    step(i, i)
                with pe.Fori(1, NG) as it:
                    for i in range(GB):
                        step(it * GB + i, i, it)
                for i in range(2):
                    step(NB + i, i)

            @block.scalar
            def _(act):
                def step(s, i):
                    if at(s, 0):
                        act.wait_ge(s_agg, s + 1)
                        act.mul(z_lo[:, i, :], k.ps[0:P, BANK3[i], D:2 * D], 1.0 / LO).then_inc(s_zlo, 1)
                    if at(s, 1):
                        act.wait_ge(s_tr, s)
                        if not isinstance(s, int) or s >= GB + 1:
                            act.wait_ge(s_y, s - GB)
                        act.copy(zt[:, slot(s, 1, i)], ps_t).then_inc(s_zt, 1)

                in_steps(act, step, 1)

            @block.vector
            def _(dve):
                dve.wait_ge(s_w, 16 * nw)
                if gin:
                    dve.tensor_scalar(rb1row[:], rb1row[:], 0.0, None, ALU.max)
                    dve.tensor_scalar(eps1[:], eps1[:], 1.0, None, ALU.add)
                    dve.drain()

                def step(s, i, it=None):
                    if at(s, 0):
                        if gin:
                            dve.wait_ge(s_e[i], 16 if it is None else it * 16 + 16)
                            dve.tensor_tensor(er[:, i, :], e_in[:, i, :], rb1row[:], ALU.add).then_inc(s_er, 1)
                        dve.wait_ge(s_zlo, s + 1)
                        dve.tensor_tensor(z[:, i, :], k.ps[0:P, BANK3[i], 0:D], z_lo[:, i, :],
                                          ALU.add).then_inc(s_z, 1)
                    if at(s, 2):
                        b = s - 2
                        dve.wait_ge(s_y, s - 1)
                        if gin:
                            dve.scalar_tensor_tensor(t[:], blk(k.xs, b), eps1[:, 0:1], z[:, slot(s, 2, i), :],
                                                     ALU.mult, ALU.add)
                            dve.scalar_tensor_tensor(g[:], brow[:], col(k.deg1, b), ps_y, ALU.mult,
                                                     ALU.add).then_inc(s_post, 1)
                            dve.drain()
                            dve.tensor_tensor(blk(k.y, b), t[:], g[:], ALU.add)
                            dve.drain()
                            return
                        dve.scalar_tensor_tensor(t[:], ps_y, col(k.dinv, b), brow[:], ALU.mult,
                                                 ALU.add).then_inc(s_post, 1)
                        dve.drain()
                        if finish == "gcn":
                            dve.tensor_scalar(g[:], t[:], 0.0, col(k.dinv_lo, b), ALU.max, ALU.mult)
                            dve.drain()
                            out = blk(out_parts, b)
                            split(dve, out[:, 0:D], out[:, D:2 * D], g[:])
                        else:
                            dve.tensor_tensor(blk(k.xs, b), t[:], blk(k.xs, b), ALU.add)
                            dve.drain()
                            dve.bn_stats(blk(k.stats, b), blk(k.xs, b))
                        dve.drain()

                for i in range(GB):
                    step(i, i)
                with dve.Fori(1, NG) as it:
                    for i in range(GB):
                        step(it * GB + i, i, it)
                for i in range(2):
                    step(NB + i, i)


def norm_factors(dve, k, s_var, s_root):
    for b in range(NB):
        dve.bn_aggr(k.mv[:, b, :], k.stats[:, b, :])
    dve.drain()
    dve.tensor_scalar(k.rstd[:], k.mv[:, :, 1], LN_EPS, None, ALU.add).then_inc(s_var, 1)
    dve.tensor_copy(k.mean[:], k.mv[:, :, 0])
    dve.wait_ge(s_root, 1)
    dve.reciprocal(k.rstd[:], k.rstd[:])
    dve.drain()


def norm_block(dve, k, out, b):
    return dve.tensor_scalar(out, blk(k.xs, b), col(k.mean, b), col(k.rstd, b), ALU.subtract, ALU.mult)


class Maxima:

    def __init__(self, nc, ctx, name):
        self.masks = sb_of(nc, ctx)(f"{name}_masks", [128, NG, GB, GB * P], BF16)
        self.qmax = sb_of(nc, ctx)(f"{name}_qmax", [P, GB, P], F32)
        self.s_mask = [sem_of(nc, ctx)(f"{name}_mask{n}") for n in range(NG)]
        self.s_max = sem_of(nc, ctx)(f"{name}_max")


def piece(dram, g, n):
    src = dram[g * GB:(g + 1) * GB] if isinstance(g, int) else dram[bass.ds(g * GB, GB)]
    return src.rearrange("b p n -> p b n")[:, :, n * GB * P:(n + 1) * GB * P]


def stage_project(nc, k, name, mx, source, norm, w, bias, wq, wk, bq=None, bk=None):
    with ExitStack() as ctx:
        sb0, sem0 = sb_of(nc, ctx), sem_of(nc, ctx)
        sb = lambda n, s, d: sb0(f"{name}_{n}", s, d)
        sem = lambda n: sem0(f"{name}_{n}")
        wt = sb("w", [128, 2, D + 2], F32)
        brow = sb("bias", [P, D], F32)
        wqk = sb("wqk", [128, 2, D], F32)
        prod = sb("prod", [128, 2, 2, D], F32)
        bqk = sb("bqk", [P, 2], F32)
        base = sb("base", [P, 2], F32)
        shift = sb("shift", [P, NB], F32)
        xin = sb("xin", [P, GB, D], F32)
        xt = sb("xt", [128, GB, 2, P], F32)
        qk = sb("qk", [P, NB, 2], F32)
        s_w, s_x, s_tr, s_xt, s_y, s_h, s_var, s_root, s_wt, s_shift, s_q, s_seen = (sem(x) for x in (
            "w", "x", "tr", "xt", "y", "h", "var", "root", "wt", "shift", "q", "seen"))
        ps_t = [k.ps[:, m, 0:2 * P].rearrange("p (h n) -> p h n", h=2) for m in range(3)]
        ps_y = [k.ps[0:P, 3 + m, 0:D + 2] for m in range(3)]
        loads = 3 + (bias is not None) + 2 * (bq is not None)
        with nc.Block() as block:
            @block.sync
            def _(sp):
                sp.dma_start(wt[:, :, 0:D], w.rearrange("(h p) n -> p h n", h=2)).then_inc(s_w, 16)
                sp.dma_start(wqk[:, 0, :], row_bcast(wq, 128, D)).then_inc(s_w, 16)
                sp.dma_start(wqk[:, 1, :], row_bcast(wk, 128, D)).then_inc(s_w, 16)
                if bias is not None:
                    sp.dma_start(brow[:], row_bcast(bias, P, D)).then_inc(s_w, 16)
                if bq is not None:
                    sp.dma_start(bqk[:, 0:1], row_bcast(bq, P, 1)).then_inc(s_w, 16)
                    sp.dma_start(bqk[:, 1:2], row_bcast(bk, P, 1)).then_inc(s_w, 16)
                for n in range(NG):
                    sp.dma_start(mx.masks[:, n], piece(k.m_dram, 0, n)).then_inc(mx.s_mask[n], 16)

            @block.scalar
            def _(act):
                if norm:
                    act.wait_ge(s_var, 1)
                    act.activation(k.rstd[:], k.rstd[:], ACT.Sqrt).then_inc(s_root, 1)

                    act.wait_ge(s_shift, 1)

                def step(s, i):
                    if at(s, 0):
                        act.wait_ge(s_tr, s + 1)
                        act.copy(xt[:, i], ps_t[BANK3[i]]).then_inc(s_xt, 1)
                        if norm:
                            act.wait_ge(s_x, s + 1)
                            act.sem_inc(s_seen, 1)
                            act.activation(blk(k.xs, s), blk(k.xs, s), ACT.Identity, bias=col(shift, s),
                                           scale=col(k.rstd, s))
                    if bias is None and at(s, 2):
                        b = s - 2
                        act.wait_ge(s_q, b + 1)
                        act.sem_inc(s_seen, 1)
                        act.copy(blk(k.h, b)[:, 0:D], ps_y[BANK3[slot(s, 2, i)]][:, 0:D]).then_inc(s_h, 1)

                in_steps(act, step, 2)

            @block.tensor
            def _(pe):
                pe.wait_ge(s_wt, 1)

                def step(s, i):
                    if at(s, 0):
                        pe.wait_ge(s_x, s + 1)
                        for h in range(2):
                            tr = pe.transpose(ps_t[BANK3[i]][:, h, :], xin[:, i, h * 128:(h + 1) * 128],
                                              k.ident[0:P, 0:P])
                        tr.then_inc(s_tr, 1)
                    if at(s, 1):
                        j = slot(s, 1, i)
                        pe.wait_ge(s_xt, s)
                        if not isinstance(s, int) or s >= 3:
                            pe.wait_ge(s_h, s - 2)
                        for h in range(2):
                            mm = pe.matmul(ps_y[BANK3[j]], xt[:, j, h, :], wt[:, h, :], start=(h == 0), stop=(h == 1))
                        mm.then_inc(s_y, 1)

                in_steps(pe, step, 1)

            @block.vector
            def _(dve):
                dve.memset(k.h[:, :, D:D + 1], 1.0)
                if norm:
                    norm_factors(dve, k, s_var, s_root)
                dve.wait_ge(s_w, 16 * loads)
                for v in range(2):
                    for h in range(2):
                        dve.tensor_tensor(prod[:, v, h, :], wt[:, h, 0:D], wqk[:, v, :], ALU.mult)
                dve.drain()
                for v in range(2):
                    dve.tensor_reduce(wt[:, :, D + v], prod[:, v], AX.X, ALU.add)
                dve.drain().then_inc(s_wt, 1)
                if norm:
                    dve.scalar_tensor_tensor(shift[:], k.mean[:], -1.0, k.rstd[:], ALU.mult, ALU.mult)
                    dve.drain().then_inc(s_shift, 1)
                if bias is not None:
                    for v in range(2):
                        dve.tensor_tensor(prod[0:P, v, 0, :], brow[:], wqk[0:P, v, :], ALU.mult)
                    dve.drain()
                    dve.tensor_reduce(base[:], prod[0:P, :, 0, :], AX.X, ALU.add)
                else:
                    dve.memset(base[:], 0.0)
                if bq is not None:
                    dve.drain()
                    dve.tensor_tensor(base[:], base[:], bqk[:], ALU.add)
                dve.drain()

                def step(s, i, it=None):
                    if at(s, 0):
                        if not isinstance(s, int) or s >= GB:
                            dve.wait_ge(s_tr, s - GB + 1)
                        if norm:
                            norm_block(dve, k, xin[:, i, :], s).then_inc(s_x, 1)
                        else:
                            dve.tensor_scalar(xin[:, i, :], blk(source, s), 1.0, None, ALU.mult).then_inc(s_x, 1)
                    if at(s, 2):
                        b = s - 2
                        y = ps_y[BANK3[slot(s, 2, i)]]
                        dve.wait_ge(s_y, s - 1)
                        dve.scalar_tensor_tensor(blk(qk, b), y[:, D:D + 2], 1.0, base[:], ALU.mult,
                                                 ALU.add).then_inc(s_q, 1)
                        if bias is not None:
                            dve.tensor_tensor(blk(k.h, b)[:, 0:D], y[:, 0:D], brow[:], ALU.add).then_inc(s_h, 1)
                    if at(s, GB):
                        c = s - GB
                        if isinstance(s, int):
                            dve.wait_ge(mx.s_mask[c // GB], 16)
                            mask = mx.masks[0:P, c // GB, :, i * P:(i + 1) * P]
                            q = qk[:, c, 0:1]
                        else:
                            mask = mx.masks[0:P, bass.ds(it - 1, 1), :, i * P:(i + 1) * P].rearrange(
                                "p a j n -> p (a j) n")
                            q = qk[:, bass.ds(c, 1), 0]
                        dve.wait_ge(s_q, c + 1)
                        dve.wait_ge(mx.s_max, c + 1)
                        dve.scalar_tensor_tensor(mx.qmax[:], mask, q, mx.qmax[:], ALU.add,
                                                 ALU.max).then_inc(mx.s_max, 1)

                dve.memset(mx.qmax[:], -BIG)
                dve.drain().then_inc(mx.s_max, 1)
                for i in range(GB):
                    step(i, i)
                for n in range(NG):
                    dve.wait_ge(mx.s_mask[n], 16)
                with dve.Fori(1, NG) as it:
                    for i in range(GB):
                        step(it * GB + i, i, it)
                for i in range(GB):
                    step(NB + i, i)
                dve.drain()
                for v, out in enumerate((k.q, k.kk)):
                    dve.tensor_copy(out[:], qk[:, :, v])
                dve.drain()
                dve.tensor_scalar(k.q_slope[:], k.q[:], SLOPE, None, ALU.mult)


def stage_norm_split(nc, k, name, ring, parts):
    with ExitStack() as ctx:
        sem = lambda n: sem_of(nc, ctx)(f"{name}_{n}")
        g = sb_of(nc, ctx)(f"{name}_g", [P, 2, GB, D], F32)
        s_var, s_root, s_x, s_g, s_hi, s_lo = (sem(x) for x in ("var", "root", "x", "g", "hi", "lo"))
        with nc.Block() as block:
            @block.sync
            def _(sp):
                for i in range(GB):
                    ring.load(sp, k, i, i)

            @block.scalar
            def _(act):
                act.wait_ge(s_var, 1)
                act.activation(k.rstd[:], k.rstd[:], ACT.Sqrt).then_inc(s_root, 1)
                for n in range(NG):
                    x, out = groups_of(k.xs)[n], groups_of(parts)[n]
                    act.wait_ge(s_x, n + 1)
                    act.copy(out[:, :, 0:D], x).then_inc(s_hi, 1)
                    if n >= 2:
                        act.wait_ge(s_lo, n - 1)
                    act.mul(g[:, n % 2], x, LO).then_inc(s_g, 1)

            @block.vector
            def _(dve):
                norm_factors(dve, k, s_var, s_root)
                for n in range(NG + 1):
                    if n < NG:
                        for b in range(n * GB, (n + 1) * GB):
                            norm_block(dve, k, blk(k.xs, b), b)
                        dve.drain().then_inc(s_x, 1)
                    if n >= 1:
                        out = groups_of(parts)[n - 1]
                        dve.wait_ge(s_hi, n)
                        dve.wait_ge(s_g, n)
                        dve.scalar_tensor_tensor(out[:, :, D:2 * D], out[:, :, 0:D], -LO, g[:, (n - 1) % 2],
                                                 ALU.mult, ALU.add).then_inc(s_lo, 1)


def stage_attention(nc, k, name, mx, finish, bias=None):
    GW = GB * P
    AHEAD = 19
    E_SLOTS, P_SLOTS = 2, 3
    with ExitStack() as ctx:
        sb0, sem0 = sb_of(nc, ctx), sem_of(nc, ctx)
        sb = lambda n, s, d: sb0(f"{name}_{n}", s, d)
        sem = lambda n: sem0(f"{name}_{n}")
        counts = sb("counts", [128, NG, GB, GB * P], F16)
        masks, qmax, s_mask, s_max = mx.masks, mx.qmax, mx.s_mask, mx.s_max
        brow = sb("bias", [P, D], F32)
        top = sb("top", [P, GB], F32)
        tops = sb("tops", [P, GB], F32)
        rcol = sb("rcol", [P, 2, GB], F32)
        kslope = sb("kslope", [P, NB], F32)
        diag = sb("diag", [P, 2, GB, P], F32)
        ones = sb("ones", [P, P], F32)
        rrow = sb("rrow", [P, 2, GB, P], F32)
        e = sb("e", [P, E_SLOTS + 1, 2, GW], F32)
        x = sb("x", [P, 2, GB, P], F32)
        p = sb("p", [P, P_SLOTS + 1, GB, P], F32)
        den = sb("den", [P, GB], F32)
        t = sb("t", [P, GB, D], F32)
        s_cnt = [sem(f"cnt{n}") for n in range(NG)]
        s_w, s_qmax, s_tr, s_diag, s_bc, s_r, s_e, s_x, s_p, s_pv, s_out, s_set = (sem(v) for v in (
            "w", "qmax", "tr", "diag", "bc", "r", "e", "x", "p", "pv", "out", "set"))
        s_relu = sem("relu")
        s_seen = sem("seen")

        def spread(r):
            return (k.ps[0:P, 5 + 2 * r, 0:4 * P].rearrange("p (j n) -> p j n", j=4),
                    k.ps[0:P, 6, r * P:(r + 1) * P])

        def chunk(tile, c):
            return tile[0:P, c // GB, :, (c % GB) * P:(c % GB + 1) * P]

        def e_slot(c):
            return c % E_SLOTS if c < NB - 1 else E_SLOTS

        def p_slot(c):
            return c % P_SLOTS if c < NB - 1 else P_SLOTS

        def maxima(c):
            return range(NB * c // AHEAD, NB * (c + 1) // AHEAD) if c < AHEAD else ()

        def groups(eng, body):
            body(0, True, False)
            with eng.Fori(1, NG - 1) as g:
                body(g, False, False)
            body(NG - 1, False, True)

        with nc.Block() as block:
            @block.sync
            def _(sp):
                if bias is not None:
                    sp.dma_start(brow[:], row_bcast(bias, P, D)).then_inc(s_w, 16)
                for n in range(NG):
                    sp.dma_start(counts[:, n], piece(k.a_dram, 0, n)).then_inc(s_cnt[n], 16)
                for n in range(NG):
                    sp.dma_start(masks[:, n], piece(k.m_dram, 1, n)).then_inc(s_mask[n], 16)

                def body(g, last_mask):
                    for n in range(NG):
                        if not last_mask:
                            sp.wait_ge(s_max, g * NB + (NB + GB * (n + 1) + 1))
                            sp.dma_start(masks[:, n], piece(k.m_dram, g + 2, n)).then_inc(s_mask[n], 16)
                        sp.wait_ge(s_p, g * NB + GB * (n + 1))
                        sp.dma_start(counts[:, n], piece(k.a_dram, g + 1, n)).then_inc(s_cnt[n], 16)

                with sp.Fori(0, NG - 2) as g:
                    body(g, False)
                body(NG - 2, True)

            @block.scalar
            def _(act):
                act.preload_act_table(ACT.Exp)

                def relus(g):
                    for j in range(GB):
                        act.wait_ge(s_out, g * GB + (j + 1))
                        act.sem_inc(s_seen, 1)
                        act.activation(blk(k.y, g * GB + j), t[:, j, :], ACT.Relu).then_inc(s_relu, 1)

                def body(g, first, last):
                    act.wait_ge(s_bc, g + 1)
                    if not first:
                        act.wait_ge(s_e, g * NB)
                    for r in range(2):
                        many, one = spread(r)
                        act.copy(rrow[:, r, 0:4, :], many)
                        act.copy(rrow[:, r, 4, :], one)
                    act.drain().then_inc(s_r, 1)
                    for c in range(NB):
                        if not (first and c < E_SLOTS):
                            act.wait_ge(s_x, g * NB + (c - E_SLOTS + 1))
                        m = e_slot(c)
                        act.activation(e[:, m, 0, :], rrow[:, 0].rearrange("p j n -> p (j n)"), ACT.Exp,
                                       bias=k.q[:, c:c + 1])
                        act.activation(e[:, m, 1, :], rrow[:, 1].rearrange("p j n -> p (j n)"), ACT.Exp,
                                       bias=k.q_slope[:, c:c + 1]).then_inc(s_e, 1)
                        if c == 2 and not first and finish == "relu":
                            relus(g - 1)

                if finish == "relu":
                    act.sem_inc(s_relu, GB)
                groups(act, body)
                if finish == "relu":
                    relus(NG - 1)

            @block.vector
            def _(dve):
                dve.memset(ones[:], 1.0)
                dve.tensor_scalar(kslope[:], k.kk[:], SLOPE, None, ALU.mult)
                if bias is not None:
                    dve.wait_ge(s_w, 16)
                dve.drain().then_inc(s_set, 1)

                def greatest(g, c):
                    if c % GB == 0:
                        dve.wait_ge(s_mask[c // GB], g * 16 + 16)
                    if c == 0:
                        dve.tensor_scalar(qmax[:], chunk(masks, c), k.q[:, c:c + 1], None, ALU.add).then_inc(s_max, 1)
                    else:
                        dve.wait_ge(s_max, g * NB + (c + 1))
                        dve.scalar_tensor_tensor(qmax[:], chunk(masks, c), k.q[:, c:c + 1], qmax[:], ALU.add,
                                                 ALU.max).then_inc(s_max, 1)

                def of_group(tile, g):
                    return tile[:, g * GB:(g + 1) * GB] if isinstance(g, int) else tile[:, bass.ds(g * GB, GB)]

                def limits(g):
                    dve.wait_ge(s_tr, g + 1)
                    many, one = spread(0)
                    dve.tensor_reduce(top[:, 0:4], many, AX.X, ALU.max)
                    dve.tensor_reduce(top[:, 4:5], one, AX.X, ALU.max)
                    dve.drain()
                    dve.tensor_tensor(top[:], top[:], of_group(k.kk, g), ALU.add)
                    dve.drain()
                    dve.tensor_scalar(tops[:], top[:], SLOPE, None, ALU.mult)
                    dve.drain()
                    dve.tensor_tensor(top[:], top[:], tops[:], ALU.max)
                    dve.drain()
                    dve.tensor_tensor(rcol[:, 0, :], of_group(k.kk, g), top[:], ALU.subtract)
                    dve.tensor_tensor(rcol[:, 1, :], of_group(kslope, g), top[:], ALU.subtract)
                    dve.drain()
                    for r in range(2):
                        dve.tensor_tensor(diag[:, r], k.ident[0:P, 0:P].unsqueeze(1).to_broadcast([P, GB, P]),
                                          rcol[:, r, :].unsqueeze(2).to_broadcast([P, GB, P]),
                                          ALU.mult).then_inc(s_diag, 1)

                def take(g):
                    dve.wait_ge(s_pv, g * NB + NB)
                    dve.tensor_scalar(den[:], k.ps[0:P, 0:GB, D], 1e-30, None, ALU.max)
                    dve.drain()
                    dve.reciprocal(den[:], den[:])
                    dve.drain()
                    if finish == "relu":
                        dve.wait_ge(s_relu, g * GB + GB)
                    for j in range(GB):
                        x_blk = blk(k.xs, g * GB + j)
                        dve.scalar_tensor_tensor(x_blk if finish == "res" else t[:, j, :], k.ps[0:P, j, 0:D],
                                                 den[:, j:j + 1], x_blk if finish == "res" else brow[:], ALU.mult,
                                                 ALU.add).then_inc(s_out, 1)

                def settle(g, j):
                    b = g * GB + j
                    if j == 0:
                        dve.drain()
                    if finish == "relu":
                        return
                    if finish == "both":
                        dve.scalar_tensor_tensor(blk(k.xs, b), t[:, j, :], 0.0, blk(k.xs, b), ALU.max, ALU.add)
                        dve.drain()
                    dve.bn_stats(blk(k.stats, b), blk(k.xs, b))

                def body(g, first, last):
                    for c in range(NB):
                        dve.wait_ge(s_e, g * NB + (c + 1))
                        m = e_slot(c)
                        if c == 0 and not first:
                            dve.wait_ge(s_p, g * NB)
                        if c >= 2:
                            dve.wait_ge(s_p, g * NB + (c - 1))
                        dve.tensor_tensor(x[:, c % 2].rearrange("p j n -> p (j n)"), e[:, m, 0, :], e[:, m, 1, :],
                                          ALU.max).then_inc(s_x, 1)
                        if not last:
                            for n in maxima(c):
                                greatest(g + 1, n)
                        if c % GB == 0:
                            dve.wait_ge(s_cnt[c // GB], g * 16 + 16)
                        if not (first and c < P_SLOTS):
                            dve.wait_ge(s_pv, g * NB + (c - P_SLOTS + 1))
                        if c == 1 and not first:
                            take(g - 1)
                        dve.wait_ge(s_x, g * NB + (c + 1))
                        dve.scalar_tensor_tensor(p[:, p_slot(c)], x[:, c % 2], 1.0, chunk(counts, c), ALU.min,
                                                 ALU.mult).then_inc(s_p, 1)
                        if 2 <= c < 2 + GB and not first:
                            settle(g - 1, c - 2)
                        if c == AHEAD - 1 and not last:
                            dve.drain().then_inc(s_qmax, 1)
                        if c == AHEAD + 2 and not last:
                            limits(g + 1)

                dve.drain().then_inc(s_qmax, 1)
                limits(0)
                groups(dve, body)
                take(NG - 1)
                for j in range(GB):
                    settle(NG - 1, j)

            @block.tensor
            def _(pe):
                pe.wait_ge(s_set, 1)

                def turn(g):
                    pe.wait_ge(s_qmax, g + 1)
                    if not isinstance(g, int) or g >= 1:
                        pe.wait_ge(s_r, g)
                    many, one = spread(0)
                    for j in range(GB):
                        tr = pe.transpose(many[:, j, :] if j < 4 else one, qmax[:, j, :], k.ident[0:P, 0:P])
                    tr.then_inc(s_tr, 1)

                def rows(g):
                    for r in range(2):
                        pe.wait_ge(s_diag, g * 2 + (r + 1))
                        many, one = spread(r)
                        pe.matmul(many, ones[:], diag[:, r, 0:4, :], start=True, stop=True, skip_group_check=True)
                        mm = pe.matmul(one, ones[:], diag[:, r, 4, :], start=True, stop=True, skip_group_check=True)
                    mm.then_inc(s_bc, 1)

                def body(g, first, last):
                    for c in range(NB):
                        pe.wait_ge(s_p, g * NB + (c + 1))
                        for j in range(GB):
                            if c == 0 and not first:
                                pe.wait_ge(s_out, (g - 1) * GB + (j + 1))
                            mm = pe.matmul(k.ps[0:P, j, 0:D + 1], p[:, p_slot(c), j, :], k.h[:, c, :],
                                           start=(c == 0), stop=(c == NB - 1))
                        mm.then_inc(s_pv, 1)
                        if c == AHEAD and not last:
                            turn(g + 1)
                        if c == AHEAD + 2 and not last:
                            rows(g + 1)

                turn(0)
                rows(0)
                groups(pe, body)


def stage_mlp(nc, k, w):
    KH = HID // 128
    US, WS = 16.0, 64.0
    W2_SLOTS = 4
    with ExitStack() as ctx:
        sb, sem = sb_of(nc, ctx), sem_of(nc, ctx)
        w1 = sb("m_w1", [128, 2, HID], F32)
        w2_in = sb("m_w2_in", [128, W2_SLOTS, HID], F32)
        w2_hi = sb("m_w2_hi", [128, KH, HID], F16)
        w2_lo = sb("m_w2_lo", [128, KH, HID], F16)
        w3 = sb("m_w3", [128, KH, D], F32)
        rows = sb("m_rows", [P, 2, HID], F32)
        rows3 = sb("m_rows3", [P, 3, D], F32)
        cols = sb("m_cols", [128, 4, KH], F32)
        hin = sb("m_hin", [P, D], F32)
        ht = sb("m_ht", [128, 2, P], F32)
        u = sb("m_u", [P, 2, HID], F32)
        un = sb("m_un", [P, 2, HID], F32)
        ut = sb("m_ut", [128, 2, KH, P], F32)
        ut_hi = sb("m_ut_hi", [128, KH, P], F16)
        ut_lo = sb("m_ut_lo", [128, KH, P], F16)
        st = sb("m_st", [P, 2, 2, 6], F32)
        mv = sb("m_mv", [P, 3, 2], F32)
        rs = sb("m_rs", [P, 3, 2], F32)
        r3 = sb("m_r3", [P, D], F32)
        st3 = sb("m_st3", [P, 6], F32)
        s_w, s_in, s_tr0, s_ht = sem("m_w"), sem("m_in"), sem("m_tr0"), sem("m_ht")
        s_mm = [sem("m_mm1"), sem("m_mm2"), sem("m_mm3")]
        s_var = [sem("m_var1"), sem("m_var2"), sem("m_var3")]
        s_root = [sem("m_root1"), sem("m_root2"), sem("m_root3")]
        s_scale = [sem("m_scale1"), sem("m_scale2")]
        s_un = [sem("m_un1"), sem("m_un2")]
        s_tr = [sem("m_tr1"), sem("m_tr2")]
        s_ut = [sem("m_ut1"), sem("m_ut2")]
        s_uhi, s_ulo = sem("m_uhi"), sem("m_ulo")
        s_win = [sem(f"m_win{n}") for n in range(W2_SLOTS)]
        s_w1, s_w3 = sem("m_w1"), sem("m_w3")
        s_whi, s_wlo, s_cols = sem("m_whi"), sem("m_wlo"), sem("m_cols")
        s_read = [sem("m_read1"), sem("m_read2"), sem("m_read3")]
        ps_h = k.ps[:, 0, 0:2 * P].rearrange("p (h n) -> p h n", h=2)
        ps_m = [k.ps[0:P, 1:3, :], k.ps[0:P, 3:5, :]]
        ps_3 = k.ps[0:P, 7, 0:D]
        ps_u = k.ps[:, 5:7, 0:4 * P].rearrange("p m (c n) -> p m c n", c=4)
        loops = sb("loops", [P, NB, P], F16)
        loops_open = sb("loops_open", [P, NB, P], BF16)
        others = sb("others", [P, P], BF16)
        s_lin, s_ladd, s_lout = sem("l_in"), sem("l_add"), sem("l_out")
        with nc.Block() as block:
            @block.gpsimd
            def _(pool):
                pool.memset(others[:], 1.0)
                pool.drain()
                pool.affine_select(out=others[:], in_=others[:], compare_op=ALU.not_equal, fill=0.0, base=0,
                                   pattern=[[-1, P]], channel_multiplier=1)
                pool.drain()
                pool.wait_ge(s_lin, 32 * NB)
                pool.tensor_tensor(loops[:], loops[:], k.ident16[:].unsqueeze(1).to_broadcast([P, NB, P]), ALU.add)
                pool.tensor_tensor(loops_open[:], loops_open[:], others[:].unsqueeze(1).to_broadcast([P, NB, P]),
                                   ALU.mult)
                pool.drain().then_inc(s_ladd, 1)

            @block.sync
            def _(sp):
                sp.dma_start(w1[:], w["w1"].rearrange("(c p) n -> p c n", p=128)).then_inc(s_w1, 16)
                w2_rows = w["w2"].rearrange("(c p) n -> p c n", p=128)
                for n, v in enumerate(("b1", "b2")):
                    sp.dma_start(rows[:, n, :], row_bcast(w[v], P, HID)).then_inc(s_w, 16)
                for n, v in enumerate(("b3", "bn_g", "bn_b")):
                    sp.dma_start(rows3[:, n, :], row_bcast(w[v], P, D)).then_inc(s_w, 16)
                for n, v in enumerate(("g1", "be1", "g2", "be2")):
                    with nc.allow_non_contiguous_dma(reason="4 vectors of 1024"):
                        sp.dma_start(cols[:, n, :], w[v].rearrange("(c p) -> p c", p=128)).then_inc(s_w, 16)
                for c in range(KH):
                    if c >= W2_SLOTS:
                        sp.wait_ge(s_wlo, c - W2_SLOTS + 1)
                    sp.dma_start(w2_in[:, c % W2_SLOTS], w2_rows[:, c]).then_inc(s_win[c % W2_SLOTS], 16)
                sp.dma_start(w3[:], w["w3"].rearrange("(c p) n -> p c n", p=128)).then_inc(s_w3, 16)
                for b in range(NB):
                    sp.dma_start(loops[:, b, :], k.a_dram[b, 0:P, b * P:(b + 1) * P]).then_inc(s_lin, 16)
                    sp.dma_start(loops_open[:, b, :], k.m_dram[b, 0:P, b * P:(b + 1) * P]).then_inc(s_lin, 16)
                sp.wait_ge(s_ladd, 1)
                for b in range(NB):
                    sp.dma_start(k.a_dram[b, 0:P, b * P:(b + 1) * P], loops[:, b, :]).then_inc(s_lout, 16)
                    sp.dma_start(k.m_dram[b, 0:P, b * P:(b + 1) * P], loops_open[:, b, :]).then_inc(s_lout, 16)
                sp.wait_ge(s_lout, 32 * NB)

            def blocks(eng, before, part):
                before()
                part(0, True, False)
                part(1, False, False)
                with eng.Fori(2, NB - 2) as b:
                    part(b, False, False)
                part(NB - 2, False, False)
                part(NB - 1, False, True)

            @block.tensor
            def _(pe):
                pe.wait_ge(s_w1, 16)

                def turn_input(b):
                    pe.wait_ge(s_in, b + 1)
                    for h in range(2):
                        tr = pe.transpose(ps_h[:, h, :], hin[:, h * 128:(h + 1) * 128], k.ident[0:P, 0:P])
                    tr.then_inc(s_tr0, 1)

                def first(b, begin=False):
                    pe.wait_ge(s_ht, b + 1)
                    if not begin:
                        pe.wait_ge(s_read[0], b)
                    for n in range(2):
                        for c in range(2):
                            mm = pe.matmul(ps_m[0][:, n, :], ht[:, c, :], w1[:, c, n * 512:(n + 1) * 512],
                                           start=(c == 0), stop=(c == 1))
                    mm.then_inc(s_mm[0], 1)

                def turn(l, b):
                    pe.wait_ge(s_un[l], b + 1)
                    for c in range(KH):
                        tr = pe.transpose(ps_u[:, c // 4, c % 4, :], un[:, l, c * 128:(c + 1) * 128], k.ident[0:P, 0:P])
                        if c % 4 == 3:
                            tr.then_inc(s_tr[l], 1)

                def second_high(b, n):
                    for c in range(KH):
                        if n == 0:
                            pe.wait_ge(s_uhi, b * KH + (c + 1))
                        for part_w in (w2_hi, w2_lo):
                            pe.matmul(ps_m[1][:, n, :], ut_hi[:, c, :], part_w[:, c, n * 512:(n + 1) * 512],
                                      start=(c == 0 and part_w is w2_hi), stop=False, skip_group_check=True)

                def second_low(b, n):
                    for c in range(KH):
                        if n == 0 and c % 4 == 0:
                            pe.wait_ge(s_ulo, b * 2 + (c // 4 + 1))
                        mm = pe.matmul(ps_m[1][:, n, :], ut_lo[:, c, :], w2_hi[:, c, n * 512:(n + 1) * 512],
                                       start=False, stop=(c == KH - 1), skip_group_check=True)
                    mm.then_inc(s_mm[1], 1)

                def third(b):
                    for c in range(KH):
                        pe.wait_ge(s_ut[1], b * KH + (c + 1))
                        mm = pe.matmul(ps_3, ut[:, 1, c, :], w3[:, c, :], start=(c == 0), stop=(c == KH - 1))
                    mm.then_inc(s_mm[2], 1)

                def before():
                    turn_input(0)
                    first(0, begin=True)
                    pe.wait_ge(s_wlo, KH)
                    pe.wait_ge(s_w3, 16)

                def part(b, begin, end):
                    if not isinstance(b, int) or b >= 2:
                        pe.wait_ge(s_ut[1], (b - 1) * KH)
                    turn(0, b)
                    if not end:
                        turn_input(b + 1)
                    if not begin:
                        pe.wait_ge(s_read[1], b * 2 - 1)
                    second_high(b, 0)
                    if not end:
                        first(b + 1)
                    second_low(b, 0)
                    if not begin:
                        pe.wait_ge(s_ut[0], b * KH + KH)
                        turn(1, b - 1)
                        if not isinstance(b, int) or b >= 2:
                            pe.wait_ge(s_read[2], b - 1)
                        third(b - 1)
                        pe.wait_ge(s_read[1], b * 2)
                    second_high(b, 1)
                    second_low(b, 1)

                blocks(pe, before, part)
                turn(1, NB - 1)
                pe.wait_ge(s_read[2], NB - 1)
                third(NB - 1)

            @block.scalar
            def _(act):
                act.preload_act_table(ACT.Sqrt)

                def head(b):
                    act.wait_ge(s_tr0, b + 1)
                    act.copy(ht[:], ps_h).then_inc(s_ht, 1)

                def root(l, b):
                    act.wait_ge(s_var[l], b + 1)
                    act.activation(rs[:, l, 0:1], rs[:, l, 0:1], ACT.Sqrt).then_inc(s_root[l], 1)

                def normalise(l, b):
                    act.wait_ge(s_scale[l], b + 1)
                    act.activation(un[:, l, :], u[:, l, :], ACT.Identity, bias=rs[:, l, 1:2],
                                   scale=rs[:, l, 0:1]).then_inc(s_un[l], 1)

                def turned(l, b, high=False):
                    for c in range(KH):
                        if c % 4 == 0:
                            act.wait_ge(s_tr[l], b * 2 + (c // 4 + 1))
                        act.activation(ut_hi[:, c, :] if high else ut[:, l, c, :], ps_u[:, c // 4, c % 4, :], ACT.Relu,
                                       bias=cols[:, 2 * l + 1, c:c + 1],
                                       scale=cols[:, 2 * l, c:c + 1]).then_inc(s_uhi if high else s_ut[l], 1)

                def before():
                    head(0)
                    root(0, 0)
                    normalise(0, 0)
                    for c in range(KH):
                        act.wait_ge(s_win[c % W2_SLOTS], 16 * (c // W2_SLOTS + 1))
                        act.mul(w2_hi[:, c], w2_in[:, c % W2_SLOTS], WS).then_inc(s_whi, 1)
                    act.wait_ge(s_cols, 1)

                def part(b, begin, end):
                    if not begin:
                        act.wait_ge(s_mm[1], b * 2)
                    turned(0, b, high=True)
                    if not begin:
                        root(1, b - 1)
                    if not end:
                        head(b + 1)
                    turned(0, b)
                    if not begin:
                        normalise(1, b - 1)
                        if not isinstance(b, int) or b >= 2:
                            act.wait_ge(s_mm[2], b - 1)
                        turned(1, b - 1)
                    if not end:
                        root(0, b + 1)
                        normalise(0, b + 1)
                    if not begin:
                        root(2, b - 1)

                blocks(act, before, part)
                root(1, NB - 1)
                normalise(1, NB - 1)
                act.wait_ge(s_mm[2], NB - 1)
                turned(1, NB - 1)
                root(2, NB - 1)

            @block.vector
            def _(dve):

                def scales(l, b):
                    dve.bn_aggr(mv[:, l, :], st[:, l] if l < 2 else st3[:])
                    dve.drain()
                    dve.tensor_scalar(rs[:, l, 0:1], mv[:, l, 1:2], LN_EPS, None, ALU.add).then_inc(s_var[l], 1)
                    dve.wait_ge(s_root[l], b + 1)
                    dve.reciprocal(rs[:, l, 0:1], rs[:, l, 0:1])
                    dve.drain()

                def add_bias(l, b, halves, begin=False):
                    many = len(halves)
                    if l == 0:
                        dve.wait_ge(s_mm[0], b + 1)
                    else:
                        dve.wait_ge(s_mm[1], b * 2 + (halves[-1] + 1))
                    if not begin:
                        dve.wait_ge(s_un[l], b)
                    part = slice(halves[0] * 512, (halves[-1] + 1) * 512)
                    dve.scalar_tensor_tensor(u[:, l, part].rearrange("p (m n) -> p m n", m=many),
                                             ps_m[l][:, halves[0]:halves[-1] + 1],
                                             1.0 / (US * WS) if l == 1 else 1.0,
                                             rows[:, l, part].rearrange("p (m n) -> p m n", m=many), ALU.mult,
                                             ALU.add).then_inc(s_read[l], 1)
                    dve.drain()
                    for m in halves:
                        dve.bn_stats(st[:, l, m, :], u[:, l, m * 512:(m + 1) * 512])

                def factors(l, b):
                    dve.drain()
                    scales(l, b)
                    dve.scalar_tensor_tensor(rs[:, l, 1:2], mv[:, l, 0:1], -1.0, rs[:, l, 0:1], ALU.mult,
                                             ALU.mult).then_inc(s_scale[l], 1)

                def bring(b, begin=False):
                    if not begin:
                        dve.wait_ge(s_tr0, b)
                    dve.tensor_scalar(hin[:], blk(k.y, b), 1.0, None, ALU.mult).then_inc(s_in, 1)

                def out(b):
                    dve.wait_ge(s_mm[2], b + 1)
                    dve.tensor_tensor(r3[:], ps_3, rows3[:, 0, :], ALU.add).then_inc(s_read[2], 1)
                    dve.drain()
                    dve.tensor_tensor(r3[:], r3[:], blk(k.xs, b), ALU.add)
                    dve.drain()
                    dve.bn_stats(st3[:], r3[:])
                    dve.drain()
                    scales(2, b)
                    dve.tensor_scalar(r3[:], r3[:], mv[:, 2, 0:1], rs[:, 2, 0:1], ALU.subtract, ALU.mult)
                    dve.drain()
                    dve.tensor_tensor(r3[:], r3[:], rows3[:, 1, :], ALU.mult)
                    dve.drain()
                    dve.tensor_tensor(r3[:], r3[:], rows3[:, 2, :], ALU.add)
                    dve.drain()
                    dve.scalar_tensor_tensor(blk(k.xs, b), r3[:], 0.0, blk(k.xs, b), ALU.max, ALU.add)
                    dve.drain()
                    dve.bn_stats(blk(k.stats, b), blk(k.xs, b))
                    dve.drain()

                def low(b):
                    for m in range(2):
                        half = slice(m * 4, (m + 1) * 4)
                        dve.wait_ge(s_ut[0], b * KH + 4 * (m + 1))
                        dve.tensor_tensor(ut_lo[:, half], ut[:, 0, half], ut_hi[:, half],
                                          ALU.subtract).then_inc(s_ulo, 1)

                def before():
                    bring(0, begin=True)
                    dve.wait_ge(s_w, 16 * 9)
                    dve.tensor_scalar(cols[:, 0:2], cols[:, 0:2], US, None, ALU.mult).then_inc(s_cols, 1)
                    add_bias(0, 0, (0, 1), begin=True)
                    factors(0, 0)
                    bring(1)
                    for c in range(KH):
                        dve.wait_ge(s_whi, c + 1)
                        dve.scalar_tensor_tensor(w2_lo[:, c], w2_in[:, c % W2_SLOTS], WS, w2_hi[:, c], ALU.mult,
                                                 ALU.subtract).then_inc(s_wlo, 1)

                def part(b, begin, end):
                    if not begin:
                        add_bias(1, b - 1, (1,), begin=True)
                        factors(1, b - 1)
                    low(b)
                    if not end:
                        add_bias(0, b + 1, (0, 1))
                        factors(0, b + 1)
                        if not isinstance(b, int) or b + 2 < NB:
                            bring(b + 2)
                    add_bias(1, b, (0,), begin=begin)
                    if not begin:
                        out(b - 1)

                blocks(dve, before, part)
                add_bias(1, NB - 1, (1,), begin=True)
                factors(1, NB - 1)
                out(NB - 1)


def stage_last(nc, k, out):
    with ExitStack() as ctx:
        sem = sem_of(nc, ctx)
        s_var, s_root, s_norm, s_store = sem("o_var"), sem("o_root"), sem("o_norm"), sem("o_store")
        rows = out.rearrange("(b p) d -> p b d", p=P)
        with nc.Block() as block:
            @block.scalar
            def _(act):
                act.wait_ge(s_var, 1)
                act.activation(k.rstd[:], k.rstd[:], ACT.Sqrt).then_inc(s_root, 1)

            @block.vector
            def _(dve):
                norm_factors(dve, k, s_var, s_root)
                for n in range(NG):
                    for b in range(n * GB, (n + 1) * GB):
                        norm_block(dve, k, blk(k.xs, b), b)
                    dve.drain().then_inc(s_norm, 1)

            @block.sync
            def _(sp):
                for n in range(NG):
                    sp.wait_ge(s_norm, n + 1)
                    sp.dma_start(rows[:, n * GB:(n + 1) * GB], groups_of(k.xs)[n]).then_inc(s_store, 16)
                sp.wait_ge(s_store, 16 * NG)


def program(nc, ins, outs):
    TAKEN.clear()
    with ExitStack() as ctx:
        sb = sb_of(nc, ctx)
        k = Core()
        k.ps = ctx.enter_context(nc.psum_tensor("ps", [128, 8, 512], F32))
        k.ident = sb("ident", [128, 128], F32)
        k.ident16 = sb("ident16", [P, P], F16)
        k.windows = sb("windows", [1, 2 * (NB + 1)], I32)
        k.deg, k.deg1, k.dinv, k.dinv_lo, k.rstd, k.mean, k.q, k.kk, k.q_slope = (sb(v, [P, NB], F32) for v in (
            "deg", "deg1", "dinv", "dinv_lo", "rstd", "mean", "q", "kk", "q_slope"))
        k.xs = sb("xs", [P, NB, D], F32)
        k.stats = sb("stats", [P, NB, 6], F32)
        k.mv = sb("mv", [P, NB, 2], F32)
        k.windows_dram = nc.dram_tensor("windows_dram", (NB, 2), I32).ap()
        k.a_dram = nc.dram_tensor("a_dram", (NB, 128, N), F16).ap()
        k.m_dram = nc.dram_tensor("m_dram", (NB, 128, N), BF16).ap()
        k.e_dram = nc.dram_tensor("e_dram", (NB, P, D), F32).ap()
        with ExitStack() as early:
            sbe = sb_of(nc, early)
            k.src_iota = sbe("src_iota", [128, NB, PAD], F16)
            k.dst_iota = sbe("dst_iota", [128, P], F32)
            stage_windows(nc, k, ins["dst"])
            stage_edges(nc, k, ins["srcT"], ins["dstT"], ins["eaT"], ins["L2_gnn_ee_w1"],
                        ins["L2_gnn_ee_b1"], ins["x"])
        with ExitStack() as gcn:
            sbg = sb_of(nc, gcn)
            pa, pb = sbg("parts_a", [P, NB, 2 * D], F16), sbg("parts_b", [P, NB, 2 * D], F16)
            ring = Ring(nc, gcn, "a_ring")
            stage_first_split(nc, k, ring, pa)
            stage_aggregate(nc, k, "g1", ring, False, pa, "gcn", ins["W1T"], ins["L0_gnn_b1"], out_parts=pb)
            stage_aggregate(nc, k, "g2", ring, False, pb, "gcn", ins["W2T"], ins["L0_gnn_b2"], out_parts=pa)
            stage_aggregate(nc, k, "g3", ring, True, pa, "last", ins["W3T"], ins["L0_gnn_b3"])
        recycle(nc)
        with ExitStack() as att:
            k.h = sb_of(nc, att)("h_att", [P, NB, D + 1], F32)
            mx = Maxima(nc, att, "m1")
            stage_project(nc, k, "p1", mx, k.xs, True, ins["L1_gnn_Wv"], ins["L1_gnn_bv"], ins["L1_gnn_wq"],
                          ins["L1_gnn_wk"], ins["L1_gnn_bq"], ins["L1_gnn_bk"])
            stage_attention(nc, k, "t1", mx, "res")
        k.y = sb("y", [P, NB, D], F32)
        with ExitStack() as gin:
            pa = sb_of(nc, gin)("parts_c", [P, NB, 2 * D], F16)
            ring = Ring(nc, gin, "a_ring2")
            stage_norm_split(nc, k, "p2", ring, pa)
            stage_aggregate(nc, k, "gi", ring, True, pa, "gin", ins["L2_gnn_ee_w2"], ins["L2_gnn_ee_b2"],
                            rb1=ins["L2_gnn_ee_b1"], eps=ins["L2_gnn_eps"])
        stage_mlp(nc, k, {v: ins["L2_gnn_" + v] for v in (
            "w1", "w2", "w3", "b1", "b2", "b3", "g1", "be1", "g2", "be2", "bn_g", "bn_b")})
        recycle(nc)
        k.h = sb("h_att2", [P, NB, D + 1], F32)
        with ExitStack() as att:
            mx = Maxima(nc, att, "m3")
            stage_project(nc, k, "p3", mx, k.xs, True, ins["L3_gnn_W1"], None, ins["L3_gnn_a1_src"],
                          ins["L3_gnn_a1_dst"])
            stage_attention(nc, k, "t3", mx, "relu", ins["L3_gnn_b1"])
        with ExitStack() as att:
            mx = Maxima(nc, att, "m4")
            stage_project(nc, k, "p4", mx, k.y, False, ins["L3_gnn_W2"], None, ins["L3_gnn_a2_src"],
                          ins["L3_gnn_a2_dst"])
            stage_attention(nc, k, "t4", mx, "both", ins["L3_gnn_b2"])
        stage_last(nc, k, outs["out"])


_AS_THEY_ARE = ("x", "dst", "L0_gnn_b1", "L0_gnn_b2", "L0_gnn_b3", "L1_gnn_Wv", "L1_gnn_bv", "L1_gnn_wq", "L1_gnn_bq",
                "L1_gnn_wk", "L1_gnn_bk", "L2_gnn_eps", "L2_gnn_ee_w1", "L2_gnn_ee_b1", "L2_gnn_ee_w2", "L2_gnn_ee_b2",
                "L2_gnn_w1", "L2_gnn_b1", "L2_gnn_g1", "L2_gnn_be1", "L2_gnn_w2", "L2_gnn_b2", "L2_gnn_g2",
                "L2_gnn_be2", "L2_gnn_w3", "L2_gnn_b3", "L2_gnn_bn_g", "L2_gnn_bn_b", "L3_gnn_W1", "L3_gnn_a1_src",
                "L3_gnn_a1_dst", "L3_gnn_b1", "L3_gnn_W2", "L3_gnn_a2_src", "L3_gnn_a2_dst", "L3_gnn_b2")


def kernel(**inputs):
    import concourse.bacc as bacc
    from concourse.bass_utils import run_bass_kernel_spmd

    a = {n: np.ascontiguousarray(inputs[n]).reshape(inputs[n].shape or (1,)) for n in _AS_THEY_ARE}
    a["srcT"] = np.ascontiguousarray(inputs["src"].reshape(E // P, P).T)
    a["dstT"] = np.ascontiguousarray(inputs["dst"].reshape(E // P, P).T)
    a["eaT"] = np.concatenate([inputs["edge_attr_64"].T] * 2)
    for n in ("W1", "W2", "W3"):
        a[n + "T"] = np.ascontiguousarray(inputs["L0_gnn_" + n].T)
    nc = bacc.Bacc("TRN2", target_bir_lowering=False, num_devices=1)
    ins = {n: nc.dram_tensor("in_" + n, v.shape, mybir.dt.from_np(v.dtype), kind="ExternalInput").ap()
           for n, v in a.items()}
    out = nc.dram_tensor("out_x", (N, D), F32, kind="ExternalOutput").ap()
    program(nc, ins, {"out": out})
    r = run_bass_kernel_spmd(nc, [{"in_" + n: v for n, v in a.items()}], core_ids=[0])
    return r.results[0]["out_x"]
```
